# Optimizing a Trainium2 kernel written in Bass

```python
import numpy as np
import jax
import jax.numpy as jnp

def _softmax(x, axis=-1):
    return jax.nn.softmax(x, axis=axis)

def _gelu(x):
    return jax.nn.gelu(x, approximate=True)

def _silu(x):
    return jax.nn.silu(x)

def _sigmoid(x):
    return jax.nn.sigmoid(x)

def _layernorm(x, axis=-1, eps=1e-05):
    m = jnp.mean(x, axis=axis, keepdims=True)
    v = jnp.var(x, axis=axis, keepdims=True)
    return (x - m) / jnp.sqrt(v + eps)

def _scatter_add(tgt, idx, src, axis=0):
    return tgt.at[idx].add(src)

def _segment_sum(src, seg, n):
    return jax.ops.segment_sum(src, seg, n)
kernel_name = 'mk_adaln_d1_jaxref_r8_f70f1d'

def setup_inputs(seed: int=0):
    np.random.seed(seed)
    _w = jnp.asarray

    def _L0_attn_setup():
        import jax, jax.numpy as jnp
        import numpy as np
        EMBED_DIM = 128
        N_HEADS = 16
        HEAD_DIM = EMBED_DIM // N_HEADS
        MAX_REL = 64
        B, S = (4, 128)
        key = jax.random.key(seed)
        ks = jax.random.split(key, 10)
        sc = 1.0 / np.sqrt(EMBED_DIM)
        return {'q': jax.random.normal(ks[0], (B, S, EMBED_DIM), jnp.float32), 'Wq': jax.random.normal(ks[1], (EMBED_DIM, EMBED_DIM), jnp.float32) * sc, 'bq': jax.random.normal(ks[2], (EMBED_DIM,), jnp.float32) * 0.02, 'Wk': jax.random.normal(ks[3], (EMBED_DIM, EMBED_DIM), jnp.float32) * sc, 'bk': jax.random.normal(ks[4], (EMBED_DIM,), jnp.float32) * 0.02, 'Wv': jax.random.normal(ks[5], (EMBED_DIM, EMBED_DIM), jnp.float32) * sc, 'bv': jax.random.normal(ks[6], (EMBED_DIM,), jnp.float32) * 0.02, 'Wo': jax.random.normal(ks[7], (EMBED_DIM, EMBED_DIM), jnp.float32) * sc, 'bo': jax.random.normal(ks[8], (EMBED_DIM,), jnp.float32) * 0.02, 'rel_table': jax.random.normal(ks[9], (2 * MAX_REL + 1, HEAD_DIM), jnp.float32) * 0.02}
    _L0_attn_in = _L0_attn_setup()

    def _L0_ffn_setup():
        import jax, jax.numpy as jnp
        import numpy as np
        EMB, HID, E, TOPK = (128, 512, 8, 2)
        key = jax.random.key(seed)
        ks = jax.random.split(key, 10)
        s = 0.02
        return {'x': jax.random.normal(ks[0], (4, 256, EMB), jnp.float32), 'rw1': s * jax.random.normal(ks[1], (EMB, HID), jnp.float32), 'rb1': jnp.zeros((HID,), jnp.float32), 'rw2': s * jax.random.normal(ks[2], (HID, E), jnp.float32), 'rb2': jnp.zeros((E,), jnp.float32), 'w1': s * jax.random.normal(ks[3], (E, EMB, HID), jnp.float32), 'b1': jnp.zeros((E, HID), jnp.float32), 'w2': s * jax.random.normal(ks[4], (E, HID, EMB), jnp.float32), 'b2': jnp.zeros((E, EMB), jnp.float32)}
    _L0_ffn_in = _L0_ffn_setup()
    _L0_c = _w((lambda *s: np.random.randn(*s).astype(np.float32) * 0.05)(16, 128))
    _L0_wmod = _w((lambda *s: np.random.randn(*s).astype(np.float32) * 0.05)(128, 6 * 128) * 128 ** (-0.5))
    _d = {'L0_attn_q': _L0_attn_in['q'], 'L0_attn_Wq': _L0_attn_in['Wq'], 'L0_attn_bq': _L0_attn_in['bq'], 'L0_attn_Wk': _L0_attn_in['Wk'], 'L0_attn_bk': _L0_attn_in['bk'], 'L0_attn_Wv': _L0_attn_in['Wv'], 'L0_attn_bv': _L0_attn_in['bv'], 'L0_attn_Wo': _L0_attn_in['Wo'], 'L0_attn_bo': _L0_attn_in['bo'], 'L0_attn_rel_table': _L0_attn_in['rel_table'], 'L0_ffn_rw1': _L0_ffn_in['rw1'], 'L0_ffn_rb1': _L0_ffn_in['rb1'], 'L0_ffn_rw2': _L0_ffn_in['rw2'], 'L0_ffn_rb2': _L0_ffn_in['rb2'], 'L0_ffn_w1': _L0_ffn_in['w1'], 'L0_ffn_b1': _L0_ffn_in['b1'], 'L0_ffn_w2': _L0_ffn_in['w2'], 'L0_ffn_b2': _L0_ffn_in['b2'], 'L0_c': _L0_c, 'L0_wmod': _L0_wmod}
    _x0 = _d['L0_attn_q']
    _d['L0_attn_q'] = jax.random.normal(jax.random.fold_in(jax.random.key(seed), 1), (16, 256, 128), dtype=_x0.dtype)
    del _x0
    return _d

def reference(L0_attn_q, L0_attn_Wq, L0_attn_bq, L0_attn_Wk, L0_attn_bk, L0_attn_Wv, L0_attn_bv, L0_attn_Wo, L0_attn_bo, L0_attn_rel_table, L0_ffn_rw1, L0_ffn_rb1, L0_ffn_rw2, L0_ffn_rb2, L0_ffn_w1, L0_ffn_b1, L0_ffn_w2, L0_ffn_b2, L0_c, L0_wmod):

    def _L0_attn_ref(q, Wq, bq, Wk, bk, Wv, bv, Wo, bo, rel_table):
        import jax, jax.numpy as jnp
        import numpy as np
        EMBED_DIM = 128
        N_HEADS = 16
        HEAD_DIM = EMBED_DIM // N_HEADS
        MAX_REL = 64
        B, S = (4, 128)
        b, s, e = q.shape
        h, d = (N_HEADS, HEAD_DIM)
        Q = (q @ Wq + bq).reshape(b, s, h, d).transpose(0, 2, 1, 3)
        K = (q @ Wk + bk).reshape(b, s, h, d).transpose(0, 2, 1, 3)
        V = (q @ Wv + bv).reshape(b, s, h, d).transpose(0, 2, 1, 3)
        scores = jnp.einsum('bhid,bhjd->bhij', Q, K) / jnp.sqrt(jnp.asarray(d, q.dtype))
        pos = jnp.arange(s)
        rel_idx = jnp.clip(pos[None, :] - pos[:, None] + MAX_REL, 0, 2 * MAX_REL)
        rel_emb = rel_table[rel_idx]
        scores = scores + jnp.einsum('bhid,ijd->bhij', Q, rel_emb)
        attn = jax.nn.softmax(scores, axis=-1)
        ctx = jnp.einsum('bhij,bhjd->bhid', attn, V)
        ctx = ctx.transpose(0, 2, 1, 3).reshape(b, s, e)
        return ctx @ Wo + bo

    def _L0_ffn_ref(x, rw1, rb1, rw2, rb2, w1, b1, w2, b2):
        import jax, jax.numpy as jnp
        import numpy as np
        EMB, HID, E, TOPK = (128, 512, 8, 2)
        B, S, D = x.shape
        logits = jax.nn.silu(jnp.einsum('bsd,dh->bsh', x, rw1) + rb1)
        logits = jnp.einsum('bsh,he->bse', logits, rw2) + rb2
        k_logits, k_index = jax.lax.top_k(logits, TOPK)
        k_prob = jax.nn.softmax(k_logits, axis=-1)
        xf = x.reshape(B * S, D)
        k_index_f = k_index.reshape(B * S, TOPK)
        k_prob_f = k_prob.reshape(B * S, TOPK)
        out = jnp.zeros_like(xf)
        for e in range(E):
            we = jnp.sum(jnp.where(k_index_f == e, k_prob_f, 0.0), axis=-1)
            h = jax.nn.silu(xf @ w1[e] + b1[e]) @ w2[e] + b2[e]
            out = out + we[:, None] * h
        return out.reshape(B, S, D)
    x = L0_attn_q
    mod = (_silu(L0_c) @ L0_wmod).reshape(L0_c.shape[0], 6, 1, -1)
    sa, ca, ga, sb, cb, gb = (mod[:, 0], mod[:, 1], mod[:, 2], mod[:, 3], mod[:, 4], mod[:, 5])
    ga = (2 * (ga >= 0) - 1) * jnp.maximum(jnp.abs(ga), 0.25)
    gb = (2 * (gb >= 0) - 1) * jnp.maximum(jnp.abs(gb), 0.25)
    h = _layernorm(x, axis=-1) * (1 + ca) + sa
    x = x + ga * _L0_attn_ref(h, L0_attn_Wq, L0_attn_bq, L0_attn_Wk, L0_attn_bk, L0_attn_Wv, L0_attn_bv, L0_attn_Wo, L0_attn_bo, L0_attn_rel_table)
    h = _layernorm(x, axis=-1) * (1 + cb) + sb
    x = x + gb * _L0_ffn_ref(h, L0_ffn_rw1, L0_ffn_rb1, L0_ffn_rw2, L0_ffn_rb2, L0_ffn_w1, L0_ffn_b1, L0_ffn_w2, L0_ffn_b2)
    return x

_drawn_inputs = setup_inputs


def setup_inputs(seed=0):
    import zlib

    import numpy as np

    out = dict(_drawn_inputs(seed))
    spreads = {'L0_ffn_rb1': (0.0, 0.8),
     'L0_ffn_rb2': (0.0, 0.431),
     'L0_ffn_b1': (0.0, 0.8),
     'L0_ffn_b2': (0.0, 0.482)}
    factors = {'L0_attn_bq': 25.976,
     'L0_attn_bk': 64.0,
     'L0_attn_bv': 8.0,
     'L0_attn_bo': 8.0,
     'L0_attn_rel_table': 8.0,
     'L0_ffn_rw1': 4.614,
     'L0_ffn_rw2': 4.428,
     'L0_ffn_w1': 6.155,
     'L0_ffn_w2': 5.551}
    for name, (base, spread) in spreads.items():
        noise = np.random.default_rng([zlib.crc32(name.encode()), seed]).standard_normal(out[name].shape)
        drawn = base * np.exp(spread * noise) if base else spread * noise
        out[name] = jnp.asarray(drawn.astype(out[name].dtype))
    for name, factor in factors.items():
        out[name] = (out[name] * factor).astype(out[name].dtype)
    return out
```

```python
import concourse.bass as bass
from concourse import mybir
from contextlib import ExitStack

B, S, E = 16, 256, 128
H, D = 16, 8
REL = 64
HID, EXP = 512, 8
EPS = 1e-5
TT = B * S // 128

HH = H // 2
QG = 128 // HH
G = S // QG
PAIRS = G // 2
JB = S // 128
VW = 128 + D
TW = S + S - QG
FP = mybir.dt.float32
FR = mybir.dt.float32r
U32 = mybir.dt.uint32
ALU = mybir.AluOpType
ACT = mybir.ActivationFunctionType
AX = mybir.AxisListType


def rep(ap, axis, n):
    shape = list(ap.shape)
    shape.insert(axis, n)
    return ap.unsqueeze(axis).broadcast_to(shape)


SLOT_JOBS = [
    [["q"], ["r0"], ["r1"], ["r2"], ["r3", "r4"], ["r5"], ["r6", "r7"], ["hv"]],
    [["q"], ["r0"], ["r1", "y"], ["r2"], ["r3", "t"], ["r4", "r5"], ["r6", "r7"], ["v"]],
]


def jobs_before(half, slot, n, with_y=True):
    flat = [j for hh in range(2) for s, js in enumerate(SLOT_JOBS[hh])
            for i, j in enumerate(js) if (hh, s, i) < (half, slot, n)]
    return sum(with_y or j not in ("y", "t") for j in flat)


LINKS = 6
START_JOBS = 11
BATCH_JOBS = jobs_before(2, 0, 0)
FIRST_JOBS = jobs_before(2, 0, 0, False)


def job_count(b, half, slot, n):
    if isinstance(b, int) and b == 0:
        return START_JOBS + jobs_before(half, slot, n, False)
    return BATCH_JOBS * b + (START_JOBS + FIRST_JOBS - BATCH_JOBS) + jobs_before(half, slot, n)


def slot_jobs(b, half, slot, last=False):
    found = []
    for n, name in enumerate(SLOT_JOBS[half][slot]):
        if name in ("y", "t"):
            if isinstance(b, int) and b == 0:
                continue
        elif last and half:
            continue
        count = job_count(b, half, slot, n)
        if last and half:
            count = job_count(b, 1, 0, 0) + ("y", "t").index(name)
        if last and name == "hv":
            name = "-v"
        bank = count % 2 if isinstance(b, int) else job_count(1, half, slot, n) % 2
        found.append((name, count, bank))
    return found


assert BATCH_JOBS % 2 == 0
Y_TO_T = jobs_before(1, 4, 1) - jobs_before(1, 2, 1)


def prepared(b, half):
    if isinstance(b, int) and b == 0 and half == 0:
        return START_JOBS
    if half == 0:
        return job_count(b - 1, 1, 7, 0)
    return job_count(b, 0, 7, 0)


def program(nc, q, Wq, bq, Wk, bk, Wv, bv, Wo, bo, rel, rw1, rb1, rw2, rb2, w1, b1, w2, b2, c,
            wmod, out):
    x_v = q.rearrange("b (n p) e -> p (b n) e", p=128)
    out_v = out.rearrange("b (n p) e -> p (b n) e", p=128)
    with ExitStack() as ctx:
        def sb(name, shape, dt=FP):
            return ctx.enter_context(nc.sbuf_tensor(name, shape, dt))

        X = sb("X", [128, TT, E])
        ident = sb("ident", [128, 128])
        modT = sb("modT", [128, 6, B])
        mv = sb("mv", [128, TT, 2])
        rstd = sb("rstd", [128, TT])
        attention(nc, x_v, X, ident, modT, mv, rstd, Wq, bq, Wk, bk, Wv, bv, Wo, bo, rel, c, wmod)
        mixture(nc, X, ident, modT, mv, rstd, rw1, rb1, rw2, rb2, w1, b1, w2, b2, out_v)


def attention(nc, x_v, X, ident, modT, mv, rstd, Wq, bq, Wk, bk, Wv, bv, Wo, bo, rel, c, wmod):
    ctx = ExitStack()
    with ctx:
        def t(name, shape, dt=FP):
            return ctx.enter_context(nc.sbuf_tensor(name, shape, dt))

        WqD = t("WqD", [128, 2, 2, 64])
        WkD = t("WkD", [128, 2, 2, 64])
        Wv_s = t("Wv_s", [128, E])
        WoD = t("WoD", [128, 2, E])
        bqD = t("bqD", [128, 2])
        bkD = t("bkD", [128, 2])
        bvD = t("bvD", [128, 2])
        boC = t("boC", [128, 1])
        bo2 = t("bo2", [128, 1])
        gabo = t("gabo", [128, B])
        wmod_s = t("wmod_s", [128, 6 * E])
        c_s = t("c_s", [B, E])
        c_e = t("c_e", [B, E])
        cT = t("cT", [128, B])
        headM = t("headM", [128, HH])
        queryM = t("queryM", [128, QG])
        headL = t("headL", [128, HH])
        queryL = t("queryL", [128, QG])
        lowM = t("lowM", [128, 1])
        sel = t("sel", [128, 2, HH, 128], FR)
        selL = t("selL", [128, 2, HH, D])
        relA = t("relA", [128, D])
        relB = t("relB", [1, D])
        relR = t("relR", [128, QG, D])
        relRb = t("relRb", [1, QG, D])
        relT = t("relT", [128, 2 * REL + 1])
        Tf = t("Tf", [128, TW])
        TH = t("TH", [128, TW], FR)
        TL = t("TL", [128, TW], FR)
        stats = t("stats", [128, 4, 6])
        tmp = t("tmp", [128, TT])
        nrm = t("nrm", [128, 2, E])
        hT = t("hT", [128, S])
        X2t = t("X2t", [128, S], FR)
        X2 = t("X2", [128, S], FR)
        KH = t("KH", [128, 2, S], FR)
        KL = t("KL", [128, 2, S], FR)
        Qbd = t("Qbd", [128, 2, G, HH, QG], FR)
        QrH = t("QrH", [128, 2, G, HH, QG], FR)
        QrL = t("QrL", [128, 2, G, HH, QG], FR)
        V2 = t("V2", [128, 2, JB, HH * VW], FR)
        nmax = t("nmax", [128, 2, G])
        lsum = t("lsum", [128, 2, G])
        P = t("P", [128, 4, 512])
        PH = t("PH", [128, 2, PAIRS, 512], FR)
        PL = t("PL", [128, 2, PAIRS, 512], FR)
        linv = t("linv", [128, G])
        ldiag = t("ldiag", [128, G, QG])
        lrow = t("lrow", [128, S])
        ctxT = t("ctxT", [128, 2, S])
        yT = t("yT", [128, S])

        def pt(name, shape):
            return ctx.enter_context(nc.psum_tensor(name, shape, FP))

        psS = pt("psS", [128, 2, 512])
        psT = pt("psT", [128, 2, 512])
        psO = pt("psO", [128, 512])
        psP = pt("psP", [128, 2, 512])
        psZ = pt("psZ", [128, 512])

        def sm(name):
            return ctx.enter_context(nc.semaphore(name))

        weights_in, x_first, x_rest, rel_in, c_in = (
            sm("weights_in"), sm("x_first"), sm("x_rest"), sm("rel_in"), sm("c_in"))
        ident_done, masks_done, c_done, rel_rows, rel_turned = (
            sm("ident_done"), sm("masks_done"), sm("c_done"), sm("rel_rows"), sm("rel_turned"))
        rel_filled, rel_shifted, mod_full, setup_pe, setup_dve, sqrt_done = (
            sm("rel_filled"), sm("rel_shifted"), sm("mod_full"), sm("setup_pe"), sm("setup_dve"),
            sm("sqrt_done"))
        scores_done, max_done, exp_done, turned, high_done, low_done = (
            sm("scores_done"), sm("max_done"), sm("exp_done"), sm("turned"), sm("high_done"),
            sm("low_done"))
        values_done, ldiag_done, lrow_full, lrow_done, ctx_done = (
            sm("values_done"), sm("ldiag_done"), sm("lrow_full"), sm("lrow_done"), sm("ctx_done"))
        job_full, job_done, nrm_done, x2_done, qbd_done, link = (
            sm("job_full"), sm("job_done"), sm("nrm_done"), sm("x2_done"), sm("qbd_done"),
            sm("link"))

        W_DMAS = 2 + 2 + 1 + 2 + 6 + 1 + 1
        block = ctx.enter_context(nc.Block())

        @block.sync
        def _(sp):
            sp.dma_start(c_s[:], c).then_inc(c_in, 16)
            sp.dma_start(wmod_s[:], wmod).then_inc(weights_in, 16)
            sp.dma_start(X[:, 0:4, :], x_v[:, 0:4, :]).then_inc(x_first, 16)
            for k in range(2):
                sp.dma_start(WqD[:, :, k, :], Wq.rearrange("e (a m) -> e a m", a=2)).then_inc(weights_in, 16)
                sp.dma_start(WkD[:, :, k, :], Wk.rearrange("e (a m) -> e a m", a=2)).then_inc(weights_in, 16)
            sp.dma_start(Wv_s[:], Wv).then_inc(weights_in, 16)
            for k in range(2):
                sp.dma_start(WoD[64 * k:64 * k + 64, :, :], Wo.rearrange("(a m) e -> m a e", a=2)).then_inc(weights_in, 16)
                for src, dst in ((bq, bqD), (bk, bkD), (bv, bvD)):
                    sp.dma_start(dst[64 * k:64 * k + 64, :], src.rearrange("(a m) -> m a", a=2),
                                 allow_slow_non_contiguous=True).then_inc(weights_in, 16)
            sp.dma_start(boC[:], bo.rearrange("(e a) -> e a", a=1)).then_inc(weights_in, 16)
            sp.dma_start(X[:, 4:TT, :], x_v[:, 4:TT, :]).then_inc(x_rest, 16)

        @block.gpsimd
        def _(pool):
            pool.memset(ident[:], 0.0).then_inc(ident_done, 1)
            pool.wait_ge(ident_done, 1)
            pool.affine_select(out=ident[:], in_=ident[:], compare_op=ALU.not_equal, fill=1.0,
                               base=0, pattern=[[-1, 128]], channel_multiplier=1).then_inc(ident_done, 1)
            pool.memset(V2[:].bitcast(FP), 0.0).then_inc(ident_done, 1)

            def spread(b, half):
                pool.wait_ge(x2_done, 2 * b + half + 1)
                for a in range(2):
                    if a == 0 and not (isinstance(b, int) and b == 0):
                        pool.wait_ge(scores_done, PAIRS * (2 * b + half - 1))
                    g = slice(a * G // 2, (a + 1) * G // 2)
                    x2 = X2[:].bitcast(FP).rearrange("p (g i) -> p g i", i=QG)[:, g, :]
                    i = pool.tensor_tensor(
                        Qbd[:, half, g, :, :], rep(x2, 2, HH),
                        rep(rep(headM[:], 1, G // 2), 3, QG), ALU.mult)
                i.then_inc(qbd_done, 1)

            pool.wait_ge(masks_done, 1)
            spread(0, 0)
            spread(0, 1)
            with pool.Fori(1, B) as b:
                spread(b, 0)
                spread(b, 1)

        @block.scalar
        def _(act):
            act.dma_start(relA[:], rel[0:128, :]).then_inc(rel_in, 16)
            act.dma_start(relB[:], rel[128:129, :]).then_inc(rel_in, 16)
            act.wait_ge(c_in, 16)
            act.activation(c_e[:], c_s[:], ACT.Exp, scale=-1.0).then_inc(c_done, 1)
            act.wait_ge(rel_filled, 1)
            for i in range(QG):
                at = S - QG - REL + i
                act.dma_start(Tf[D * i:D * i + D, at:at + 2 * REL + 1],
                              relT[D * i:D * i + D, :]).then_inc(rel_shifted, 16)
            act.wait_ge(setup_dve, 1)
            act.activation(rstd[:], mv[:, :, 1], ACT.Sqrt).then_inc(sqrt_done, 1)

            def exps(b, half, p):
                n = 16 * b + 8 * half + p
                act.wait_ge(max_done, n + 1)
                if not (isinstance(b, int) and b == 0) or 8 * half + p >= 4:
                    act.wait_ge(turned, n - 3)
                for k in range(2):
                    g = 2 * p + k
                    i = act.activation(P[:, p % 4, 256 * k:256 * k + 256],
                                       psS[:, p % 2, 256 * k:256 * k + 256], ACT.Exp,
                                       bias=nmax[:, half, g:g + 1],
                                       accum_out=lsum[:, half, g:g + 1])
                i.then_inc(exp_done, 1)

            def high(b, half, p):
                n = 16 * b + 8 * half + p
                act.wait_ge(turned, n + 1)
                if not (isinstance(b, int) and b == 0) and p == 0:
                    act.wait_ge(values_done, 2 * b + half - 1)
                act.activation(PH[:, half, p, :], psT[:, p % 2, :], ACT.Copy).then_inc(high_done, 1)

            def rows(b, half):
                act.wait_ge(lrow_full, 2 * b + half + 1)
                if not (isinstance(b, int) and b == 0 and half == 0):
                    act.wait_ge(ctx_done, 2 * b + half)
                act.activation(lrow[:], psO[:, S:2 * S], ACT.Copy).then_inc(lrow_done, 1)

            def batch(b):
                for half in range(2):
                    pb, ph = (b, 0) if half else (b - 1, 1)
                    before = not (isinstance(b, int) and b == 0 and half == 0)
                    for p in range(PAIRS):
                        if p >= 2:
                            high(b, half, p - 2)
                        elif before:
                            high(pb, ph, PAIRS - 2 + p)
                        exps(b, half, p)
                        if p == 7 and before:
                            rows(pb, ph)

            batch(0)
            with act.Fori(1, B) as b:
                batch(b)
            high(B - 1, 1, PAIRS - 2)
            high(B - 1, 1, PAIRS - 1)
            rows(B - 1, 1)

        @block.tensor
        def _(pe):
            pe.wait_ge(ident_done, 2)
            pe.wait_ge(c_done, 3)
            pe.transpose(psZ[:, 0:B], c_s[:], ident[0:B, 0:B]).then_inc(setup_pe, 1)
            pe.wait_ge(c_done, 4)
            pe.wait_ge(weights_in, 16 * W_DMAS)
            for k in range(6):
                mm = pe.matmul(psP[:, 0, B * k:B * k + B], wmod_s[:, E * k:E * k + E], cT[:],
                               start=True, stop=True)
            mm.then_inc(mod_full, 1)
            for half in range(2):
                mm = pe.matmul(psP[:, 1, 0:1], WoD[0:64, half, :], bvD[0:64, half:half + 1],
                               start=(half == 0), stop=(half == 1))
            mm.then_inc(mod_full, 1)
            pe.wait_ge(rel_rows, 2)
            pe.transpose(psT[:, 0, 0:128], relR[:].rearrange("r i d -> r (i d)"), ident[:])
            pe.transpose(psT[:, 0, 128:129], relRb[:].rearrange("r i d -> r (i d)"),
                         ident[0:1, 0:1]).then_inc(rel_turned, 1)

            def job(count, bank, work):
                if not (isinstance(count, int) and count < 2):
                    pe.wait_ge(job_done, count - 1)
                work(psP[:, bank, :]).then_inc(job_full, 1)

            def turn_nrm(bank):
                for k in range(2):
                    mm = pe.transpose(bank[:, 128 * k:128 * k + 128], nrm[:, k, :], ident[:])
                return mm

            def values(bank, half, at):
                for k in range(JB):
                    mm = pe.matmul(bank[:, at + 64 * k:at + 64 * k + 64], hT[:, 128 * k:128 * k + 128],
                                   Wv_s[:, 64 * half:64 * half + 64], start=True, stop=True)
                return mm

            def project(bank, half):
                pe.matmul(bank[:, 0:S], WqD[:, half, :, :].rearrange("e a m -> e (a m)"), hT[:],
                          start=True, stop=True)
                return pe.matmul(bank[:, S:2 * S], WkD[:, half, :, :].rearrange("e a m -> e (a m)"),
                                 hT[:], start=True, stop=True)

            def spread(bank, r):
                part, h0 = r // 4, 2 * (r % 4)
                for k in range(2):
                    mm = pe.matmul(bank[:, S * k:S * k + S], sel[:, part, h0 + k, :], X2[:],
                                   start=True, stop=True)
                return mm

            def out_project(bank):
                for half in range(2):
                    mm = pe.matmul(bank[:, 0:S], WoD[:, half, :], ctxT[:, half, :],
                                   start=(half == 0), stop=(half == 1))
                return mm

            def turn_y(bank):
                for k in range(2):
                    mm = pe.transpose(bank[:, 128 * k:128 * k + 128], yT[:, 128 * k:128 * k + 128],
                                      ident[:])
                return mm

            def run_job(name, b, half, count, bank):
                other = 1 - half
                if name == "q":
                    if half:
                        pe.wait_ge(job_done, count)
                    job(count, bank, lambda k: project(k, other))
                elif name[0] == "r":
                    r = int(name[1])
                    if r == 0:
                        pe.wait_ge(job_done, count)
                    job(count, bank, lambda k: spread(k, r))
                elif name == "hv":
                    pe.wait_ge(nrm_done, b + 2)
                    def both(k):
                        turn_nrm(k)
                        return values(k, other, S)
                    job(count, bank, both)
                elif name == "v":
                    job(count, bank, lambda k: values(k, other, 0))
                elif name == "-v":
                    job(count, bank, lambda k: values(k, other, S))
                elif name == "y":
                    pe.wait_ge(ctx_done, 2 * b)
                    job(count, bank, out_project)
                elif name == "t":
                    last = isinstance(b, int) and b == B - 1
                    pe.wait_ge(job_done, count + 1 - (1 if last else Y_TO_T))
                    job(count, bank, turn_y)

            def scores(b, half, p):
                n = 16 * b + 8 * half + p
                if p == 0:
                    pe.wait_ge(job_done, prepared(b, half))
                    pe.wait_ge(qbd_done, 2 * b + half + 1)
                if not (isinstance(b, int) and b == 0) or 8 * half + p >= 2:
                    pe.wait_ge(exp_done, n - 1)
                for k in range(2):
                    g = 2 * p + k
                    dst = psS[:, p % 2, 256 * k:256 * k + 256]
                    at = S - QG - QG * g
                    qb = Qbd[:, half, g, :, :].rearrange("p h i -> p (h i)")
                    qh = QrH[:, half, g, :, :].rearrange("p h i -> p (h i)")
                    ql = QrL[:, half, g, :, :].rearrange("p h i -> p (h i)")
                    pe.matmul(dst, qb, KH[:, half, :], start=True, stop=False)
                    pe.matmul(dst, qb, KL[:, half, :], start=False, stop=False)
                    pe.matmul(dst, qh, TH[:, at:at + S], start=False, stop=False)
                    pe.matmul(dst, qh, TL[:, at:at + S], start=False, stop=False)
                    mm = pe.matmul(dst, ql, TH[:, at:at + S], start=False, stop=True)
                mm.then_inc(scores_done, 1)

            def turn(b, half, p):
                n = 16 * b + 8 * half + p
                pe.wait_ge(exp_done, n + 1)
                if not (isinstance(b, int) and b == 0) or 8 * half + p >= 2:
                    pe.wait_ge(low_done, n - 1)
                for k in range(4):
                    mm = pe.transpose(psT[:, p % 2, 128 * k:128 * k + 128],
                                      P[:, p % 4, 128 * k:128 * k + 128], ident[:])
                mm.then_inc(turned, 1)

            def weigh(b, half, part):
                if part == 0:
                    pe.wait_ge(low_done, 16 * b + 8 * half + 8)
                    if not (isinstance(b, int) and b == 0 and half == 0):
                        pe.wait_ge(ctx_done, 2 * b + half)
                for h in (2 * part, 2 * part + 1):
                    for k in range(JB):
                        for n, pr in enumerate((PH, PL)):
                            rhs = pr[:, half, :, :].rearrange("j p (t x) -> j (p t) x", t=2)
                            at = 128 * k + QG * h
                            mm = pe.matmul(psO[:, 0:S], V2[:, half, k, 128 * h:128 * h + 128],
                                           rhs[:, :, at:at + QG],
                                           start=(h == 0 and k == 0 and n == 0),
                                           stop=(h == HH - 1 and k == JB - 1 and n == 1))
                if part == 3:
                    mm.then_inc(values_done, 1)

            def spread_l(b, half):
                pe.wait_ge(ldiag_done, 2 * b + half + 1)
                pe.matmul(psO[:, S:2 * S], selL[:].rearrange("p a h d -> p (a h d)"),
                          ldiag[:].rearrange("p g i -> p (g i)"), start=True, stop=True)\
                    .then_inc(lrow_full, 1)

            pe.wait_ge(nrm_done, 1)
            job(0, 0, turn_nrm)
            pe.wait_ge(job_done, 1)
            job(1, 1, lambda k: values(k, 0, 0))
            job(2, 0, lambda k: project(k, 0))
            pe.wait_ge(job_done, 3)
            pe.wait_ge(masks_done, 1)
            for r in range(8):
                job(3 + r, (3 + r) % 2, lambda k, r=r: spread(k, r))

            def batch(b, last=False):
                first = isinstance(b, int) and b == 0
                for half in range(2):
                    pb, ph = (b, 0) if half else (b - 1, 1)
                    before = not (first and half == 0)
                    for p in range(PAIRS):
                        if p >= 2:
                            turn(b, half, p - 2)
                        elif before:
                            turn(pb, ph, PAIRS - 2 + p)
                        scores(b, half, p)
                        if p == 7 and before:
                            spread_l(pb, ph)
                        if 3 <= p < 7 and before:
                            weigh(pb, ph, p - 3)
                        for name, count, bank in slot_jobs(b, half, p, last):
                            run_job(name, b, half, count, bank)

            pe.wait_ge(setup_dve, 2)
            batch(0)
            with pe.Fori(1, B - 1) as b:
                batch(b)
            batch(B - 1, last=True)
            for p in (PAIRS - 2, PAIRS - 1):
                turn(B - 1, 1, p)
            for part in range(4):
                weigh(B - 1, 1, part)
            spread_l(B - 1, 1)
            done = job_count(B - 1, 1, 0, 0) + 2
            pe.wait_ge(ctx_done, 2 * B)
            job(done, done % 2, out_project)
            pe.wait_ge(job_done, done + 1)
            job(done + 1, (done + 1) % 2, turn_y)

        @block.vector
        def _(dve):
            linked = {"base": 0, "n": 0}

            def then(i):
                i.then_inc(link, 1)
                linked["n"] += 1
                dve.wait_ge(link, linked["base"] + linked["n"])

            dve.wait_ge(ident_done, 2)
            dve.tensor_reduce(headM[:], ident[:].rearrange("p (a h d) -> p h a d", a=2, d=D), AX.XY, ALU.add)
            dve.tensor_reduce(queryM[:], ident[:].rearrange("p (i d) -> p i d", d=D), AX.X, ALU.add)
            dve.tensor_reduce(headL[:], ident[:].rearrange("p (h i) -> p h i", i=QG), AX.X, ALU.add)
            dve.tensor_reduce(queryL[:], ident[:].rearrange("p (h i) -> p i h", i=QG), AX.X, ALU.add)
            then(dve.tensor_reduce(lowM[:], ident[:, 64:128], AX.X, ALU.add))
            for part in range(2):
                for h in range(HH):
                    at = 64 * part + D * h
                    dve.tensor_copy(sel[:, part, h, :].rearrange("p (i d) -> p i d", d=D),
                                    rep(ident[:, at:at + D], 1, QG))
            dve.tensor_copy(selL[:], rep(rep(headL[:], 1, 2), 3, D)).then_inc(masks_done, 1)
            dve.wait_ge(c_done, 1)
            dve.tensor_scalar(c_e[:], c_e[:], 1.0, None, ALU.add).then_inc(c_done, 1)
            dve.wait_ge(c_done, 2)
            then(dve.reciprocal(c_e[:], c_e[:]))
            dve.tensor_tensor(c_s[:], c_s[:], c_e[:], ALU.mult).then_inc(c_done, 1)
            dve.wait_ge(setup_pe, 1)
            dve.tensor_copy(cT[:], psZ[:, 0:B]).then_inc(c_done, 1)
            dve.wait_ge(rel_in, 32)
            dve.tensor_copy(relR[:], rep(relA[:], 1, QG)).then_inc(rel_rows, 1)
            dve.tensor_copy(relRb[:], rep(relB[:], 1, QG)).then_inc(rel_rows, 1)
            dve.wait_ge(rel_turned, 1)
            then(dve.tensor_copy(relT[:], psT[:, 0, 0:2 * REL + 1]))
            mid = S - QG
            dve.tensor_copy(Tf[:, 0:mid], relT[:, 0:1].broadcast_to([128, mid]))
            dve.tensor_copy(Tf[:, mid:TW], relT[:, 2 * REL:2 * REL + 1].broadcast_to([128, TW - mid]))\
                .then_inc(rel_filled, 1)
            dve.wait_ge(mod_full, 2)
            then(dve.tensor_copy(modT[:].rearrange("p k b -> p (k b)"), psP[:, 0, 0:6 * B]))
            for k in (1, 4):
                dve.tensor_scalar(modT[:, k, :], modT[:, k, :], 1.0, None, ALU.add)
            for k in (2, 5):
                then(dve.tensor_scalar(gabo[:], modT[:, k, :], 0.0, 2.0, ALU.is_ge, ALU.mult))
                then(dve.tensor_scalar(gabo[:], gabo[:], -1.0, None, ALU.add))
                then(dve.tensor_tensor(modT[:, k, :], modT[:, k, :], gabo[:], ALU.mult))
                then(dve.scalar_tensor_tensor(out=modT[:, k, :], in0=modT[:, k, :], scalar=0.25,
                                              in1=gabo[:], op0=ALU.max, op1=ALU.mult))
            then(dve.tensor_tensor(bo2[:], psP[:, 1, 0:1], boC[:], ALU.add))
            then(dve.tensor_scalar(gabo[:], modT[:, 2, :], bo2[:, 0:1], None, ALU.mult))
            then(dve.tensor_scalar(WkD[:].rearrange("e a b m -> e (a b m)"),
                                   WkD[:].rearrange("e a b m -> e (a b m)"), float(D) ** -0.5, None, ALU.mult))
            then(dve.tensor_scalar(bkD[:], bkD[:], float(D) ** -0.5, None, ALU.mult))
            for n in range(TT):
                if n in (0, 4):
                    dve.wait_ge(x_first if n == 0 else x_rest, 16)
                then(dve.bn_stats(stats[:, n % 4, :], X[:, n, :]))
                i = dve.bn_aggr(mv[:, n, :], stats[:, n % 4, :])
            then(i)
            mvar = mv[:, :, 1]
            dve.tensor_scalar(mvar, mvar, EPS, None, ALU.add).then_inc(setup_dve, 1)
            dve.wait_ge(sqrt_done, 1)
            then(dve.reciprocal(rstd[:], rstd[:]))
            newton(then, dve, rstd[:], mvar, tmp[:])
            dve.wait_ge(rel_shifted, 16 * QG)
            then(dve.tensor_copy(TH[:], Tf[:]))
            dve.tensor_tensor(TL[:], Tf[:], TH[:].bitcast(FP), ALU.subtract).then_inc(setup_dve, 1)

            def normalise(b):
                for k in range(2):
                    n = 2 * b + k
                    i = dve.tensor_scalar(nrm[:, k, :], at(X, n), at(mv, n, 0), at(rstd, n),
                                          ALU.subtract, ALU.mult)
                i.then_inc(nrm_done, 1)

            def at(tile, n, *more):
                if len(tile[:].shape) == 2:
                    return tile[:, bass.ds(n, 1)]
                v = tile[:, bass.ds(n, 1), :].rearrange("p a e -> p (a e)")
                return v[:, more[0]:more[0] + 1] if more else v

            def mod(k, b):
                return modT[:, k, bass.ds(b, 1)]

            def take(name, b, half, count, bank):
                other = 1 - half
                dve.wait_ge(job_full, count + 1)
                if name == "h":
                    i = dve.tensor_scalar(hT[:], bank[:, 0:S], mod(1, b), mod(0, b), ALU.mult, ALU.add)
                if name[-1] == "v":
                    src = bank[:, S:S + 128] if name in ("hv", "-v") else bank[:, 0:128]
                    src = src.rearrange("p (k h d) -> p k h d", k=JB, d=D)
                    win = V2[:, other, :, :].rearrange("p k (h c) -> p k h c", c=VW)
                    then(dve.tensor_copy(win[:, :, :, 0:D], src))
                    i = dve.tensor_tensor(win[:, :, :, 64:64 + D], src,
                                          win[:, :, :, 0:D].bitcast(FP), ALU.subtract)
                if name == "hv":
                    i = dve.tensor_scalar(hT[:], bank[:, 0:S], mod(1, b + 1), mod(0, b + 1),
                                          ALU.mult, ALU.add)
                elif name == "q":
                    if not (isinstance(b, int) and b == 0 and count == 2):
                        dve.wait_ge(qbd_done, 2 * b + half + 1)
                    qs, ks = bank[:, 0:S], bank[:, S:2 * S]
                    qbias, kbias = bqD[:, other:other + 1], bkD[:, other:other + 1]
                    dve.tensor_scalar(KH[:, other, :], ks, kbias, None, ALU.add)
                    then(dve.tensor_scalar(X2t[:], qs, qbias, lowM[:, 0:1], ALU.add, ALU.mult))
                    dve.scalar_tensor_tensor(out=X2[:], in0=qs, scalar=qbias,
                                             in1=X2t[:].bitcast(FP), op0=ALU.add,
                                             op1=ALU.subtract).then_inc(x2_done, 1)
                    i = dve.scalar_tensor_tensor(out=KL[:, other, :], in0=ks, scalar=kbias,
                                                 in1=KH[:, other, :].bitcast(FP), op0=ALU.add,
                                                 op1=ALU.subtract)
                elif name[0] == "r":
                    r = int(name[1])
                    dst = (QrH, QrL)[r // 4]
                    h0 = 2 * (r % 4)
                    i = dve.tensor_tensor(
                        dst[:, other, :, h0:h0 + 2, :].rearrange("p g h i -> p h g i"),
                        bank.rearrange("p (h g i) -> p h g i", h=2, i=QG),
                        rep(rep(queryM[:], 1, G), 1, 2), ALU.mult)
                elif name == "y":
                    i = dve.tensor_scalar(yT[:], bank[:, 0:S], mod(2, b - 1), gabo[:, bass.ds(b - 1, 1)],
                                          ALU.mult, ALU.add)
                elif name == "t":
                    xb = X[:, bass.ds(2 * (b - 1), 2), :]
                    i = dve.tensor_tensor(xb, bank[:, 0:S].rearrange("p (k e) -> p k e", k=2), xb,
                                          ALU.add)
                i.then_inc(job_done, 1)

            def maxima(b, half, p):
                dve.wait_ge(scores_done, 16 * b + 8 * half + p + 1)
                dve.tensor_reduce(nmax[:, half, 2 * p:2 * p + 2],
                                  psS[:, p % 2, :].rearrange("p (t j) -> p t j", t=2), AX.X,
                                  ALU.max, negate=True).then_inc(max_done, 1)

            def low(b, half, p):
                dve.wait_ge(high_done, 16 * b + 8 * half + p + 1)
                dve.tensor_tensor(PL[:, half, p, :], psT[:, p % 2, :], PH[:, half, p, :].bitcast(FP),
                                  ALU.subtract).then_inc(low_done, 1)

            def sums(b, half):
                dve.wait_ge(exp_done, 16 * b + 8 * half + 8)
                then(dve.reciprocal(linv[:], lsum[:, half, :]))
                dve.tensor_tensor(ldiag[:], rep(linv[:], 2, QG), rep(queryL[:], 1, G), ALU.mult)\
                    .then_inc(ldiag_done, 1)

            def context(b, half):
                dve.wait_ge(lrow_done, 2 * b + half + 1)
                dve.tensor_tensor(ctxT[:, half, :], psO[:, 0:S], lrow[:], ALU.mult)\
                    .then_inc(ctx_done, 1)

            dve.wait_ge(ident_done, 3)
            normalise(0)
            for n, name in enumerate(["h", "v", "q"] + [f"r{r}" for r in range(8)]):
                take(name, 0, 1, n, psP[:, n % 2, :])

            def batch(b, last=False):
                first = isinstance(b, int) and b == 0
                for half in range(2):
                    pb, ph = (b, 0) if half else (b - 1, 1)
                    before = not (first and half == 0)
                    for p in range(PAIRS):
                        if p == 0 and not first:
                            context(b - 1, half)
                        if p >= 2:
                            low(b, half, p - 2)
                        elif before:
                            low(pb, ph, PAIRS - 2 + p)
                        maxima(b, half, p)
                        if p == 2 and before:
                            sums(pb, ph)
                        if p == 5 and half == 0 and not last:
                            normalise(b + 1)
                        for name, count, bank in slot_jobs(b, half, p, last):
                            take(name, b, half, count, psP[:, bank, :])

            batch(0)
            used = linked["n"]
            per = LINKS
            with dve.Fori(1, B - 1) as b:
                linked["base"], linked["n"] = per * b + (used - per), 0
                batch(b)
                assert linked["n"] == per, linked["n"]
            linked["base"], linked["n"] = used + per * (B - 2), 0
            batch(B - 1, last=True)
            context(B - 1, 0)
            low(B - 1, 1, PAIRS - 2)
            low(B - 1, 1, PAIRS - 1)
            sums(B - 1, 1)
            context(B - 1, 1)
            done = job_count(B - 1, 1, 0, 0) + 2
            take("y", B, 1, done, psP[:, done % 2, :])
            take("t", B, 1, done + 1, psP[:, (done + 1) % 2, :])


def newton(then, dve, r, v, tmp):
    then(dve.tensor_tensor(tmp, r, r, ALU.mult))
    then(dve.tensor_tensor(tmp, tmp, v, ALU.mult))
    then(dve.tensor_scalar(tmp, tmp, -0.5, 1.5, ALU.mult, ALU.add))
    then(dve.tensor_tensor(r, r, tmp, ALU.mult))


CT = 512
CHUNKS = B * S // CT
CK = CT // 128
HK = HID // 128


def past(engine, semaphore, count):
    if not isinstance(count, int) or count > 0:
        engine.wait_ge(semaphore, count)


def mixture(nc, X, ident, modT, mv, rstd, rw1, rb1, rw2, rb2, w1, b1, w2, b2, out_v):
    with ExitStack() as ctx:
        def t(name, shape, dt=FP):
            return ctx.enter_context(nc.sbuf_tensor(name, shape, dt))

        def sm(name):
            return ctx.enter_context(nc.semaphore(name))

        h2H = t("h2H", [128, B * S], FR)
        h2L = t("h2L", [128, B * S], FR)
        b1T = t("b1T", [128, EXP, HK])
        b2T = t("b2T", [128, EXP])
        prob = t("prob", [128, TT, EXP])
        route(nc, X, ident, modT, mv, rstd, rw1, rb1, rw2, rb2, b1, b2, h2H, h2L, b1T, b2T, prob)
        experts(nc, X, ident, modT, w1, w2, h2H, h2L, b1T, b2T, prob, out_v)


def route(nc, X, ident, modT, mv, rstd, rw1, rb1, rw2, rb2, b1, b2, h2H, h2L, b1T, b2T, prob):
    with ExitStack() as ctx:
        def t(name, shape, dt=FP):
            return ctx.enter_context(nc.sbuf_tensor(name, shape, dt))

        def sm(name):
            return ctx.enter_context(nc.semaphore(name))

        rw1_s = t("rw1_s", [128, HID])
        rw2_s = t("rw2_s", [128, HK, EXP])
        rb1T = t("rb1T", [128, HK])
        rb2B = t("rb2B", [128, EXP])
        stats2 = t("stats2", [128, TT, 6])
        tmp2 = t("tmp2", [128, TT])
        n2 = t("n2", [128, 2, CK, E])
        h2T = t("h2T", [128, 2, CT])
        hid = t("hid", [128, HK, CT])
        logit = t("logit", [128, TT, EXP])
        order = t("order", [128, EXP])
        key = t("key", [128, TT, EXP])
        first = t("first", [128, TT, EXP])
        v1 = t("v1", [128, TT])
        v2 = t("v2", [128, TT])
        kmax = t("kmax", [128, TT])
        psA = ctx.enter_context(nc.psum_tensor("psA", [128, 2, CT], FP))
        psU = ctx.enter_context(nc.psum_tensor("psU", [128, 2, CT], FP))
        psL = ctx.enter_context(nc.psum_tensor("psL", [128, 2, 512], FP))

        in2, sqrt2, stat2, norm2, turn2, mod2, up2, silu2, logit2, logit_out, link2, diff2, prob2, order2 = (
            sm("in2"), sm("sqrt2"), sm("stat2"), sm("norm2"), sm("turn2"), sm("mod2"), sm("up2"),
            sm("silu2"), sm("logit2"), sm("logit_out"), sm("link2"), sm("diff2"), sm("prob2"),
            sm("order2"))
        IN = 6
        block = ctx.enter_context(nc.Block())

        @block.sync
        def _(sp):
            sp.dma_start(rw1_s[:], rw1).then_inc(in2, 16)
            sp.dma_start(rw2_s[:], rw2.rearrange("(k p) e -> p k e", p=128)).then_inc(in2, 16)
            sp.dma_start(rb1T[:], rb1.rearrange("(k p) -> p k", p=128),
                         allow_slow_non_contiguous=True).then_inc(in2, 16)
            sp.dma_start(rb2B[:], rb2.rearrange("(a e) -> a e", a=1).broadcast_to([128, EXP])).then_inc(in2, 16)
            sp.dma_start(b1T[:], b1.rearrange("x (k p) -> p x k", p=128),
                         allow_slow_non_contiguous=True).then_inc(in2, 16)
            sp.dma_start(b2T[:], b2.rearrange("x p -> p x"),
                         allow_slow_non_contiguous=True).then_inc(in2, 16)

        @block.gpsimd
        def _(pool):
            pool.iota(order[:], [[-1, EXP]], base=EXP, channel_multiplier=0,
                      allow_small_or_imprecise_dtypes=True).then_inc(order2, 1)

        @block.scalar
        def _(act):
            past(act, stat2, 1)
            act.activation(rstd[:], mv[:, :, 1], ACT.Sqrt).then_inc(sqrt2, 1)
            past(act, in2, 16 * IN)
            def step(c):
                for k in range(HK):
                    past(act, up2, HK * c + k + 1)
                    if k == 0:
                        past(act, logit2, c)
                    act.activation(hid[:, k, :], psU[:, k % 2, :], ACT.Silu,
                                   bias=rb1T[:, k:k + 1]).then_inc(silu2, 1)

            step(0)
            with act.Fori(1, CHUNKS) as c:
                step(c)
            past(act, diff2, 1)
            act.activation(v2[:], v2[:], ACT.Exp).then_inc(diff2, 1)

        @block.tensor
        def _(pe):
            past(pe, in2, 16 * IN)

            def turn(c, par):
                past(pe, norm2, c + 1)
                for k in range(CK):
                    mm = pe.transpose(psA[:, par, 128 * k:128 * k + 128], n2[:, par, k, :], ident[:])
                mm.then_inc(turn2, 1)

            def router(c, par):
                past(pe, mod2, c + 1)
                for k in range(HK):
                    if k < 2:
                        past(pe, silu2, HK * c)
                    else:
                        past(pe, silu2, HK * c + k - 1)
                    pe.matmul(psU[:, k % 2, :], rw1_s[:, 128 * k:128 * k + 128], h2T[:, par, :],
                              start=True, stop=True).then_inc(up2, 1)
                past(pe, silu2, HK * c + HK)
                past(pe, logit_out, c)
                for n in range(CK):
                    for k in range(HK):
                        mm = pe.matmul(psL[:, par, EXP * n:EXP * n + EXP],
                                       hid[:, k, 128 * n:128 * n + 128], rw2_s[:, k, :],
                                       start=(k == 0), stop=(k == HK - 1))
                mm.then_inc(logit2, 1)

            turn(0, 0)
            def step(c2):
                turn(2 * c2 + 1, 1)
                router(2 * c2, 0)
                turn(2 * c2 + 2, 0)
                router(2 * c2 + 1, 1)

            step(0)
            with pe.Fori(1, CHUNKS // 2 - 1) as c2:
                step(c2)
            turn(CHUNKS - 1, 1)
            router(CHUNKS - 2, 0)
            router(CHUNKS - 1, 1)

        @block.vector
        def _(dve):
            linked = {"base": 0, "n": 0}

            def then(i):
                i.then_inc(link2, 1)
                linked["n"] += 1
                past(dve, link2, linked["base"] + linked["n"])

            for n in range(TT):
                i = dve.bn_stats(stats2[:, n, :], X[:, n, :])
            then(i)
            for n in range(TT):
                i = dve.bn_aggr(mv[:, n, :], stats2[:, n, :])
            then(i)
            mvar = mv[:, :, 1]
            dve.tensor_scalar(mvar, mvar, EPS, None, ALU.add).then_inc(stat2, 1)
            past(dve, sqrt2, 1)
            then(dve.reciprocal(rstd[:], rstd[:]))
            newton(then, dve, rstd[:], mvar, tmp2[:])
            past(dve, in2, 16 * IN)

            def normalise(c, par):
                if not isinstance(c, int) or c >= 2:
                    past(dve, turn2, c - 1)
                for k in range(CK):
                    n = CK * c + k
                    i = dve.tensor_scalar(
                        n2[:, par, k, :], X[:, bass.ds(n, 1), :].rearrange("p a e -> p (a e)"),
                        mv[:, bass.ds(n, 1), 0:1].rearrange("p a e -> p (a e)"),
                        rstd[:, bass.ds(n, 1)], ALU.subtract, ALU.mult)
                i.then_inc(norm2, 1)

            def modulate(c, par):
                past(dve, turn2, c + 1)
                if not isinstance(c, int) or c >= 2:
                    past(dve, up2, HK * (c - 1))
                for k in range(2):
                    i = dve.tensor_scalar(h2T[:, par, S * k:S * k + S], psA[:, par, S * k:S * k + S],
                                          modT[:, 4, bass.ds(2 * c + k, 1)],
                                          modT[:, 3, bass.ds(2 * c + k, 1)], ALU.mult, ALU.add)
                i.then_inc(mod2, 1)
                past(dve, mod2, c + 1)
                high = h2H[:, bass.ds(CT * c, CT)]
                then(dve.tensor_copy(high, h2T[:, par, :]))
                dve.tensor_tensor(h2L[:, bass.ds(CT * c, CT)], h2T[:, par, :], high.bitcast(FP),
                                  ALU.subtract)

            def take(c, par):
                past(dve, logit2, c + 1)
                dve.tensor_tensor(logit[:, bass.ds(CK * c, CK), :],
                                  psL[:, par, 0:CK * EXP].rearrange("p (n e) -> p n e", e=EXP),
                                  rep(rb2B[:], 1, CK), ALU.add).then_inc(logit_out, 1)

            normalise(0, 0)
            modulate(0, 0)
            used = linked["n"]
            def step(c2):
                linked["base"], linked["n"] = 2 * c2 + used, 0
                normalise(2 * c2 + 1, 1)
                modulate(2 * c2 + 1, 1)
                take(2 * c2, 0)
                normalise(2 * c2 + 2, 0)
                modulate(2 * c2 + 2, 0)
                take(2 * c2 + 1, 1)
                assert linked["n"] == 2

            step(0)
            with dve.Fori(1, CHUNKS // 2 - 1) as c2:
                step(c2)
            linked["base"], linked["n"] = used + CHUNKS - 2, 0
            normalise(CHUNKS - 1, 1)
            modulate(CHUNKS - 1, 1)
            take(CHUNKS - 2, 0)
            take(CHUNKS - 1, 1)
            past(dve, order2, 1)
            past(dve, logit_out, CHUNKS)
            orderB = rep(order[:], 1, TT)
            for r, v in enumerate((v1, v2)):
                mask = (first, prob)[r]
                then(dve.tensor_reduce(v[:], logit[:], AX.X, ALU.max))
                then(dve.tensor_tensor(key[:], logit[:], rep(v[:], 2, EXP), ALU.is_equal))
                then(dve.tensor_tensor(key[:], key[:], orderB, ALU.mult))
                then(dve.tensor_reduce(kmax[:], key[:], AX.X, ALU.max))
                then(dve.tensor_tensor(mask[:], key[:], rep(kmax[:], 2, EXP), ALU.is_equal))
                if r == 0:
                    then(dve.scalar_tensor_tensor(out=logit[:], in0=first[:], scalar=-3e38,
                                                  in1=logit[:], op0=ALU.mult, op1=ALU.add))
            dve.tensor_tensor(v2[:], v2[:], v1[:], ALU.subtract).then_inc(diff2, 1)
            past(dve, diff2, 2)
            then(dve.tensor_scalar(v1[:], v2[:], 1.0, None, ALU.add))
            then(dve.reciprocal(v1[:], v1[:]))
            then(dve.tensor_tensor(v2[:], v2[:], v1[:], ALU.mult))
            then(dve.tensor_tensor(first[:], first[:], rep(v1[:], 2, EXP), ALU.mult))
            then(dve.tensor_tensor(prob[:], prob[:], rep(v2[:], 2, EXP), ALU.mult))
            dve.tensor_tensor(prob[:], prob[:], first[:], ALU.add).then_inc(prob2, 1)


def experts(nc, X, ident, modT, w1, w2, h2H, h2L, b1T, b2T, prob, out_v):
    with ExitStack() as ctx:
        def t(name, shape, dt=FP):
            return ctx.enter_context(nc.sbuf_tensor(name, shape, dt))

        def sm(name):
            return ctx.enter_context(nc.semaphore(name))

        raw = t("raw", [128, 2, 512])
        w1H = t("w1H", [128, EXP, HID], FR)
        w1L = t("w1L", [128, EXP, HID], FR)
        w2H = t("w2H", [128, EXP, HK, E], FR)
        w2L = t("w2L", [128, EXP, HK, E], FR)
        weT = t("weT", [128, 2, CT])
        F = t("F", [128, 2, CT])
        FH = t("FH", [128, 2, HK, CT], FR)
        FL = t("FL", [128, 2, HK, CT], FR)
        wy = t("wy", [128, 2, CT])
        acc = t("acc", [128, CT])
        probC = t("probC", [128, CK, EXP])
        prob_in = sm("prob_in")
        yo = t("yo", [128, CK, E])
        psU = ctx.enter_context(nc.psum_tensor("psH", [128, 2, CT], FP))
        psY = ctx.enter_context(nc.psum_tensor("psY", [128, 2, CT], FP))
        psW = ctx.enter_context(nc.psum_tensor("psW", [128, 2, CT], FP))
        psX = ctx.enter_context(nc.psum_tensor("psX", [128, CT], FP))
        w_in, w_split, w_link, up, silu, high, low, down, wide, wide_out, y_out, summed, alink, turned, added, stored = (
            [sm("w_in0"), sm("w_in1")], sm("w_split"), sm("w_link"), sm("up"), sm("silu"), sm("high"), sm("low"), sm("down"),
            sm("wide"), sm("wide_out"), sm("y_out"), sm("summed"), sm("alink"), sm("turned3"), sm("added"), sm("stored"))
        block = ctx.enter_context(nc.Block())

        @block.sync
        def _(sp):
            for n in range(2 * EXP):
                x = n // 2
                if n >= 2:
                    past(sp, w_split, n - 1)
                src = w1[x] if n % 2 == 0 else w2[x].rearrange("(k p) e -> p k e", p=128)
                dst = raw[:, n % 2, :]
                if n % 2:
                    dst = dst.rearrange("p (k e) -> p k e", k=HK)
                sp.dma_start(dst, src).then_inc(w_in[n % 2], 16)
            def step(c):
                past(sp, added, c + 1)
                sp.dma_start(out_v[:, bass.ds(CK * c, CK), :], yo[:]).then_inc(stored, 16)

            step(0)
            with sp.Fori(1, CHUNKS) as c:
                step(c)
            past(sp, stored, 16 * CHUNKS)

        @block.scalar
        def _(act):
            def step(c):
                for x in range(EXP):
                    n = EXP * c + x
                    past(act, wide, n + 1)
                    if x >= 2:
                        past(act, y_out, n - 1)
                    else:
                        past(act, y_out, EXP * c)
                    act.activation(weT[:, x % 2, :], psW[:, x % 2, :], ACT.Copy).then_inc(wide_out, 1)
                    for k in range(HK):
                        past(act, up, HK * n + k + 1)
                        if k >= 2:
                            past(act, low, HK * n + k - 1)
                        else:
                            past(act, low, HK * n)
                        act.activation(F[:, k % 2, :], psU[:, k % 2, :], ACT.Silu,
                                       bias=b1T[:, x, k:k + 1]).then_inc(silu, 1)
                        past(act, silu, HK * n + k + 1)
                        if k == 0 and x >= 2:
                            past(act, down, n - 1)
                        elif k == 0:
                            past(act, down, EXP * c)
                        act.activation(FH[:, x % 2, k, :], F[:, k % 2, :], ACT.Copy).then_inc(high, 1)

            step(0)
            with act.Fori(1, CHUNKS) as c:
                step(c)
        @block.tensor
        def _(pe):
            past(pe, w_split, 2 * EXP)

            def downs(n, x):
                past(pe, low, HK * n + HK)
                if x >= 2:
                    past(pe, y_out, n - 1)
                else:
                    past(pe, y_out, n - x)
                for k in range(HK):
                    for j, (a, f) in enumerate(((w2H, FH), (w2H, FL), (w2L, FH))):
                        mm = pe.matmul(psY[:, x % 2, :], a[:, x, k, :], f[:, x % 2, k, :],
                                       start=(k == 0 and j == 0), stop=(k == HK - 1 and j == 2))
                mm.then_inc(down, 1)

            def step(c):
                for x in range(EXP):
                    n = EXP * c + x
                    past(pe, wide_out, n - 1 if x >= 2 else EXP * c)
                    if x == 0:
                        past(pe, prob_in, c + 1)
                    for k in range(CK):
                        col = probC[:, k, x:x + 1]
                        mm = pe.transpose(psW[:, x % 2, 128 * k:128 * k + 128],
                                          col.broadcast_to([128, 128]), ident[:])
                    mm.then_inc(wide, 1)
                    for k in range(HK):
                        past(pe, silu, HK * n + k - 1 if k >= 2 else HK * n)
                        w = (w1H[:, x, 128 * k:128 * k + 128], w1L[:, x, 128 * k:128 * k + 128])
                        src = (h2H[:, bass.ds(CT * c, CT)], h2L[:, bass.ds(CT * c, CT)])
                        for j, (a, f) in enumerate(((0, 0), (0, 1), (1, 0))):
                            mm = pe.matmul(psU[:, k % 2, :], w[a], src[f], start=(j == 0), stop=(j == 2))
                        mm.then_inc(up, 1)
                    if x:
                        downs(n - 1, x - 1)
                downs(EXP * c + EXP - 1, EXP - 1)
                past(pe, summed, c + 1)
                past(pe, added, c)
                for k in range(CK):
                    mm = pe.transpose(psX[:, 128 * k:128 * k + 128], acc[:, 128 * k:128 * k + 128], ident[:])
                mm.then_inc(turned, 1)

            step(0)
            with pe.Fori(1, CHUNKS) as c:
                step(c)
        @block.vector
        def _(dve):
            for n in range(2 * EXP):
                x = n // 2
                past(dve, w_in[n % 2], 16 * (x + 1))
                hi = (w1H, w2H)[n % 2][:, x]
                lo = (w1L, w2L)[n % 2][:, x]
                if n % 2:
                    hi, lo = hi.rearrange("p k e -> p (k e)"), lo.rearrange("p k e -> p (k e)")
                dve.tensor_copy(hi, raw[:, n % 2, :]).then_inc(w_link, 1)
                past(dve, w_link, n + 1)
                dve.tensor_tensor(lo, raw[:, n % 2, :], hi.bitcast(FP), ALU.subtract).then_inc(w_split, 1)

            def step(c):
                past(dve, wide_out, EXP * c)
                dve.tensor_copy(probC[:], prob[:, bass.ds(CK * c, CK), :]).then_inc(prob_in, 1)
                for x in range(EXP + 1):
                    n = EXP * c + x
                    if x < EXP:
                        for k in range(HK):
                            past(dve, high, HK * n + k + 1)
                            dve.tensor_tensor(FL[:, x % 2, k, :], F[:, k % 2, :],
                                              FH[:, x % 2, k, :].bitcast(FP), ALU.subtract).then_inc(low, 1)
                    if x:
                        past(dve, down, n)
                        past(dve, wide_out, n)
                        dst = acc if x == 1 else wy
                        dst = acc[:] if x == 1 else wy[:, x % 2, :]
                        if x == 1:
                            past(dve, turned, c)
                        dve.scalar_tensor_tensor(out=dst, in0=psY[:, (x - 1) % 2, :],
                                                 scalar=b2T[:, x - 1:x],
                                                 in1=weT[:, (x - 1) % 2, :], op0=ALU.add, op1=ALU.mult).then_inc(y_out, 1)
                        past(dve, y_out, n)
                        if x > 1:
                            dve.tensor_tensor(acc[:], acc[:], dst, ALU.add).then_inc(alink, 1)
                            past(dve, alink, (EXP - 1) * c + x - 1)
                for k in range(2):
                    i = dve.tensor_scalar(acc[:, S * k:S * k + S], acc[:, S * k:S * k + S],
                                          modT[:, 5, bass.ds(2 * c + k, 1)], None, ALU.mult)
                i.then_inc(summed, 1)
                past(dve, turned, c + 1)
                past(dve, stored, 16 * c)
                dve.tensor_tensor(yo[:], psX[:].rearrange("p (k e) -> p k e", k=CK),
                                  X[:, bass.ds(CK * c, CK), :], ALU.add).then_inc(added, 1)

            step(0)
            with dve.Fori(1, CHUNKS) as c:
                step(c)
_INS = ['L0_attn_q', 'L0_attn_Wq', 'L0_attn_bq', 'L0_attn_Wk', 'L0_attn_bk', 'L0_attn_Wv',
        'L0_attn_bv', 'L0_attn_Wo', 'L0_attn_bo', 'L0_attn_rel_table', 'L0_ffn_rw1', 'L0_ffn_rb1',
        'L0_ffn_rw2', 'L0_ffn_rb2', 'L0_ffn_w1', 'L0_ffn_b1', 'L0_ffn_w2', 'L0_ffn_b2', 'L0_c',
        'L0_wmod']
_OUTS = [((16, 256, 128), 'float32')]


def kernel(**inputs):
    import numpy as _np
    import concourse.bacc as _bacc
    from concourse import mybir as _mybir
    from concourse.bass_utils import run_bass_kernel_spmd as _run

    nc = _bacc.Bacc("TRN2", target_bir_lowering=False, num_devices=1)
    arrays, args = {}, []
    for name in _INS:
        a = _np.ascontiguousarray(inputs[name])
        arrays[f"in_{name}_dram"] = a
        args.append(nc.dram_tensor(f"in_{name}_dram", a.shape, _mybir.dt.from_np(a.dtype), kind="ExternalInput").ap())
    for i, (shape, dtype) in enumerate(_OUTS):
        dt = _mybir.dt.from_np(_np.dtype(dtype))
        args.append(nc.dram_tensor(f"out_{i}_dram", shape, dt, kind="ExternalOutput").ap())
    program(nc, *args)
    r = _run(nc, [arrays], core_ids=[0])
    return r.results[0]["out_0_dram"]
```

```python
import concourse.bass as bass
from concourse import mybir
from contextlib import ExitStack

B, S, E = 16, 256, 128
H, D = 16, 8
REL = 64
HID, EXP = 512, 8
EPS = 1e-5
TT = B * S // 128

HH = H // 2
QG = 128 // HH
G = S // QG
PAIRS = G // 2
JB = S // 128
VW = 128 + D
TW = S + S - QG
FP = mybir.dt.float32
FR = mybir.dt.float32r
U32 = mybir.dt.uint32
ALU = mybir.AluOpType
ACT = mybir.ActivationFunctionType
AX = mybir.AxisListType


def rep(ap, axis, n):
    shape = list(ap.shape)
    shape.insert(axis, n)
    return ap.unsqueeze(axis).broadcast_to(shape)


SLOT_JOBS = [
    [["q"], ["r0"], ["r1"], ["r2"], ["r3", "r4"], ["r5"], ["r6", "r7"], ["hv"]],
    [["q"], ["r0"], ["r1", "y"], ["r2"], ["r3", "t"], ["r4", "r5"], ["r6", "r7"], ["v"]],
]


def jobs_before(half, slot, n, with_y=True):
    flat = [j for hh in range(2) for s, js in enumerate(SLOT_JOBS[hh])
            for i, j in enumerate(js) if (hh, s, i) < (half, slot, n)]
    return sum(with_y or j not in ("y", "t") for j in flat)


LINKS = 6
START_JOBS = 11
BATCH_JOBS = jobs_before(2, 0, 0)
FIRST_JOBS = jobs_before(2, 0, 0, False)


def job_count(b, half, slot, n):
    if isinstance(b, int) and b == 0:
        return START_JOBS + jobs_before(half, slot, n, False)
    return BATCH_JOBS * b + (START_JOBS + FIRST_JOBS - BATCH_JOBS) + jobs_before(half, slot, n)


def slot_jobs(b, half, slot, last=False):
    found = []
    for n, name in enumerate(SLOT_JOBS[half][slot]):
        if name in ("y", "t"):
            if isinstance(b, int) and b == 0:
                continue
        elif last and half:
            continue
        count = job_count(b, half, slot, n)
        if last and half:
            count = job_count(b, 1, 0, 0) + ("y", "t").index(name)
        if last and name == "hv":
            name = "-v"
        bank = count % 2 if isinstance(b, int) else job_count(1, half, slot, n) % 2
        found.append((name, count, bank))
    return found


assert BATCH_JOBS % 2 == 0
Y_TO_T = jobs_before(1, 4, 1) - jobs_before(1, 2, 1)


def prepared(b, half):
    if isinstance(b, int) and b == 0 and half == 0:
        return START_JOBS
    if half == 0:
        return job_count(b - 1, 1, 7, 0)
    return job_count(b, 0, 7, 0)


def program(nc, q, Wq, bq, Wk, bk, Wv, bv, Wo, bo, rel, rw1, rb1, rw2, rb2, w1, b1, w2, b2, c,
            wmod, out):
    x_v = q.rearrange("b (n p) e -> p (b n) e", p=128)
    out_v = out.rearrange("b (n p) e -> p (b n) e", p=128)
    with ExitStack() as ctx:
        def sb(name, shape, dt=FP):
            return ctx.enter_context(nc.sbuf_tensor(name, shape, dt))

        X = sb("X", [128, TT, E])
        ident = sb("ident", [128, 128])
        modT = sb("modT", [128, 6, B])
        mv = sb("mv", [128, TT, 2])
        rstd = sb("rstd", [128, TT])
        attention(nc, x_v, X, ident, modT, mv, rstd, Wq, bq, Wk, bk, Wv, bv, Wo, bo, rel, c, wmod)
        mixture(nc, X, ident, modT, mv, rstd, rw1, rb1, rw2, rb2, w1, b1, w2, b2, out_v)


def attention(nc, x_v, X, ident, modT, mv, rstd, Wq, bq, Wk, bk, Wv, bv, Wo, bo, rel, c, wmod):
    ctx = ExitStack()
    with ctx:
        def t(name, shape, dt=FP):
            return ctx.enter_context(nc.sbuf_tensor(name, shape, dt))

        WqD = t("WqD", [128, 2, 2, 64])
        WkD = t("WkD", [128, 2, 2, 64])
        Wv_s = t("Wv_s", [128, E])
        WoD = t("WoD", [128, 2, E])
        bqD = t("bqD", [128, 2])
        bkD = t("bkD", [128, 2])
        bvD = t("bvD", [128, 2])
        boC = t("boC", [128, 1])
        bo2 = t("bo2", [128, 1])
        gabo = t("gabo", [128, B])
        wmod_s = t("wmod_s", [128, 6 * E])
        c_s = t("c_s", [B, E])
        c_e = t("c_e", [B, E])
        cT = t("cT", [128, B])
        headM = t("headM", [128, HH])
        queryM = t("queryM", [128, QG])
        headL = t("headL", [128, HH])
        queryL = t("queryL", [128, QG])
        lowM = t("lowM", [128, 1])
        sel = t("sel", [128, 2, HH, 128], FR)
        selL = t("selL", [128, 2, HH, D])
        relA = t("relA", [128, D])
        relB = t("relB", [1, D])
        relR = t("relR", [128, QG, D])
        relRb = t("relRb", [1, QG, D])
        relT = t("relT", [128, 2 * REL + 1])
        Tf = t("Tf", [128, TW])
        TH = t("TH", [128, TW], FR)
        TL = t("TL", [128, TW], FR)
        stats = t("stats", [128, 4, 6])
        tmp = t("tmp", [128, TT])
        nrm = t("nrm", [128, 2, E])
        hT = t("hT", [128, S])
        X2t = t("X2t", [128, S], FR)
        X2 = t("X2", [128, S], FR)
        KH = t("KH", [128, 2, S], FR)
        KL = t("KL", [128, 2, S], FR)
        Qbd = t("Qbd", [128, 2, G, HH, QG], FR)
        QrH = t("QrH", [128, 2, G, HH, QG], FR)
        QrL = t("QrL", [128, 2, G, HH, QG], FR)
        V2 = t("V2", [128, 2, JB, HH * VW], FR)
        nmax = t("nmax", [128, 2, G])
        lsum = t("lsum", [128, 2, G])
        P = t("P", [128, 4, 512])
        PH = t("PH", [128, 2, PAIRS, 512], FR)
        PL = t("PL", [128, 2, PAIRS, 512], FR)
        linv = t("linv", [128, G])
        ldiag = t("ldiag", [128, G, QG])
        lrow = t("lrow", [128, S])
        ctxT = t("ctxT", [128, 2, S])
        yT = t("yT", [128, S])

        def pt(name, shape):
            return ctx.enter_context(nc.psum_tensor(name, shape, FP))

        psS = pt("psS", [128, 2, 512])
        psT = pt("psT", [128, 2, 512])
        psO = pt("psO", [128, 512])
        psP = pt("psP", [128, 2, 512])
        psZ = pt("psZ", [128, 512])

        def sm(name):
            return ctx.enter_context(nc.semaphore(name))

        weights_in, x_first, x_rest, rel_in, c_in = (
            sm("weights_in"), sm("x_first"), sm("x_rest"), sm("rel_in"), sm("c_in"))
        ident_done, masks_done, c_done, rel_rows, rel_turned = (
            sm("ident_done"), sm("masks_done"), sm("c_done"), sm("rel_rows"), sm("rel_turned"))
        rel_filled, rel_shifted, mod_full, setup_pe, setup_dve, sqrt_done = (
            sm("rel_filled"), sm("rel_shifted"), sm("mod_full"), sm("setup_pe"), sm("setup_dve"),
            sm("sqrt_done"))
        scores_done, max_done, exp_done, turned, high_done, low_done = (
            sm("scores_done"), sm("max_done"), sm("exp_done"), sm("turned"), sm("high_done"),
            sm("low_done"))
        values_done, ldiag_done, lrow_full, lrow_done, ctx_done = (
            sm("values_done"), sm("ldiag_done"), sm("lrow_full"), sm("lrow_done"), sm("ctx_done"))
        job_full, job_done, nrm_done, x2_done, qbd_done, link = (
            sm("job_full"), sm("job_done"), sm("nrm_done"), sm("x2_done"), sm("qbd_done"),
            sm("link"))

        W_DMAS = 2 + 2 + 1 + 2 + 6 + 1 + 1
        block = ctx.enter_context(nc.Block())

        @block.sync
        def _(sp):
            sp.dma_start(c_s[:], c).then_inc(c_in, 16)
            sp.dma_start(wmod_s[:], wmod).then_inc(weights_in, 16)
            sp.dma_start(X[:, 0:4, :], x_v[:, 0:4, :]).then_inc(x_first, 16)
            for k in range(2):
                sp.dma_start(WqD[:, :, k, :], Wq.rearrange("e (a m) -> e a m", a=2)).then_inc(weights_in, 16)
                sp.dma_start(WkD[:, :, k, :], Wk.rearrange("e (a m) -> e a m", a=2)).then_inc(weights_in, 16)
            sp.dma_start(Wv_s[:], Wv).then_inc(weights_in, 16)
            for k in range(2):
                sp.dma_start(WoD[64 * k:64 * k + 64, :, :], Wo.rearrange("(a m) e -> m a e", a=2)).then_inc(weights_in, 16)
                for src, dst in ((bq, bqD), (bk, bkD), (bv, bvD)):
                    sp.dma_start(dst[64 * k:64 * k + 64, :], src.rearrange("(a m) -> m a", a=2),
                                 allow_slow_non_contiguous=True).then_inc(weights_in, 16)
            sp.dma_start(boC[:], bo.rearrange("(e a) -> e a", a=1)).then_inc(weights_in, 16)
            sp.dma_start(X[:, 4:TT, :], x_v[:, 4:TT, :]).then_inc(x_rest, 16)

        @block.gpsimd
        def _(pool):
            pool.memset(ident[:], 0.0).then_inc(ident_done, 1)
            pool.wait_ge(ident_done, 1)
            pool.affine_select(out=ident[:], in_=ident[:], compare_op=ALU.not_equal, fill=1.0,
                               base=0, pattern=[[-1, 128]], channel_multiplier=1).then_inc(ident_done, 1)
            pool.memset(V2[:].bitcast(FP), 0.0).then_inc(ident_done, 1)

            def spread(b, half):
                pool.wait_ge(x2_done, 2 * b + half + 1)
                for a in range(2):
                    if a == 0 and not (isinstance(b, int) and b == 0):
                        pool.wait_ge(scores_done, PAIRS * (2 * b + half - 1))
                    g = slice(a * G // 2, (a + 1) * G // 2)
                    x2 = X2[:].bitcast(FP).rearrange("p (g i) -> p g i", i=QG)[:, g, :]
                    i = pool.tensor_tensor(
                        Qbd[:, half, g, :, :], rep(x2, 2, HH),
                        rep(rep(headM[:], 1, G // 2), 3, QG), ALU.mult)
                i.then_inc(qbd_done, 1)

            pool.wait_ge(masks_done, 1)
            spread(0, 0)
            spread(0, 1)
            with pool.Fori(1, B) as b:
                spread(b, 0)
                spread(b, 1)

        @block.scalar
        def _(act):
            act.dma_start(relA[:], rel[0:128, :]).then_inc(rel_in, 16)
            act.dma_start(relB[:], rel[128:129, :]).then_inc(rel_in, 16)
            act.wait_ge(c_in, 16)
            act.activation(c_e[:], c_s[:], ACT.Exp, scale=-1.0).then_inc(c_done, 1)
            act.wait_ge(rel_filled, 1)
            for i in range(QG):
                at = S - QG - REL + i
                act.dma_start(Tf[D * i:D * i + D, at:at + 2 * REL + 1],
                              relT[D * i:D * i + D, :]).then_inc(rel_shifted, 16)
            act.wait_ge(setup_dve, 1)
            act.activation(rstd[:], mv[:, :, 1], ACT.Sqrt).then_inc(sqrt_done, 1)

            def exps(b, half, p):
                n = 16 * b + 8 * half + p
                act.wait_ge(max_done, n + 1)
                if not (isinstance(b, int) and b == 0) or 8 * half + p >= 4:
                    act.wait_ge(turned, n - 3)
                for k in range(2):
                    g = 2 * p + k
                    i = act.activation(P[:, p % 4, 256 * k:256 * k + 256],
                                       psS[:, p % 2, 256 * k:256 * k + 256], ACT.Exp,
                                       bias=nmax[:, half, g:g + 1],
                                       accum_out=lsum[:, half, g:g + 1])
                i.then_inc(exp_done, 1)

            def high(b, half, p):
                n = 16 * b + 8 * half + p
                act.wait_ge(turned, n + 1)
                if not (isinstance(b, int) and b == 0) and p == 0:
                    act.wait_ge(values_done, 2 * b + half - 1)
                act.activation(PH[:, half, p, :], psT[:, p % 2, :], ACT.Copy).then_inc(high_done, 1)

            def rows(b, half):
                act.wait_ge(lrow_full, 2 * b + half + 1)
                if not (isinstance(b, int) and b == 0 and half == 0):
                    act.wait_ge(ctx_done, 2 * b + half)
                act.activation(lrow[:], psO[:, S:2 * S], ACT.Copy).then_inc(lrow_done, 1)

            def batch(b):
                for half in range(2):
                    pb, ph = (b, 0) if half else (b - 1, 1)
                    before = not (isinstance(b, int) and b == 0 and half == 0)
                    for p in range(PAIRS):
                        if p >= 2:
                            high(b, half, p - 2)
                        elif before:
                            high(pb, ph, PAIRS - 2 + p)
                        exps(b, half, p)
                        if p == 7 and before:
                            rows(pb, ph)

            batch(0)
            with act.Fori(1, B) as b:
                batch(b)
            high(B - 1, 1, PAIRS - 2)
            high(B - 1, 1, PAIRS - 1)
            rows(B - 1, 1)

        @block.tensor
        def _(pe):
            pe.wait_ge(ident_done, 2)
            pe.wait_ge(c_done, 3)
            pe.transpose(psZ[:, 0:B], c_s[:], ident[0:B, 0:B]).then_inc(setup_pe, 1)
            pe.wait_ge(c_done, 4)
            pe.wait_ge(weights_in, 16 * W_DMAS)
            for k in range(6):
                mm = pe.matmul(psP[:, 0, B * k:B * k + B], wmod_s[:, E * k:E * k + E], cT[:],
                               start=True, stop=True)
            mm.then_inc(mod_full, 1)
            for half in range(2):
                mm = pe.matmul(psP[:, 1, 0:1], WoD[0:64, half, :], bvD[0:64, half:half + 1],
                               start=(half == 0), stop=(half == 1))
            mm.then_inc(mod_full, 1)
            pe.wait_ge(rel_rows, 2)
            pe.transpose(psT[:, 0, 0:128], relR[:].rearrange("r i d -> r (i d)"), ident[:])
            pe.transpose(psT[:, 0, 128:129], relRb[:].rearrange("r i d -> r (i d)"),
                         ident[0:1, 0:1]).then_inc(rel_turned, 1)

            def job(count, bank, work):
                if not (isinstance(count, int) and count < 2):
                    pe.wait_ge(job_done, count - 1)
                work(psP[:, bank, :]).then_inc(job_full, 1)

            def turn_nrm(bank):
                for k in range(2):
                    mm = pe.transpose(bank[:, 128 * k:128 * k + 128], nrm[:, k, :], ident[:])
                return mm

            def values(bank, half, at):
                for k in range(JB):
                    mm = pe.matmul(bank[:, at + 64 * k:at + 64 * k + 64], hT[:, 128 * k:128 * k + 128],
                                   Wv_s[:, 64 * half:64 * half + 64], start=True, stop=True)
                return mm

            def project(bank, half):
                pe.matmul(bank[:, 0:S], WqD[:, half, :, :].rearrange("e a m -> e (a m)"), hT[:],
                          start=True, stop=True)
                return pe.matmul(bank[:, S:2 * S], WkD[:, half, :, :].rearrange("e a m -> e (a m)"),
                                 hT[:], start=True, stop=True)

            def spread(bank, r):
                part, h0 = r // 4, 2 * (r % 4)
                for k in range(2):
                    mm = pe.matmul(bank[:, S * k:S * k + S], sel[:, part, h0 + k, :], X2[:],
                                   start=True, stop=True)
                return mm

            def out_project(bank):
                for half in range(2):
                    mm = pe.matmul(bank[:, 0:S], WoD[:, half, :], ctxT[:, half, :],
                                   start=(half == 0), stop=(half == 1))
                return mm

            def turn_y(bank):
                for k in range(2):
                    mm = pe.transpose(bank[:, 128 * k:128 * k + 128], yT[:, 128 * k:128 * k + 128],
                                      ident[:])
                return mm

            def run_job(name, b, half, count, bank):
                other = 1 - half
                if name == "q":
                    if half:
                        pe.wait_ge(job_done, count)
                    job(count, bank, lambda k: project(k, other))
                elif name[0] == "r":
                    r = int(name[1])
                    if r == 0:
                        pe.wait_ge(job_done, count)
                    job(count, bank, lambda k: spread(k, r))
                elif name == "hv":
                    pe.wait_ge(nrm_done, b + 2)
                    def both(k):
                        turn_nrm(k)
                        return values(k, other, S)
                    job(count, bank, both)
                elif name == "v":
                    job(count, bank, lambda k: values(k, other, 0))
                elif name == "-v":
                    job(count, bank, lambda k: values(k, other, S))
                elif name == "y":
                    pe.wait_ge(ctx_done, 2 * b)
                    job(count, bank, out_project)
                elif name == "t":
                    last = isinstance(b, int) and b == B - 1
                    pe.wait_ge(job_done, count + 1 - (1 if last else Y_TO_T))
                    job(count, bank, turn_y)

            def scores(b, half, p):
                n = 16 * b + 8 * half + p
                if p == 0:
                    pe.wait_ge(job_done, prepared(b, half))
                    pe.wait_ge(qbd_done, 2 * b + half + 1)
                if not (isinstance(b, int) and b == 0) or 8 * half + p >= 2:
                    pe.wait_ge(exp_done, n - 1)
                for k in range(2):
                    g = 2 * p + k
                    dst = psS[:, p % 2, 256 * k:256 * k + 256]
                    at = S - QG - QG * g
                    qb = Qbd[:, half, g, :, :].rearrange("p h i -> p (h i)")
                    qh = QrH[:, half, g, :, :].rearrange("p h i -> p (h i)")
                    ql = QrL[:, half, g, :, :].rearrange("p h i -> p (h i)")
                    pe.matmul(dst, qb, KH[:, half, :], start=True, stop=False)
                    pe.matmul(dst, qb, KL[:, half, :], start=False, stop=False)
                    pe.matmul(dst, qh, TH[:, at:at + S], start=False, stop=False)
                    pe.matmul(dst, qh, TL[:, at:at + S], start=False, stop=False)
                    mm = pe.matmul(dst, ql, TH[:, at:at + S], start=False, stop=True)
                mm.then_inc(scores_done, 1)

            def turn(b, half, p):
                n = 16 * b + 8 * half + p
                pe.wait_ge(exp_done, n + 1)
                if not (isinstance(b, int) and b == 0) or 8 * half + p >= 2:
                    pe.wait_ge(low_done, n - 1)
                for k in range(4):
                    mm = pe.transpose(psT[:, p % 2, 128 * k:128 * k + 128],
                                      P[:, p % 4, 128 * k:128 * k + 128], ident[:])
                mm.then_inc(turned, 1)

            def weigh(b, half, part):
                if part == 0:
                    pe.wait_ge(low_done, 16 * b + 8 * half + 8)
                    if not (isinstance(b, int) and b == 0 and half == 0):
                        pe.wait_ge(ctx_done, 2 * b + half)
                for h in (2 * part, 2 * part + 1):
                    for k in range(JB):
                        for n, pr in enumerate((PH, PL)):
                            rhs = pr[:, half, :, :].rearrange("j p (t x) -> j (p t) x", t=2)
                            at = 128 * k + QG * h
                            mm = pe.matmul(psO[:, 0:S], V2[:, half, k, 128 * h:128 * h + 128],
                                           rhs[:, :, at:at + QG],
                                           start=(h == 0 and k == 0 and n == 0),
                                           stop=(h == HH - 1 and k == JB - 1 and n == 1))
                if part == 3:
                    mm.then_inc(values_done, 1)

            def spread_l(b, half):
                pe.wait_ge(ldiag_done, 2 * b + half + 1)
                pe.matmul(psO[:, S:2 * S], selL[:].rearrange("p a h d -> p (a h d)"),
                          ldiag[:].rearrange("p g i -> p (g i)"), start=True, stop=True)\
                    .then_inc(lrow_full, 1)

            pe.wait_ge(nrm_done, 1)
            job(0, 0, turn_nrm)
            pe.wait_ge(job_done, 1)
            job(1, 1, lambda k: values(k, 0, 0))
            job(2, 0, lambda k: project(k, 0))
            pe.wait_ge(job_done, 3)
            pe.wait_ge(masks_done, 1)
            for r in range(8):
                job(3 + r, (3 + r) % 2, lambda k, r=r: spread(k, r))

            def batch(b, last=False):
                first = isinstance(b, int) and b == 0
                for half in range(2):
                    pb, ph = (b, 0) if half else (b - 1, 1)
                    before = not (first and half == 0)
                    for p in range(PAIRS):
                        if p >= 2:
                            turn(b, half, p - 2)
                        elif before:
                            turn(pb, ph, PAIRS - 2 + p)
                        scores(b, half, p)
                        if p == 7 and before:
                            spread_l(pb, ph)
                        if 3 <= p < 7 and before:
                            weigh(pb, ph, p - 3)
                        for name, count, bank in slot_jobs(b, half, p, last):
                            run_job(name, b, half, count, bank)

            pe.wait_ge(setup_dve, 2)
            batch(0)
            with pe.Fori(1, B - 1) as b:
                batch(b)
            batch(B - 1, last=True)
            for p in (PAIRS - 2, PAIRS - 1):
                turn(B - 1, 1, p)
            for part in range(4):
                weigh(B - 1, 1, part)
            spread_l(B - 1, 1)
            done = job_count(B - 1, 1, 0, 0) + 2
            pe.wait_ge(ctx_done, 2 * B)
            job(done, done % 2, out_project)
            pe.wait_ge(job_done, done + 1)
            job(done + 1, (done + 1) % 2, turn_y)

        @block.vector
        def _(dve):
            linked = {"base": 0, "n": 0}

            def then(i):
                i.then_inc(link, 1)
                linked["n"] += 1
                dve.wait_ge(link, linked["base"] + linked["n"])

            dve.wait_ge(ident_done, 2)
            dve.tensor_reduce(headM[:], ident[:].rearrange("p (a h d) -> p h a d", a=2, d=D), AX.XY, ALU.add)
            dve.tensor_reduce(queryM[:], ident[:].rearrange("p (i d) -> p i d", d=D), AX.X, ALU.add)
            dve.tensor_reduce(headL[:], ident[:].rearrange("p (h i) -> p h i", i=QG), AX.X, ALU.add)
            dve.tensor_reduce(queryL[:], ident[:].rearrange("p (h i) -> p i h", i=QG), AX.X, ALU.add)
            then(dve.tensor_reduce(lowM[:], ident[:, 64:128], AX.X, ALU.add))
            for part in range(2):
                for h in range(HH):
                    at = 64 * part + D * h
                    dve.tensor_copy(sel[:, part, h, :].rearrange("p (i d) -> p i d", d=D),
                                    rep(ident[:, at:at + D], 1, QG))
            dve.tensor_copy(selL[:], rep(rep(headL[:], 1, 2), 3, D)).then_inc(masks_done, 1)
            dve.wait_ge(c_done, 1)
            dve.tensor_scalar(c_e[:], c_e[:], 1.0, None, ALU.add).then_inc(c_done, 1)
            dve.wait_ge(c_done, 2)
            then(dve.reciprocal(c_e[:], c_e[:]))
            dve.tensor_tensor(c_s[:], c_s[:], c_e[:], ALU.mult).then_inc(c_done, 1)
            dve.wait_ge(setup_pe, 1)
            dve.tensor_copy(cT[:], psZ[:, 0:B]).then_inc(c_done, 1)
            dve.wait_ge(rel_in, 32)
            dve.tensor_copy(relR[:], rep(relA[:], 1, QG)).then_inc(rel_rows, 1)
            dve.tensor_copy(relRb[:], rep(relB[:], 1, QG)).then_inc(rel_rows, 1)
            dve.wait_ge(rel_turned, 1)
            then(dve.tensor_copy(relT[:], psT[:, 0, 0:2 * REL + 1]))
            mid = S - QG
            dve.tensor_copy(Tf[:, 0:mid], relT[:, 0:1].broadcast_to([128, mid]))
            dve.tensor_copy(Tf[:, mid:TW], relT[:, 2 * REL:2 * REL + 1].broadcast_to([128, TW - mid]))\
                .then_inc(rel_filled, 1)
            dve.wait_ge(mod_full, 2)
            then(dve.tensor_copy(modT[:].rearrange("p k b -> p (k b)"), psP[:, 0, 0:6 * B]))
            for k in (1, 4):
                dve.tensor_scalar(modT[:, k, :], modT[:, k, :], 1.0, None, ALU.add)
            for k in (2, 5):
                then(dve.tensor_scalar(gabo[:], modT[:, k, :], 0.0, 2.0, ALU.is_ge, ALU.mult))
                then(dve.tensor_scalar(gabo[:], gabo[:], -1.0, None, ALU.add))
                then(dve.tensor_tensor(modT[:, k, :], modT[:, k, :], gabo[:], ALU.mult))
                then(dve.scalar_tensor_tensor(out=modT[:, k, :], in0=modT[:, k, :], scalar=0.25,
                                              in1=gabo[:], op0=ALU.max, op1=ALU.mult))
            then(dve.tensor_tensor(bo2[:], psP[:, 1, 0:1], boC[:], ALU.add))
            then(dve.tensor_scalar(gabo[:], modT[:, 2, :], bo2[:, 0:1], None, ALU.mult))
            then(dve.tensor_scalar(WkD[:].rearrange("e a b m -> e (a b m)"),
                                   WkD[:].rearrange("e a b m -> e (a b m)"), float(D) ** -0.5, None, ALU.mult))
            then(dve.tensor_scalar(bkD[:], bkD[:], float(D) ** -0.5, None, ALU.mult))
            for n in range(TT):
                if n in (0, 4):
                    dve.wait_ge(x_first if n == 0 else x_rest, 16)
                then(dve.bn_stats(stats[:, n % 4, :], X[:, n, :]))
                i = dve.bn_aggr(mv[:, n, :], stats[:, n % 4, :])
            then(i)
            mvar = mv[:, :, 1]
            dve.tensor_scalar(mvar, mvar, EPS, None, ALU.add).then_inc(setup_dve, 1)
            dve.wait_ge(sqrt_done, 1)
            then(dve.reciprocal(rstd[:], rstd[:]))
            newton(then, dve, rstd[:], mvar, tmp[:])
            dve.wait_ge(rel_shifted, 16 * QG)
            then(dve.tensor_copy(TH[:], Tf[:]))
            dve.tensor_tensor(TL[:], Tf[:], TH[:].bitcast(FP), ALU.subtract).then_inc(setup_dve, 1)

            def normalise(b):
                for k in range(2):
                    n = 2 * b + k
                    i = dve.tensor_scalar(nrm[:, k, :], at(X, n), at(mv, n, 0), at(rstd, n),
                                          ALU.subtract, ALU.mult)
                i.then_inc(nrm_done, 1)

            def at(tile, n, *more):
                if len(tile[:].shape) == 2:
                    return tile[:, bass.ds(n, 1)]
                v = tile[:, bass.ds(n, 1), :].rearrange("p a e -> p (a e)")
                return v[:, more[0]:more[0] + 1] if more else v

            def mod(k, b):
                return modT[:, k, bass.ds(b, 1)]

            def take(name, b, half, count, bank):
                other = 1 - half
                dve.wait_ge(job_full, count + 1)
                if name == "h":
                    i = dve.tensor_scalar(hT[:], bank[:, 0:S], mod(1, b), mod(0, b), ALU.mult, ALU.add)
                if name[-1] == "v":
                    src = bank[:, S:S + 128] if name in ("hv", "-v") else bank[:, 0:128]
                    src = src.rearrange("p (k h d) -> p k h d", k=JB, d=D)
                    win = V2[:, other, :, :].rearrange("p k (h c) -> p k h c", c=VW)
                    then(dve.tensor_copy(win[:, :, :, 0:D], src))
                    i = dve.tensor_tensor(win[:, :, :, 64:64 + D], src,
                                          win[:, :, :, 0:D].bitcast(FP), ALU.subtract)
                if name == "hv":
                    i = dve.tensor_scalar(hT[:], bank[:, 0:S], mod(1, b + 1), mod(0, b + 1),
                                          ALU.mult, ALU.add)
                elif name == "q":
                    if not (isinstance(b, int) and b == 0 and count == 2):
                        dve.wait_ge(qbd_done, 2 * b + half + 1)
                    qs, ks = bank[:, 0:S], bank[:, S:2 * S]
                    qbias, kbias = bqD[:, other:other + 1], bkD[:, other:other + 1]
                    dve.tensor_scalar(KH[:, other, :], ks, kbias, None, ALU.add)
                    then(dve.tensor_scalar(X2t[:], qs, qbias, lowM[:, 0:1], ALU.add, ALU.mult))
                    dve.scalar_tensor_tensor(out=X2[:], in0=qs, scalar=qbias,
                                             in1=X2t[:].bitcast(FP), op0=ALU.add,
                                             op1=ALU.subtract).then_inc(x2_done, 1)
                    i = dve.scalar_tensor_tensor(out=KL[:, other, :], in0=ks, scalar=kbias,
                                                 in1=KH[:, other, :].bitcast(FP), op0=ALU.add,
                                                 op1=ALU.subtract)
                elif name[0] == "r":
                    r = int(name[1])
                    dst = (QrH, QrL)[r // 4]
                    h0 = 2 * (r % 4)
                    i = dve.tensor_tensor(
                        dst[:, other, :, h0:h0 + 2, :].rearrange("p g h i -> p h g i"),
                        bank.rearrange("p (h g i) -> p h g i", h=2, i=QG),
                        rep(rep(queryM[:], 1, G), 1, 2), ALU.mult)
                elif name == "y":
                    i = dve.tensor_scalar(yT[:], bank[:, 0:S], mod(2, b - 1), gabo[:, bass.ds(b - 1, 1)],
                                          ALU.mult, ALU.add)
                elif name == "t":
                    xb = X[:, bass.ds(2 * (b - 1), 2), :]
                    i = dve.tensor_tensor(xb, bank[:, 0:S].rearrange("p (k e) -> p k e", k=2), xb,
                                          ALU.add)
                i.then_inc(job_done, 1)

            def maxima(b, half, p):
                dve.wait_ge(scores_done, 16 * b + 8 * half + p + 1)
                dve.tensor_reduce(nmax[:, half, 2 * p:2 * p + 2],
                                  psS[:, p % 2, :].rearrange("p (t j) -> p t j", t=2), AX.X,
                                  ALU.max, negate=True).then_inc(max_done, 1)

            def low(b, half, p):
                dve.wait_ge(high_done, 16 * b + 8 * half + p + 1)
                dve.tensor_tensor(PL[:, half, p, :], psT[:, p % 2, :], PH[:, half, p, :].bitcast(FP),
                                  ALU.subtract).then_inc(low_done, 1)

            def sums(b, half):
                dve.wait_ge(exp_done, 16 * b + 8 * half + 8)
                then(dve.reciprocal(linv[:], lsum[:, half, :]))
                dve.tensor_tensor(ldiag[:], rep(linv[:], 2, QG), rep(queryL[:], 1, G), ALU.mult)\
                    .then_inc(ldiag_done, 1)

            def context(b, half):
                dve.wait_ge(lrow_done, 2 * b + half + 1)
                dve.tensor_tensor(ctxT[:, half, :], psO[:, 0:S], lrow[:], ALU.mult)\
                    .then_inc(ctx_done, 1)

            dve.wait_ge(ident_done, 3)
            normalise(0)
            for n, name in enumerate(["h", "v", "q"] + [f"r{r}" for r in range(8)]):
                take(name, 0, 1, n, psP[:, n % 2, :])

            def batch(b, last=False):
                first = isinstance(b, int) and b == 0
                for half in range(2):
                    pb, ph = (b, 0) if half else (b - 1, 1)
                    before = not (first and half == 0)
                    for p in range(PAIRS):
                        if p == 0 and not first:
                            context(b - 1, half)
                        if p >= 2:
                            low(b, half, p - 2)
                        elif before:
                            low(pb, ph, PAIRS - 2 + p)
                        maxima(b, half, p)
                        if p == 2 and before:
                            sums(pb, ph)
                        if p == 5 and half == 0 and not last:
                            normalise(b + 1)
                        for name, count, bank in slot_jobs(b, half, p, last):
                            take(name, b, half, count, psP[:, bank, :])

            batch(0)
            used = linked["n"]
            per = LINKS
            with dve.Fori(1, B - 1) as b:
                linked["base"], linked["n"] = per * b + (used - per), 0
                batch(b)
                assert linked["n"] == per, linked["n"]
            linked["base"], linked["n"] = used + per * (B - 2), 0
            batch(B - 1, last=True)
            context(B - 1, 0)
            low(B - 1, 1, PAIRS - 2)
            low(B - 1, 1, PAIRS - 1)
            sums(B - 1, 1)
            context(B - 1, 1)
            done = job_count(B - 1, 1, 0, 0) + 2
            take("y", B, 1, done, psP[:, done % 2, :])
            take("t", B, 1, done + 1, psP[:, (done + 1) % 2, :])


def newton(then, dve, r, v, tmp):
    then(dve.tensor_tensor(tmp, r, r, ALU.mult))
    then(dve.tensor_tensor(tmp, tmp, v, ALU.mult))
    then(dve.tensor_scalar(tmp, tmp, -0.5, 1.5, ALU.mult, ALU.add))
    then(dve.tensor_tensor(r, r, tmp, ALU.mult))


def past(engine, semaphore, count):
    if not isinstance(count, int) or count > 0:
        engine.wait_ge(semaphore, count)


CT = 512
CHUNKS = B * S // CT
CK = CT // 128
HK = HID // 128
TOKENS = B * S
AREA = TOKENS + CT
ROW = E + 1
JOBS = (2 * TOKENS + EXP * (CT - 1)) // CT
UNUSED = EXP * AREA
NO_ROW = 2 * TOKENS


def mixture(nc, X, ident, modT, mv, rstd, rw1, rb1, rw2, rb2, w1, b1, w2, b2, out_v):
    with ExitStack() as ctx:
        def t(name, shape, dt=FP):
            return ctx.enter_context(nc.sbuf_tensor(name, shape, dt))

        slots_d = nc.dram_tensor("slots_d", (UNUSED + CT, ROW), FP, kind="Internal").ap()
        results_d = nc.dram_tensor("results_d", (2 * TOKENS, E), FP, kind="Internal").ap()
        W = t("W", [128, EXP, 2, 512])
        b1T = t("b1T", [128, EXP, HK])
        b2T = t("b2T", [128, EXP])
        p1 = t("p1", [128, TT])
        p2 = t("p2", [128, TT])
        gbB = t("gbB", [128, B, E])
        firstrow = t("firstrow", [128, JOBS], U32)
        expert = t("expert", [128, JOBS], U32)
        route(nc, X, ident, modT, mv, rstd, rw1, rb1, rw2, rb2, w1, w2, b1, b2, slots_d, W, b1T,
              b2T, p1, p2, gbB, firstrow, expert)
        experts(nc, ident, slots_d, results_d, W, b1T, b2T, firstrow, expert)
        combine(nc, X, results_d, p1, p2, gbB, out_v)


def route(nc, X, ident, modT, mv, rstd, rw1, rb1, rw2, rb2, w1, w2, b1, b2, slots_d, W, b1T,
          b2T, p1, p2, gbB, firstrow, expert):
    with ExitStack() as ctx:
        def t(name, shape, dt=FP):
            return ctx.enter_context(nc.sbuf_tensor(name, shape, dt))

        def pt(name, shape):
            return ctx.enter_context(nc.psum_tensor(name, shape, FP))

        def sm(name):
            return ctx.enter_context(nc.semaphore(name))

        rw1_s = t("rw1_s", [128, HID])
        rw2_s = t("rw2_s", [128, HK, EXP])
        rb1T = t("rb1T", [128, HK])
        rb2B = t("rb2B", [128, EXP])
        stats2 = t("stats2", [128, TT, 6])
        tmp2 = t("tmp2", [128, TT])
        n2 = t("n2", [128, 2, CK, E])
        h2T = t("h2T", [128, 2, CT])
        hid = t("hid", [128, HK, CT])
        rows = t("rows", [128, 2, 2, CK, ROW])
        logit = t("logit", [128, CK, EXP])
        v1 = t("v1", [128, TT])
        v2 = t("v2", [128, TT])
        key = t("key", [128, CK, EXP])
        kmax = t("kmax", [128, CK])
        chosen = t("chosen", [128, 2, 2, CK, EXP])
        both = t("both", [128, 2, CK, EXP])
        earlier = t("earlier", [128, 2, CK + 1, EXP])
        slot_f = t("slot_f", [128, 2, CK])
        slot_u = t("slot_u", [128, 2, 2, CK], U32)
        slot_e = t("slot_e", [128, CK, EXP])
        slot_c = t("slot_c", [128, 2, CK, EXP])
        order = t("order", [128, EXP])
        area = t("area", [128, EXP])
        token = t("token", [128, 2, TT])
        before = t("before", [128, 128])
        ones = t("ones", [128, 128])
        fill = t("fill", [128, CK, ROW])
        gbR = t("gbR", [B, E])
        steps = t("steps", [128, EXP, EXP])
        until = t("until", [128, EXP, EXP])
        cnt = t("cnt", [128, EXP])
        cnt_u = t("cnt_u", [128, EXP], U32)
        wide = t("wide", [128, EXP, EXP])
        ntile = t("ntile", [128, EXP])
        cum = t("cum", [128, EXP])
        jobno = t("jobno", [128, JOBS])
        gone = t("gone", [128, JOBS, EXP])
        gone_t = t("gone_t", [128, JOBS, EXP])
        ex = t("ex", [128, JOBS])
        start = t("start", [128, JOBS])

        psA = pt("psA", [128, 2, CT])
        psU = pt("psU", [128, 2, CT])
        psB = pt("psB", [128, 512])
        psL = pt("psL", [128, 512])
        psR = pt("psR", [128, 512])

        in2, weights2, sqrt2, stat2, norm2, turn2, mod2, up2, silu2, logit2, link2 = (
            sm("in2"), sm("weights2"), sm("sqrt2"), sm("stat2"), sm("norm2"), sm("turn2"),
            sm("mod2"), sm("up2"), sm("silu2"), sm("logit2"), sm("link2"))
        took, chose, ranked, slotted, back, rows_done, diff2, const2, gate2, filled = (
            sm("took"), sm("chose"), sm("ranked"), sm("slotted"), sm("back"), sm("rows_done"),
            sm("diff2"), sm("const2"), sm("gate2"), sm("filled"))
        counted, table, rows_out = sm("counted"), sm("table"), sm("rows_out")
        sent = [sm("sent0"), sm("sent1")]
        IN = 6
        block = ctx.enter_context(nc.Block())

        @block.sync
        def _(sp):
            sp.dma_start(rw1_s[:], rw1).then_inc(in2, 16)
            sp.dma_start(rw2_s[:], rw2.rearrange("(k p) e -> p k e", p=128)).then_inc(in2, 16)
            sp.dma_start(rb1T[:], rb1.rearrange("(k p) -> p k", p=128),
                         allow_slow_non_contiguous=True).then_inc(in2, 16)
            sp.dma_start(rb2B[:], rb2.rearrange("(a e) -> a e", a=1).broadcast_to([128, EXP])).then_inc(in2, 16)
            sp.dma_start(b1T[:], b1.rearrange("x (k p) -> p x k", p=128),
                         allow_slow_non_contiguous=True).then_inc(in2, 16)
            sp.dma_start(b2T[:], b2.rearrange("x p -> p x"),
                         allow_slow_non_contiguous=True).then_inc(in2, 16)
            sp.dma_start(W[:, :, 0, :], w1.rearrange("x p h -> p x h")).then_inc(weights2, 16)
            for x in range(EXP):
                sp.dma_start(W[:, x, 1, :].rearrange("p (k e) -> p k e", k=HK),
                             w2[x].rearrange("(k p) e -> p k e", p=128)).then_inc(weights2, 16)
            sp.wait_ge(const2, 2)
            sp.dma_start(slots_d[UNUSED:UNUSED + CT, :].rearrange("(p k) e -> p k e", p=128),
                         fill[:]).then_inc(filled, 16)
            sp.wait_ge(table, 1)
            for x in range(EXP):
                n = sp.value_load(cnt_u[0:1, x:x + 1], min_val=0, max_val=TOKENS)
                sp.dma_start(slots_d[bass.ds(n + AREA * x, CT), :].rearrange("(p k) e -> p k e", p=128),
                             fill[:]).then_inc(filled, 16)
            sp.wait_ge(filled, 16 * (EXP + 1))
            sp.wait_ge(weights2, 16 * (1 + EXP))

        @block.gpsimd
        def _(pool):
            pool.memset(fill[:], 0.0).then_inc(const2, 1)
            pool.wait_ge(const2, 1)
            pool.memset(fill[:, :, E:ROW], float(NO_ROW))
            pool.memset(ones[:], 1.0).then_inc(const2, 1)
            pool.wait_ge(const2, 2)
            pool.affine_select(out=before[:], in_=ones[:], compare_op=ALU.is_gt, fill=0.0, base=0,
                               pattern=[[1, 128]], channel_multiplier=-1)
            pool.iota(order[:], [[-1, EXP]], base=EXP, channel_multiplier=0,
                      allow_small_or_imprecise_dtypes=True)
            pool.iota(area[:], [[AREA, EXP]], base=0, channel_multiplier=0,
                      allow_small_or_imprecise_dtypes=True)
            pool.iota(token[:], [[TOKENS, 2], [128, TT]], base=0, channel_multiplier=1,
                      allow_small_or_imprecise_dtypes=True)
            pool.iota(steps[:], [[0, EXP], [CT, EXP]], base=0, channel_multiplier=0,
                      allow_small_or_imprecise_dtypes=True)
            pool.iota(until[:], [[1, EXP], [-1, EXP]], base=0, channel_multiplier=0,
                      allow_small_or_imprecise_dtypes=True)
            pool.iota(jobno[:], [[1, JOBS]], base=0, channel_multiplier=0,
                      allow_small_or_imprecise_dtypes=True).then_inc(const2, 1)

            def dispatch(c, par):
                pool.wait_ge(slotted, c + 1)
                pool.wait_ge(rows_out, c + 1)
                for j in range(2):
                    for k in range(CK):
                        pool.indirect_dma_start(
                            out=slots_d,
                            out_offset=bass.IndirectOffsetOnAxis(ap=slot_u[:, par, j, k:k + 1], axis=0),
                            in_=rows[:, par, j, k, :], in_offset=None).then_inc(sent[par], 16)

            for c in range(CHUNKS):
                dispatch(c, c % 2)
            for par in range(2):
                pool.wait_ge(sent[par], 16 * 2 * CK * CHUNKS // 2)

        @block.scalar
        def _(act):
            act.wait_ge(stat2, 1)
            act.activation(rstd[:], mv[:, :, 1], ACT.Sqrt).then_inc(sqrt2, 1)
            act.wait_ge(in2, 16 * IN)
            act.wait_ge(gate2, 1)
            act.activation(gbR[:], psL[0:B, 0:E], ACT.Copy).then_inc(gate2, 1)
            for g in range(B * E // 512):
                act.wait_ge(gate2, 3 + g)
                act.activation(gbB[:, 4 * g:4 * g + 4, :].rearrange("p b e -> p (b e)"),
                               (psB, psL)[g % 2][:], ACT.Copy).then_inc(rows_done, 1)

            def step(c, par):
                for k in range(HK):
                    past(act, up2, HK * c + k + 1)
                    if k == 0:
                        past(act, logit2, c)
                    act.activation(hid[:, k, :], psU[:, k % 2, :], ACT.Silu,
                                   bias=rb1T[:, k:k + 1]).then_inc(silu2, 1)
                act.wait_ge(back, c + 1)
                if not isinstance(c, int) or c >= 2:
                    act.wait_ge(sent[par], (c - par) * (16 * CK))
                for j in range(2):
                    i = act.activation(rows[:, par, j, :, 0:E],
                                       psB[:].rearrange("p (k e) -> p k e", k=CK), ACT.Copy)
                i.then_inc(rows_out, 1)

            for c in range(2):
                step(c, c)
            with act.Fori(1, CHUNKS // 2) as m:
                step(2 * m, 0)
                step(2 * m + 1, 1)
            act.wait_ge(diff2, 1)
            act.activation(p2[:], v2[:], ACT.Exp).then_inc(diff2, 1)

        @block.tensor
        def _(pe):
            pe.wait_ge(in2, 16 * IN)
            pe.transpose(psL[0:B, 0:E], modT[:, 5, :], ident[:]).then_inc(gate2, 1)
            pe.wait_ge(gate2, 2)
            for g in range(B * E // 512):
                if g >= 2:
                    pe.wait_ge(rows_done, g - 1)
                for k in range(4):
                    b = 4 * g + k
                    mm = pe.matmul((psB, psL)[g % 2][:, 128 * k:128 * k + 128],
                                   ident[0:B, b:b + 1].broadcast_to([B, 128]), gbR[:],
                                   start=True, stop=True)
                mm.then_inc(gate2, 1)
            pe.wait_ge(rows_done, B * E // 512)

            def turn(c, par):
                pe.wait_ge(norm2, c + 1)
                past(pe, mod2, c - 1)
                for k in range(CK):
                    mm = pe.transpose(psA[:, par, 128 * k:128 * k + 128], n2[:, par, k, :], ident[:])
                mm.then_inc(turn2, 1)

            def rank(c, par):
                pe.wait_ge(chose, c + 1)
                past(pe, slotted, c)
                pe.matmul(psR[:, 0:CK * EXP], before[:], both[:, par, :, :].rearrange("p k e -> p (k e)"),
                          start=True, stop=False)
                pe.matmul(psR[:, 0:CK * EXP], ones[:],
                          earlier[:, par, 0:CK, :].rearrange("p k e -> p (k e)"),
                          start=False, stop=True).then_inc(ranked, 1)

            def step(c, par, last=False):
                if not last:
                    turn(c + 1, 1 - par)
                pe.wait_ge(mod2, c + 1)
                for k in range(HK):
                    past(pe, silu2, HK * c + k - 1)
                    pe.matmul(psU[:, k % 2, :], rw1_s[:, 128 * k:128 * k + 128], h2T[:, par, :],
                              start=True, stop=True).then_inc(up2, 1)
                past(pe, rows_out, c)
                for k in range(CK):
                    mm = pe.transpose(psB[:, 128 * k:128 * k + 128],
                                      h2T[:, par, 128 * k:128 * k + 128], ident[:])
                mm.then_inc(back, 1)
                if not isinstance(c, int) or c > 0:
                    rank(c - 1, 1 - par)
                pe.wait_ge(silu2, HK * c + HK)
                past(pe, took, c)
                for n in range(CK):
                    for k in range(HK):
                        mm = pe.matmul(psL[:, EXP * n:EXP * n + EXP],
                                       hid[:, k, 128 * n:128 * n + 128], rw2_s[:, k, :],
                                       start=(k == 0), stop=(k == HK - 1))
                mm.then_inc(logit2, 1)

            turn(0, 0)
            for c in range(3):
                step(c, c % 2)
            with pe.Fori(1, CHUNKS // 2 - 1) as m:
                step(2 * m + 1, 1)
                step(2 * m + 2, 0)
            step(CHUNKS - 1, 1, last=True)
            rank(CHUNKS - 1, 1)
            pe.wait_ge(slotted, CHUNKS)
            pe.matmul(psR[:, 0:EXP], ones[:], earlier[:, 1, CK, :], start=True, stop=True)\
                .then_inc(counted, 1)

        @block.vector
        def _(dve):
            linked = {"base": 0, "n": 0}

            def then(i):
                i.then_inc(link2, 1)
                linked["n"] += 1
                dve.wait_ge(link2, linked["base"] + linked["n"])

            for n in range(TT):
                i = dve.bn_stats(stats2[:, n, :], X[:, n, :])
            then(i)
            for n in range(TT):
                i = dve.bn_aggr(mv[:, n, :], stats2[:, n, :])
            then(i)
            mvar = mv[:, :, 1]
            dve.tensor_scalar(mvar, mvar, EPS, None, ALU.add).then_inc(stat2, 1)
            dve.wait_ge(sqrt2, 1)
            then(dve.reciprocal(rstd[:], rstd[:]))
            newton(then, dve, rstd[:], mvar, tmp2[:])
            dve.wait_ge(in2, 16 * IN)
            dve.wait_ge(const2, 3)
            dve.tensor_scalar(until[:], until[:], 0.0, None, ALU.is_ge)
            then(dve.memset(earlier[:], 0.0))

            def normalise(c, par):
                past(dve, turn2, c - 1)
                for k in range(CK):
                    n = CK * c + k
                    i = dve.tensor_scalar(
                        n2[:, par, k, :], X[:, bass.ds(n, 1), :].rearrange("p a e -> p (a e)"),
                        mv[:, bass.ds(n, 1), 0:1].rearrange("p a e -> p (a e)"),
                        rstd[:, bass.ds(n, 1)], ALU.subtract, ALU.mult)
                i.then_inc(norm2, 1)

            def modulate(c, par):
                dve.wait_ge(turn2, c + 1)
                past(dve, back, c - 1)
                for k in range(2):
                    i = dve.tensor_scalar(h2T[:, par, S * k:S * k + S], psA[:, par, S * k:S * k + S],
                                          modT[:, 4, bass.ds(2 * c + k, 1)],
                                          modT[:, 3, bass.ds(2 * c + k, 1)], ALU.mult, ALU.add)
                i.then_inc(mod2, 1)

            def choose(c, par):
                dve.wait_ge(logit2, c + 1)
                dve.tensor_tensor(logit[:], psL[:, 0:CK * EXP].rearrange("p (n e) -> p n e", e=EXP),
                                  rep(rb2B[:], 1, CK), ALU.add).then_inc(took, 1)
                dve.wait_ge(took, c + 1)
                for r, v in enumerate((v1, v2)):
                    v = v[:, bass.ds(CK * c, CK)]
                    mask = chosen[:, par, r, :, :]
                    then(dve.tensor_reduce(v, logit[:], AX.X, ALU.max))
                    then(dve.tensor_tensor(key[:], logit[:], rep(v, 2, EXP), ALU.is_equal))
                    then(dve.tensor_tensor(key[:], key[:], rep(order[:], 1, CK), ALU.mult))
                    then(dve.tensor_reduce(kmax[:], key[:], AX.X, ALU.max))
                    then(dve.tensor_tensor(mask, key[:], rep(kmax[:], 2, EXP), ALU.is_equal))
                    if r == 0:
                        then(dve.scalar_tensor_tensor(out=logit[:], in0=mask, scalar=-3e38,
                                                      in1=logit[:], op0=ALU.mult, op1=ALU.add))
                dve.tensor_copy(earlier[:, par, 0, :], earlier[:, 1 - par, CK, :])
                then(dve.tensor_tensor(both[:, par, :, :], chosen[:, par, 0, :, :],
                                       chosen[:, par, 1, :, :], ALU.add))
                for k in range(CK):
                    i = dve.tensor_tensor(earlier[:, par, k + 1, :], earlier[:, par, k, :],
                                          both[:, par, k, :], ALU.add)
                    if k < CK - 1:
                        then(i)
                i.then_inc(chose, 1)
                dve.wait_ge(chose, c + 1)

            def slots(c, par):
                dve.wait_ge(ranked, c + 1)
                if not isinstance(c, int) or c >= 2:
                    dve.wait_ge(sent[par], (c - par) * (16 * CK))
                then(dve.tensor_tensor(slot_e[:], psR[:, 0:CK * EXP].rearrange("p (k e) -> p k e", e=EXP),
                                       rep(area[:], 1, CK), ALU.add))
                then(dve.tensor_tensor(slot_c[:], chosen[:, par, :, :, :], rep(slot_e[:], 1, 2),
                                       ALU.mult))
                then(dve.tensor_reduce(slot_f[:], slot_c[:], AX.X, ALU.add))
                dve.tensor_copy(rows[:, par, :, :, E:ROW].rearrange("p j k a -> p j (k a)"),
                                token[:, :, bass.ds(CK * c, CK)])
                dve.tensor_copy(slot_u[:, par, :, :], slot_f[:]).then_inc(slotted, 1)
                dve.wait_ge(slotted, c + 1)

            normalise(0, 0)
            modulate(0, 0)

            def step(c, par, last=False):
                if not last:
                    normalise(c + 1, 1 - par)
                    modulate(c + 1, 1 - par)
                if not isinstance(c, int) or c > 0:
                    slots(c - 1, 1 - par)
                choose(c, par)

            for c in range(3):
                step(c, c % 2)
            used = linked["n"]
            LINKS2 = 18
            with dve.Fori(1, CHUNKS // 2 - 1) as m:
                linked["base"], linked["n"] = 2 * LINKS2 * m + (used - 2 * LINKS2), 0
                step(2 * m + 1, 1)
                step(2 * m + 2, 0)
                assert linked["n"] == 2 * LINKS2, linked["n"]
            linked["base"], linked["n"] = used + LINKS2 * (CHUNKS - 4), 0
            step(CHUNKS - 1, 1, last=True)
            slots(CHUNKS - 1, 1)
            dve.tensor_tensor(v2[:], v2[:], v1[:], ALU.subtract).then_inc(diff2, 1)
            dve.wait_ge(counted, 1)
            then(dve.tensor_copy(cnt[:], psR[:, 0:EXP]))
            dve.tensor_copy(cnt_u[:], cnt[:]).then_inc(table, 1)
            then(dve.tensor_tensor(wide[:], rep(cnt[:], 2, EXP), steps[:], ALU.is_gt))
            then(dve.tensor_reduce(ntile[:], wide[:], AX.X, ALU.add))
            then(dve.tensor_tensor(wide[:], rep(ntile[:], 1, EXP), until[:], ALU.mult))
            then(dve.tensor_reduce(cum[:], wide[:], AX.X, ALU.add))
            then(dve.tensor_tensor(gone[:], rep(jobno[:], 2, EXP), rep(cum[:], 1, JOBS), ALU.is_ge))
            then(dve.tensor_tensor(gone_t[:], gone[:], rep(ntile[:], 1, JOBS), ALU.mult))
            dve.tensor_reduce(ex[:], gone[:], AX.X, ALU.add)
            then(dve.tensor_reduce(start[:], gone_t[:], AX.X, ALU.add))
            then(dve.tensor_tensor(start[:], jobno[:], start[:], ALU.subtract))
            then(dve.tensor_scalar(start[:], start[:], float(CT), None, ALU.mult))
            then(dve.scalar_tensor_tensor(out=start[:], in0=ex[:], scalar=float(AREA), in1=start[:],
                                          op0=ALU.mult, op1=ALU.add))
            dve.tensor_scalar(ex[:], ex[:], float(EXP - 1), None, ALU.min)
            then(dve.tensor_scalar(start[:], start[:], float(UNUSED), None, ALU.min))
            dve.tensor_copy(expert[:], ex[:])
            dve.tensor_copy(firstrow[:], start[:])
            dve.wait_ge(diff2, 2)
            then(dve.tensor_scalar(p1[:], p2[:], 1.0, None, ALU.add))
            then(dve.reciprocal(p1[:], p1[:]))
            dve.tensor_tensor(p2[:], p2[:], p1[:], ALU.mult)


def experts(nc, ident, slots_d, results_d, W, b1T, b2T, firstrow, expert):
    with ExitStack() as ctx:
        def t(name, shape, dt=FP):
            return ctx.enter_context(nc.sbuf_tensor(name, shape, dt))

        def pt(name, shape):
            return ctx.enter_context(nc.psum_tensor(name, shape, FP))

        def sm(name):
            return ctx.enter_context(nc.semaphore(name))

        x = t("x", [128, 2, CK, ROW])
        w1H = t("w1H", [128, 2, HID], FR)
        w1L = t("w1L", [128, 2, HID], FR)
        w2H = t("w2H", [128, 2, HID], FR)
        w2L = t("w2L", [128, 2, HID], FR)
        xH = t("xH", [128, 2, CT], FR)
        xL = t("xL", [128, 2, CT], FR)
        F = t("F", [128, 2, CT])
        FH = t("FH", [128, 2, HK, CT], FR)
        FL = t("FL", [128, 2, HK, CT], FR)
        yT = t("yT2", [128, 2, CT])
        y = t("y", [128, 2, CK, E])
        row_f = t("row_f", [128, JOBS, CK])
        row_u = t("row_u", [128, 2, CK], U32)

        psX = pt("psX", [128, CT])
        psH = pt("psH", [128, 2, CT])
        psD = pt("psD", [128, 2, CT])
        psY = pt("psY", [128, 2, CT])

        x_in = [sm("x_in0"), sm("x_in1")]
        y_sent = [sm("y_sent0"), sm("y_sent1")]
        x_turned, x_high, x_low, w1_high, w1_low, w2_high, w2_low = (
            sm("x_turned"), sm("x_high"), sm("x_low"), sm("w1_high"), sm("w1_low"), sm("w2_high"),
            sm("w2_low"))
        up, silu, high, low, down, y_biased, y_turned, y_rows, rows_known = (
            sm("up"), sm("silu"), sm("high"), sm("low"), sm("down"), sm("y_biased"),
            sm("y_turned"), sm("y_rows"), sm("rows_known"))
        block = ctx.enter_context(nc.Block())

        def each(step, engine):
            for j in range(3):
                step(j, j % 2)
            with engine.Fori(1, JOBS // 2 - 1) as m:
                step(2 * m + 1, 1)
                step(2 * m + 2, 0)
            for j in range(JOBS - 2, JOBS + 2):
                step(j, j % 2)

        assert JOBS % 2

        def has(j, n):
            return (j + n >= 0 and j + n < JOBS) if isinstance(j, int) else True

        def of_tile(engine, j):
            return engine.value_load(expert[0:1, bass.ds(j, 1)], min_val=0, max_val=EXP - 1)

        @block.sync
        def _(sp):
            def load(j, par):
                past(sp, x_turned, j - 1)
                past(sp, rows_known, j - 1)
                n = sp.value_load(firstrow[0:1, bass.ds(j, 1)], min_val=0, max_val=UNUSED)
                sp.dma_start(x[:, par, :, :], slots_d[bass.ds(n, CT), :].rearrange(
                    "(p k) e -> p k e", p=128)).then_inc(x_in[par], 16)

            for j in range(3):
                load(j, j % 2)
            with sp.Fori(1, JOBS // 2) as m:
                load(2 * m + 1, 1)
                load(2 * m + 2, 0)

        @block.gpsimd
        def _(pool):
            def send(j, par):
                pool.wait_ge(y_rows, j + 1)
                for k in range(CK):
                    pool.indirect_dma_start(
                        out=results_d,
                        out_offset=bass.IndirectOffsetOnAxis(ap=row_u[:, par, k:k + 1], axis=0),
                        in_=y[:, par, k, :], in_offset=None, bounds_check=2 * TOKENS - 1,
                        oob_is_err=False).then_inc(y_sent[par], 16)

            for j in range(JOBS):
                send(j, j % 2)
            for par in range(2):
                pool.wait_ge(y_sent[par], 16 * CK * ((JOBS + 1 - par) // 2))

        def sent_before(j, par):
            return (j - par) * (16 * CK // 2)

        @block.scalar
        def _(act):
            def split_x(j, par):
                act.wait_ge(x_turned, j + 1)
                past(act, up, HK * (j - 1))
                act.activation(xH[:, par, :], psX[:], ACT.Copy).then_inc(x_high, 1)

            def split_w1(j, par):
                e = of_tile(act, j)
                past(act, up, HK * (j - 1))
                act.activation(w1H[:, par, :], W[:, bass.ds(e, 1), 0, :].rearrange("p a h -> p (a h)"),
                               ACT.Copy).then_inc(w1_high, 1)

            split_w1(0, 0)
            split_x(0, 0)

            def step(j, par):
                if has(j, 1):
                    split_x(j + 1, 1 - par)
                    split_w1(j + 1, 1 - par)
                if has(j, 0):
                    e = of_tile(act, j)
                for k in range(HK):
                    if has(j, 0):
                        act.wait_ge(up, HK * j + k + 1)
                        past(act, low, HK * j + k - 1)
                        act.activation(F[:, k % 2, :], psH[:, k % 2, :], ACT.Silu,
                                       bias=b1T[:, bass.ds(e, 1), k:k + 1].rearrange("p a k -> p (a k)"))\
                            .then_inc(silu, 1)
                        act.wait_ge(silu, HK * j + k + 1)
                        if k == 0:
                            past(act, down, j - 1)
                        act.activation(FH[:, par, k, :], F[:, k % 2, :], ACT.Copy).then_inc(high, 1)
                    if k == 1 and has(j, -2):
                        act.wait_ge(y_turned, j - 1)
                        if not isinstance(j, int) or j >= 4:
                            act.wait_ge(y_sent[par], sent_before(j - 2, par))
                        act.activation(y[:, par, :, :], psY[:, par, :].rearrange("p (k e) -> p k e", k=CK),
                                       ACT.Copy).then_inc(y_rows, 1)
                    if k == 2 and has(j, 0):
                        past(act, down, j - 1)
                        act.activation(w2H[:, par, :], W[:, bass.ds(e, 1), 1, :].rearrange("p a h -> p (a h)"),
                                       ACT.Copy).then_inc(w2_high, 1)

            each(step, act)

        @block.tensor
        def _(pe):
            def turn_x(j, par):
                pe.wait_ge(x_in[par], (j - par + 2) * 8)
                past(pe, x_high, j)
                past(pe, x_low, j)
                for k in range(CK):
                    mm = pe.transpose(psX[:, 128 * k:128 * k + 128], x[:, par, k, 0:E], ident[:])
                mm.then_inc(x_turned, 1)

            def step(j, par):
                if has(j, 1):
                    turn_x(j + 1, 1 - par)
                if has(j, 0):
                    pe.wait_ge(x_low, j + 1)
                    pe.wait_ge(w1_low, j + 1)
                for k in range(HK):
                    if has(j, 0):
                        past(pe, silu, HK * j + k - 1)
                        at = slice(128 * k, 128 * k + 128)
                        pe.matmul(psH[:, k % 2, :], w1H[:, par, at], xH[:, par, :], start=True, stop=False)
                        pe.matmul(psH[:, k % 2, :], w1H[:, par, at], xL[:, par, :], start=False, stop=False)
                        pe.matmul(psH[:, k % 2, :], w1L[:, par, at], xH[:, par, :], start=False, stop=True)\
                            .then_inc(up, 1)
                    if k == 1 and has(j, -2):
                        pe.wait_ge(y_biased, j - 1)
                        past(pe, y_rows, j - 3)
                        for i in range(CK):
                            mm = pe.transpose(psY[:, par, 128 * i:128 * i + 128],
                                              yT[:, par, 128 * i:128 * i + 128], ident[:])
                        mm.then_inc(y_turned, 1)
                if has(j, -1):
                    n, q = j - 1, 1 - par
                    pe.wait_ge(w2_low, n + 1)
                    pe.wait_ge(low, HK * n + HK)
                    past(pe, y_biased, n - 1)
                    for k in range(HK):
                        at = slice(128 * k, 128 * k + 128)
                        pe.matmul(psD[:, q, :], w2H[:, q, at], FH[:, q, k, :], start=(k == 0), stop=False)
                        pe.matmul(psD[:, q, :], w2H[:, q, at], FL[:, q, k, :], start=False, stop=False)
                        mm = pe.matmul(psD[:, q, :], w2L[:, q, at], FH[:, q, k, :], start=False,
                                       stop=(k == HK - 1))
                    mm.then_inc(down, 1)

            turn_x(0, 0)
            each(step, pe)

        @block.vector
        def _(dve):
            def split_x(j, par):
                dve.wait_ge(x_high, j + 1)
                past(dve, up, HK * (j - 1))
                dve.tensor_copy(row_f[:, bass.ds(j, 1), :], x[:, par, :, E:ROW].rearrange("p k a -> p a k"))\
                    .then_inc(rows_known, 1)
                dve.tensor_tensor(xL[:, par, :], psX[:], xH[:, par, :].bitcast(FP), ALU.subtract)\
                    .then_inc(x_low, 1)

            def split_w(j, par, n, hi, lo, hi_done, lo_done):
                e = of_tile(dve, j)
                dve.wait_ge(hi_done, j + 1)
                dve.tensor_tensor(lo[:, par, :], W[:, bass.ds(e, 1), n, :].rearrange("p a h -> p (a h)"),
                                  hi[:, par, :].bitcast(FP), ALU.subtract).then_inc(lo_done, 1)

            split_w(0, 0, 0, w1H, w1L, w1_high, w1_low)
            split_x(0, 0)

            def step(j, par):
                if has(j, -2):
                    n = j - 2
                    e = of_tile(dve, n)
                    dve.wait_ge(down, n + 1)
                    past(dve, y_turned, n - 1)
                    if not isinstance(j, int) or n >= 2:
                        dve.wait_ge(y_sent[par], sent_before(n, par))
                    dve.tensor_copy(row_u[:, par, :], row_f[:, bass.ds(n, 1), :].rearrange("p a k -> p (a k)"))
                    dve.tensor_scalar(yT[:, par, :], psD[:, par, :], b2T[:, bass.ds(e, 1)], None,
                                      ALU.add).then_inc(y_biased, 1)
                if has(j, 1):
                    split_x(j + 1, 1 - par)
                    split_w(j + 1, 1 - par, 0, w1H, w1L, w1_high, w1_low)
                for k in range(HK):
                    if has(j, 0):
                        dve.wait_ge(high, HK * j + k + 1)
                        if k == 0:
                            past(dve, down, j - 1)
                        dve.tensor_tensor(FL[:, par, k, :], F[:, k % 2, :],
                                          FH[:, par, k, :].bitcast(FP), ALU.subtract).then_inc(low, 1)
                        if k == 2:
                            split_w(j, par, 1, w2H, w2L, w2_high, w2_low)

            each(step, dve)


def combine(nc, X, results_d, p1, p2, gbB, out_v):
    with ExitStack() as ctx:
        def t(name, shape, dt=FP):
            return ctx.enter_context(nc.sbuf_tensor(name, shape, dt))

        def sm(name):
            return ctx.enter_context(nc.semaphore(name))

        y1 = t("y1", [128, TT, E])
        y2 = t("y2", [128, TT, E])
        loaded = [sm(f"loaded{c}") for c in range(CHUNKS)]
        weighted, summed, gated, added, stored = (
            sm("weighted"), sm("summed"), sm("gated"), sm("added"), sm("stored"))
        block = ctx.enter_context(nc.Block())

        @block.sync
        def _(sp):
            for c in range(CHUNKS):
                at = slice(CK * c, CK * c + CK)
                for j, y in enumerate((y1, y2)):
                    src = results_d[TOKENS * j:TOKENS * j + TOKENS, :].rearrange("(n p) e -> p n e", p=128)
                    sp.dma_start(y[:, at, :], src[:, at, :]).then_inc(loaded[c], 16)
            for c in range(CHUNKS):
                at = slice(CK * c, CK * c + CK)
                sp.wait_ge(added, c + 1)
                sp.dma_start(out_v[:, at, :], y2[:, at, :]).then_inc(stored, 16)
            sp.wait_ge(stored, 16 * CHUNKS)

        @block.scalar
        def _(act):
            for c in range(CHUNKS):
                act.wait_ge(loaded[c], 32)
                for k in range(CK):
                    n = CK * c + k
                    i = act.activation(y1[:, n, :], y1[:, n, :], ACT.Copy, scale=p1[:, n:n + 1])
                i.then_inc(weighted, 1)

        @block.vector
        def _(dve):
            for c in range(CHUNKS):
                at = slice(CK * c, CK * c + CK)
                dve.wait_ge(weighted, c + 1)
                for k in range(CK):
                    n = CK * c + k
                    i = dve.scalar_tensor_tensor(out=y2[:, n, :], in0=y2[:, n, :], scalar=p2[:, n:n + 1],
                                                 in1=y1[:, n, :], op0=ALU.mult, op1=ALU.add)
                i.then_inc(summed, 1)
                dve.wait_ge(summed, c + 1)
                yb = y2[:, at, :].rearrange("p (b k) e -> p b k e", b=2)
                dve.tensor_tensor(yb, yb, rep(gbB[:, 2 * c:2 * c + 2, :], 2, 2), ALU.mult)\
                    .then_inc(gated, 1)

        @block.gpsimd
        def _(pool):
            for c in range(CHUNKS):
                at = slice(CK * c, CK * c + CK)
                pool.wait_ge(gated, c + 1)
                pool.tensor_tensor(y2[:, at, :], y2[:, at, :], X[:, at, :], ALU.add).then_inc(added, 1)


_INS = ['L0_attn_q', 'L0_attn_Wq', 'L0_attn_bq', 'L0_attn_Wk', 'L0_attn_bk', 'L0_attn_Wv',
        'L0_attn_bv', 'L0_attn_Wo', 'L0_attn_bo', 'L0_attn_rel_table', 'L0_ffn_rw1', 'L0_ffn_rb1',
        'L0_ffn_rw2', 'L0_ffn_rb2', 'L0_ffn_w1', 'L0_ffn_b1', 'L0_ffn_w2', 'L0_ffn_b2', 'L0_c',
        'L0_wmod']
_OUTS = [((16, 256, 128), 'float32')]


def kernel(**inputs):
    import numpy as _np
    import concourse.bacc as _bacc
    from concourse import mybir as _mybir
    from concourse.bass_utils import run_bass_kernel_spmd as _run

    nc = _bacc.Bacc("TRN2", target_bir_lowering=False, num_devices=1)
    arrays, args = {}, []
    for name in _INS:
        a = _np.ascontiguousarray(inputs[name])
        arrays[f"in_{name}_dram"] = a
        args.append(nc.dram_tensor(f"in_{name}_dram", a.shape, _mybir.dt.from_np(a.dtype), kind="ExternalInput").ap())
    for i, (shape, dtype) in enumerate(_OUTS):
        dt = _mybir.dt.from_np(_np.dtype(dtype))
        args.append(nc.dram_tensor(f"out_{i}_dram", shape, dt, kind="ExternalOutput").ap())
    program(nc, *args)
    r = _run(nc, [arrays], core_ids=[0])
    return r.results[0]["out_0_dram"]
```

```python
import concourse.bass as bass
from concourse import mybir
from contextlib import ExitStack

B, S, E = 16, 256, 128
H, D = 16, 8
REL = 64
HID, EXP = 512, 8
EPS = 1e-5
TT = B * S // 128

HH = H // 2
QG = 128 // HH
G = S // QG
PAIRS = G // 2
JB = S // 128
VW = 128 + D
TW = S + S - QG
FP = mybir.dt.float32
FR = mybir.dt.float32r
U32 = mybir.dt.uint32
ALU = mybir.AluOpType
ACT = mybir.ActivationFunctionType
AX = mybir.AxisListType


def rep(ap, axis, n):
    shape = list(ap.shape)
    shape.insert(axis, n)
    return ap.unsqueeze(axis).broadcast_to(shape)


SLOT_JOBS = [
    [["q"], [], ["r0"], ["r1"], ["r2", "r3"], ["r4", "r5"], ["r6", "r7"], ["hv"]],
    [["q"], [], ["r0", "y"], ["r1", "r2"], ["r3", "t"], ["r4", "r5"], ["r6", "r7"], ["v"]],
]


def jobs_before(half, slot, n, with_y=True):
    flat = [j for hh in range(2) for s, js in enumerate(SLOT_JOBS[hh])
            for i, j in enumerate(js) if (hh, s, i) < (half, slot, n)]
    return sum(with_y or j not in ("y", "t") for j in flat)


LINKS = 8
START_JOBS = 11
BATCH_JOBS = jobs_before(2, 0, 0)
FIRST_JOBS = jobs_before(2, 0, 0, False)


def job_count(b, half, slot, n):
    if isinstance(b, int) and b == 0:
        return START_JOBS + jobs_before(half, slot, n, False)
    return BATCH_JOBS * b + (START_JOBS + FIRST_JOBS - BATCH_JOBS) + jobs_before(half, slot, n)


def slot_jobs(b, half, slot, last=False):
    found = []
    for n, name in enumerate(SLOT_JOBS[half][slot]):
        if name in ("y", "t"):
            if isinstance(b, int) and b == 0:
                continue
        elif last and half:
            continue
        count = job_count(b, half, slot, n)
        if last and half:
            count = job_count(b, 1, 0, 0) + ("y", "t").index(name)
        if last and name == "hv":
            name = "-v"
        bank = count % 2 if isinstance(b, int) else job_count(1, half, slot, n) % 2
        found.append((name, count, bank))
    return found


assert BATCH_JOBS % 2 == 0
Y_TO_T = jobs_before(1, 4, 1) - jobs_before(1, 2, 1)


def prepared(b, half):
    if isinstance(b, int) and b == 0 and half == 0:
        return START_JOBS
    if half == 0:
        return job_count(b - 1, 1, 7, 0)
    return job_count(b, 0, 7, 0)


CT = 512
CHUNKS = B * S // CT
CK = CT // 128
EARLY = slice(0, 2 * CK)
LATER = slice(2 * CK, TT)
HK = HID // 128
TOKENS = B * S
ET = 512
EK = ET // 128
MOST = -(-TOKENS // ET)
AREA = TOKENS + ET
ROW = E + 1
JOBS = (2 * TOKENS + EXP * (ET - 1)) // ET
UNUSED = EXP * AREA
NO_ROW = 2 * TOKENS


def program(nc, q, Wq, bq, Wk, bk, Wv, bv, Wo, bo, rel, rw1, rb1, rw2, rb2, w1, b1, w2, b2, c,
            wmod, out):
    x_v = q.rearrange("b (n p) e -> p (b n) e", p=128)
    out_v = out.rearrange("b (n p) e -> p (b n) e", p=128)
    with ExitStack() as ctx:
        def sb(name, shape, dt=FP):
            return ctx.enter_context(nc.sbuf_tensor(name, shape, dt))

        X = sb("X", [128, TT, E])
        ident = sb("ident", [128, 128])
        modT = sb("modT", [128, 6, B])
        mv = sb("mv", [128, TT, 2])
        rstd = sb("rstd", [128, TT])
        rw1_s = sb("rw1_s", [128, HID])
        rw2_s = sb("rw2_s", [128, HK, 128])
        rb1T = sb("rb1T", [128, HK])
        rb2T = sb("rb2T", [128, 1])
        b1T = sb("b1T", [128, EXP, HK])
        b2T = sb("b2T", [128, EXP])
        ahead = [(rw1_s[:], rw1),
                 (rw2_s[:, :, 0:EXP], rw2.rearrange("(k p) e -> p k e", p=128)),
                 (rb1T[:], rb1.rearrange("(k p) -> p k", p=128)),
                 (rb2T[0:EXP, :], rb2.rearrange("(e a) -> e a", a=1)),
                 (b1T[:], b1.rearrange("x (k p) -> p x k", p=128)),
                 (b2T[:], b2.rearrange("x p -> p x"))]
        attention(nc, x_v, X, ident, modT, mv, rstd, Wq, bq, Wk, bk, Wv, bv, Wo, bo, rel, c, wmod,
                  ahead, (rw2_s, rb2T))
        mixture(nc, X, ident, modT, mv, rstd, rw1_s, rb1T, rw2_s, rb2T, w1, b1T, w2, b2T, out_v)


def attention(nc, x_v, X, ident, modT, mv, rstd, Wq, bq, Wk, bk, Wv, bv, Wo, bo, rel, c, wmod,
              ahead, padded):
    ctx = ExitStack()
    with ctx:
        def t(name, shape, dt=FP):
            return ctx.enter_context(nc.sbuf_tensor(name, shape, dt))

        Wqk = t("Wqk", [128, 2, 2, 64])
        Wv_s = t("Wv_s", [128, E])
        WoD = t("WoD", [128, 2, E])
        bqk = t("bqk", [128, 2])
        bvT = t("bvT", [64, 2])
        boC = t("boC", [128, 1])
        bo2 = t("bo2", [128, 1])
        gabo = t("gabo", [128, B])
        wmod_s = t("wmod_s", [128, 6 * E])
        c_s = t("c_s", [B, E])
        c_e = t("c_e", [B, E])
        cT = t("cT", [128, B])
        headM = t("headM", [128, HH])
        queryM = t("queryM", [128, QG])
        headL = t("headL", [128, HH])
        queryL = t("queryL", [128, QG])
        sel = t("sel", [128, 2, HH, 128], FR)
        selL = t("selL", [128, 2, HH, D])
        relA = t("relA", [128, D])
        relB = t("relB", [1, D])
        relR = t("relR", [128, QG, D])
        relRb = t("relRb", [1, QG, D])
        relT = t("relT", [128, 2 * REL + 1])
        Tf = t("Tf", [128, TW])
        TH = t("TH", [128, TW], FR)
        TL = t("TL", [128, TW], FR)
        stats = t("stats", [128, TT, 6])
        tmp = t("tmp", [128, TT])
        nrm = t("nrm", [128, 2, E])
        hT = t("hT", [128, S])
        X2 = t("X2", [128, S], FR)
        KK = t("KK", [128, 2, 2, S], FR)
        Qbd = t("Qbd", [128, 2, G, HH, QG], FR)
        QrH = t("QrH", [128, 2, G, HH, QG], FR)
        QrL = t("QrL", [128, 2, G, HH, QG], FR)
        V2 = t("V2", [128, 2, JB, HH * VW], FR)
        nmax = t("nmax", [128, 2, G])
        lsum = t("lsum", [128, 2, G])
        P = t("P", [128, 4, 512])
        PH = t("PH", [128, 2, PAIRS, 512], FR)
        PL = t("PL", [128, 2, PAIRS, 512], FR)
        linv = t("linv", [128, G])
        ldiag = t("ldiag", [128, G, QG])
        lrow = t("lrow", [128, S])
        ctxT = t("ctxT", [128, 2, S])
        yT = t("yT", [128, S])

        def pt(name, shape):
            return ctx.enter_context(nc.psum_tensor(name, shape, FP))

        psS = pt("psS", [128, 2, 512])
        psT = pt("psT", [128, 2, 512])
        psO = pt("psO", [128, 512])
        psP = pt("psP", [128, 2, 512])
        psZ = pt("psZ", [128, 512])

        def sm(name):
            return ctx.enter_context(nc.semaphore(name))

        weights_in, wmod_in, x_first, x_rest, rel_in, c_in = (
            sm("weights_in"), sm("wmod_in"), sm("x_first"), sm("x_rest"), sm("rel_in"), sm("c_in"))
        ident_done, masks_done, c_done, rel_rows, rel_turned = (
            sm("ident_done"), sm("masks_done"), sm("c_done"), sm("rel_rows"), sm("rel_turned"))
        rel_filled, rel_shifted, mod_full, setup_pe, setup_dve, sqrt_done = (
            sm("rel_filled"), sm("rel_shifted"), sm("mod_full"), sm("setup_pe"), sm("setup_dve"),
            sm("sqrt_done"))
        rel_odd, ahead_in = sm("rel_odd"), sm("ahead_in")
        scores_done, max_done, exp_done, turned, high_done, low_done = (
            sm("scores_done"), sm("max_done"), sm("exp_done"), sm("turned"), sm("high_done"),
            sm("low_done"))
        values_done, ldiag_done, lrow_full, lrow_done, ctx_done = (
            sm("values_done"), sm("ldiag_done"), sm("lrow_full"), sm("lrow_done"), sm("ctx_done"))
        job_full, job_done, nrm_done, x2_done, keys_done, qbd_done, link = (
            sm("job_full"), sm("job_done"), sm("nrm_done"), sm("x2_done"), sm("keys_done"),
            sm("qbd_done"), sm("link"))

        W_DMAS = 2 + 2 + 1 + 1 + 2 + 1
        block = ctx.enter_context(nc.Block())

        @block.sync
        def _(sp):
            sp.dma_start(c_s[:], c).then_inc(c_in, 16)
            sp.dma_start(X[:, EARLY, :], x_v[:, EARLY, :]).then_inc(x_first, 16)
            sp.dma_start(wmod_s[:], wmod).then_inc(wmod_in, 16)
            sp.dma_start(X[:, LATER, :], x_v[:, LATER, :]).then_inc(x_rest, 16)
            for k, (w, bias) in enumerate(((Wq, bq), (Wk, bk))):
                sp.dma_start(Wqk[:, :, k, :], w.rearrange("e (a m) -> e a m", a=2)).then_inc(weights_in, 16)
                sp.dma_start(bqk[64 * k:64 * k + 64, :], bias.rearrange("(a m) -> m a", a=2),
                             allow_slow_non_contiguous=True).then_inc(weights_in, 16)
            sp.dma_start(bvT[:], bv.rearrange("(a m) -> m a", a=2),
                         allow_slow_non_contiguous=True).then_inc(weights_in, 16)
            sp.dma_start(Wv_s[:], Wv).then_inc(weights_in, 16)
            for k in range(2):
                sp.dma_start(WoD[64 * k:64 * k + 64, :, :], Wo.rearrange("(a m) e -> m a e", a=2)).then_inc(weights_in, 16)
            sp.dma_start(boC[:], bo.rearrange("(e a) -> e a", a=1)).then_inc(weights_in, 16)
            sp.wait_ge(ident_done, 1)
            for dst, src in ahead:
                sp.dma_start(dst, src, allow_slow_non_contiguous=True).then_inc(ahead_in, 16)
            sp.wait_ge(ahead_in, 16 * len(ahead))

        @block.gpsimd
        def _(pool):
            for tile in padded:
                pool.memset(tile[:], 0.0)
            pool.memset(ident[:], 0.0).then_inc(ident_done, 1)
            pool.wait_ge(ident_done, 1)
            pool.affine_select(out=ident[:], in_=ident[:], compare_op=ALU.not_equal, fill=1.0,
                               base=0, pattern=[[-1, 128]], channel_multiplier=1).then_inc(ident_done, 1)
            pool.memset(V2[:].bitcast(FP), 0.0).then_inc(ident_done, 1)

            pool.wait_ge(rel_filled, 1)
            for i in range(1, QG, 2):
                at = S - QG - REL + i
                pool.dma_start(Tf[D * i:D * i + D, at:at + 2 * REL + 1],
                               relT[D * i:D * i + D, :]).then_inc(rel_odd, 16)

            def spread(b, half):
                pool.wait_ge(x2_done, 2 * b + half + 1)
                for a in range(2):
                    if a == 0 and not (isinstance(b, int) and b == 0):
                        pool.wait_ge(scores_done, PAIRS * (2 * b + half - 1))
                    g = slice(a * G // 2, (a + 1) * G // 2)
                    x2 = X2[:].bitcast(FP).rearrange("p (g i) -> p g i", i=QG)[:, g, :]
                    i = pool.tensor_tensor(
                        Qbd[:, half, g, :, :], rep(x2, 2, HH),
                        rep(rep(headM[:], 1, G // 2), 3, QG), ALU.mult)
                i.then_inc(qbd_done, 1)

            pool.wait_ge(masks_done, 1)
            spread(0, 0)
            spread(0, 1)
            with pool.Fori(1, B) as b:
                spread(b, 0)
                spread(b, 1)

        @block.scalar
        def _(act):
            act.dma_start(relA[:], rel[0:128, :]).then_inc(rel_in, 16)
            act.dma_start(relB[:], rel[128:129, :]).then_inc(rel_in, 16)
            act.wait_ge(c_in, 16)
            act.activation(c_e[:], c_s[:], ACT.Exp, scale=-1.0).then_inc(c_done, 1)
            act.wait_ge(rel_filled, 1)
            for i in range(0, QG, 2):
                at = S - QG - REL + i
                act.dma_start(Tf[D * i:D * i + D, at:at + 2 * REL + 1],
                              relT[D * i:D * i + D, :]).then_inc(rel_shifted, 16)
            act.wait_ge(setup_dve, 1)
            act.activation(rstd[:], mv[:, :, 1], ACT.Sqrt).then_inc(sqrt_done, 1)

            def exps(b, half, p):
                n = 16 * b + 8 * half + p
                act.wait_ge(max_done, n + 1)
                if not (isinstance(b, int) and b == 0) or 8 * half + p >= 4:
                    act.wait_ge(turned, n - 3)
                for k in range(2):
                    g = 2 * p + k
                    i = act.activation(P[:, p % 4, 256 * k:256 * k + 256],
                                       psS[:, p % 2, 256 * k:256 * k + 256], ACT.Exp,
                                       bias=nmax[:, half, g:g + 1],
                                       accum_out=lsum[:, half, g:g + 1])
                i.then_inc(exp_done, 1)

            def high(b, half, p):
                n = 16 * b + 8 * half + p
                act.wait_ge(turned, n + 1)
                if not (isinstance(b, int) and b == 0) and p == 0:
                    act.wait_ge(values_done, 2 * b + half - 1)
                act.activation(PH[:, half, p, :], psT[:, p % 2, :], ACT.Copy).then_inc(high_done, 1)

            def rows(b, half):
                act.wait_ge(lrow_full, 2 * b + half + 1)
                if not (isinstance(b, int) and b == 0 and half == 0):
                    act.wait_ge(ctx_done, 2 * b + half)
                act.activation(lrow[:], psO[:, S:2 * S], ACT.Copy).then_inc(lrow_done, 1)

            def copy_keys(half, jobs):
                act.wait_ge(job_done, jobs)
                act.activation(KK[0:64, half, :, :], KK[64:128, half, :, :], ACT.Copy)\
                    .then_inc(keys_done, 1)

            def batch(b, last=False):
                for half in range(2):
                    pb, ph = (b, 0) if half else (b - 1, 1)
                    before = not (isinstance(b, int) and b == 0 and half == 0)
                    for p in range(PAIRS):
                        if p >= 2:
                            high(b, half, p - 2)
                        elif before:
                            high(pb, ph, PAIRS - 2 + p)
                        exps(b, half, p)
                        if p == 2 and not (last and half):
                            copy_keys(1 - half, job_count(b, half, 0, 0) + 1)
                        if p == 7 and before:
                            rows(pb, ph)

            copy_keys(0, 3)
            batch(0)
            with act.Fori(1, B - 1) as b:
                batch(b)
            batch(B - 1, last=True)
            high(B - 1, 1, PAIRS - 2)
            high(B - 1, 1, PAIRS - 1)
            act.wait_ge(setup_dve, 3)
            act.activation(rstd[:, EARLY], mv[:, EARLY, 1], ACT.Sqrt).then_inc(sqrt_done, 1)
            rows(B - 1, 1)

        @block.tensor
        def _(pe):
            pe.wait_ge(ident_done, 2)
            pe.wait_ge(rel_rows, 2)
            pe.transpose(psT[:, 0, 0:128], relR[:].rearrange("r i d -> r (i d)"), ident[:])
            pe.transpose(psT[:, 0, 128:129], relRb[:].rearrange("r i d -> r (i d)"),
                         ident[0:1, 0:1]).then_inc(rel_turned, 1)
            pe.wait_ge(c_done, 3)
            pe.transpose(psZ[:, 0:B], c_s[:], ident[0:B, 0:B]).then_inc(setup_pe, 1)
            pe.wait_ge(c_done, 4)
            pe.wait_ge(wmod_in, 16)
            for k in range(6):
                mm = pe.matmul(psP[:, 0, B * k:B * k + B], wmod_s[:, E * k:E * k + E], cT[:],
                               start=True, stop=True)
            mm.then_inc(mod_full, 1)
            pe.wait_ge(weights_in, 16 * W_DMAS)
            for half in range(2):
                mm = pe.matmul(psP[:, 1, 0:1], WoD[0:64, half, :], bvT[:, half:half + 1],
                               start=(half == 0), stop=(half == 1))
            mm.then_inc(mod_full, 1)

            def job(count, bank, work):
                if not (isinstance(count, int) and count < 2):
                    pe.wait_ge(job_done, count - 1)
                work(psP[:, bank, :]).then_inc(job_full, 1)

            def turn_nrm(bank):
                for k in range(2):
                    mm = pe.transpose(bank[:, 128 * k:128 * k + 128], nrm[:, k, :], ident[:])
                return mm

            def values(bank, half, at):
                for k in range(JB):
                    mm = pe.matmul(bank[:, at + 64 * k:at + 64 * k + 64], hT[:, 128 * k:128 * k + 128],
                                   Wv_s[:, 64 * half:64 * half + 64], start=True, stop=True)
                return mm

            def project(bank, half):
                return pe.matmul(bank[:, 0:S], Wqk[:, half, :, :].rearrange("e a m -> e (a m)"),
                                 hT[:], start=True, stop=True)

            def spread(bank, r):
                part, h0 = r // 4, 2 * (r % 4)
                for k in range(2):
                    mm = pe.matmul(bank[:, S * k:S * k + S], sel[:, part, h0 + k, :], X2[:],
                                   start=True, stop=True)
                return mm

            def out_project(bank):
                for half in range(2):
                    mm = pe.matmul(bank[:, 0:S], WoD[:, half, :], ctxT[:, half, :],
                                   start=(half == 0), stop=(half == 1))
                return mm

            def turn_y(bank):
                for k in range(2):
                    mm = pe.transpose(bank[:, 128 * k:128 * k + 128], yT[:, 128 * k:128 * k + 128],
                                      ident[:])
                return mm

            def run_job(name, b, half, count, bank):
                other = 1 - half
                if name == "q":
                    if half:
                        pe.wait_ge(job_done, count)
                    job(count, bank, lambda k: project(k, other))
                elif name[0] == "r":
                    r = int(name[1])
                    if r == 0:
                        pe.wait_ge(x2_done, 2 * b + half + 2)
                    job(count, bank, lambda k: spread(k, r))
                elif name == "hv":
                    pe.wait_ge(nrm_done, b + 2)
                    def both(k):
                        turn_nrm(k)
                        return values(k, other, S)
                    job(count, bank, both)
                elif name == "v":
                    job(count, bank, lambda k: values(k, other, 0))
                elif name == "-v":
                    job(count, bank, lambda k: values(k, other, S))
                elif name == "y":
                    pe.wait_ge(ctx_done, 2 * b)
                    job(count, bank, out_project)
                elif name == "t":
                    last = isinstance(b, int) and b == B - 1
                    pe.wait_ge(job_done, count + 1 - (1 if last else Y_TO_T))
                    job(count, bank, turn_y)

            def scores(b, half, p):
                n = 16 * b + 8 * half + p
                if p == 0:
                    pe.wait_ge(job_done, prepared(b, half))
                    pe.wait_ge(keys_done, 2 * b + half + 1)
                    pe.wait_ge(qbd_done, 2 * b + half + 1)
                if not (isinstance(b, int) and b == 0) or 8 * half + p >= 2:
                    pe.wait_ge(exp_done, n - 1)
                for k in range(2):
                    g = 2 * p + k
                    dst = psS[:, p % 2, 256 * k:256 * k + 256]
                    at = S - QG - QG * g
                    qb = Qbd[:, half, g, :, :].rearrange("p h i -> p (h i)")
                    qh = QrH[:, half, g, :, :].rearrange("p h i -> p (h i)")
                    ql = QrL[:, half, g, :, :].rearrange("p h i -> p (h i)")
                    pe.matmul(dst, qb, KK[:, half, 0, :], start=True, stop=False)
                    pe.matmul(dst, qb, KK[:, half, 1, :], start=False, stop=False)
                    pe.matmul(dst, qh, TH[:, at:at + S], start=False, stop=False)
                    pe.matmul(dst, qh, TL[:, at:at + S], start=False, stop=False)
                    mm = pe.matmul(dst, ql, TH[:, at:at + S], start=False, stop=True)
                mm.then_inc(scores_done, 1)

            def turn(b, half, p):
                n = 16 * b + 8 * half + p
                pe.wait_ge(exp_done, n + 1)
                if not (isinstance(b, int) and b == 0) or 8 * half + p >= 2:
                    pe.wait_ge(low_done, n - 1)
                for k in range(4):
                    mm = pe.transpose(psT[:, p % 2, 128 * k:128 * k + 128],
                                      P[:, p % 4, 128 * k:128 * k + 128], ident[:])
                mm.then_inc(turned, 1)

            def weigh(b, half, part):
                if part == 0:
                    pe.wait_ge(low_done, 16 * b + 8 * half + 8)
                    if not (isinstance(b, int) and b == 0 and half == 0):
                        pe.wait_ge(ctx_done, 2 * b + half)
                for h in (2 * part, 2 * part + 1):
                    for k in range(JB):
                        for n, pr in enumerate((PH, PL)):
                            rhs = pr[:, half, :, :].rearrange("j p (t x) -> j (p t) x", t=2)
                            at = 128 * k + QG * h
                            mm = pe.matmul(psO[:, 0:S], V2[:, half, k, 128 * h:128 * h + 128],
                                           rhs[:, :, at:at + QG],
                                           start=(h == 0 and k == 0 and n == 0),
                                           stop=(h == HH - 1 and k == JB - 1 and n == 1))
                if part == 3:
                    mm.then_inc(values_done, 1)

            def spread_l(b, half):
                pe.wait_ge(ldiag_done, 2 * b + half + 1)
                pe.matmul(psO[:, S:2 * S], selL[:].rearrange("p a h d -> p (a h d)"),
                          ldiag[:].rearrange("p g i -> p (g i)"), start=True, stop=True)\
                    .then_inc(lrow_full, 1)

            pe.wait_ge(nrm_done, 1)
            job(0, 0, turn_nrm)
            pe.wait_ge(job_done, 1)
            job(1, 1, lambda k: values(k, 0, 0))
            job(2, 0, lambda k: project(k, 0))
            pe.wait_ge(x2_done, 1)
            pe.wait_ge(masks_done, 1)
            for r in range(8):
                job(3 + r, (3 + r) % 2, lambda k, r=r: spread(k, r))

            def batch(b, last=False):
                first = isinstance(b, int) and b == 0
                for half in range(2):
                    pb, ph = (b, 0) if half else (b - 1, 1)
                    before = not (first and half == 0)
                    for p in range(PAIRS):
                        if p >= 2:
                            turn(b, half, p - 2)
                        elif before:
                            turn(pb, ph, PAIRS - 2 + p)
                        scores(b, half, p)
                        if p == 7 and before:
                            spread_l(pb, ph)
                        if 2 <= p < 6 and before:
                            weigh(pb, ph, p - 2)
                        for name, count, bank in slot_jobs(b, half, p, last):
                            run_job(name, b, half, count, bank)

            pe.wait_ge(setup_dve, 2)
            batch(0)
            with pe.Fori(1, B - 1) as b:
                batch(b)
            batch(B - 1, last=True)
            for p in (PAIRS - 2, PAIRS - 1):
                turn(B - 1, 1, p)
            for part in range(4):
                weigh(B - 1, 1, part)
            spread_l(B - 1, 1)
            done = job_count(B - 1, 1, 0, 0) + 2
            pe.wait_ge(ctx_done, 2 * B)
            job(done, done % 2, out_project)
            pe.wait_ge(job_done, done + 1)
            job(done + 1, (done + 1) % 2, turn_y)

        @block.vector
        def _(dve):
            linked = {"base": 0, "n": 0}

            def then(i):
                i.then_inc(link, 1)
                linked["n"] += 1
                dve.wait_ge(link, linked["base"] + linked["n"])

            dve.wait_ge(ident_done, 2)
            dve.tensor_reduce(headM[:], ident[:].rearrange("p (a h d) -> p h a d", a=2, d=D), AX.XY, ALU.add)
            dve.tensor_reduce(queryM[:], ident[:].rearrange("p (i d) -> p i d", d=D), AX.X, ALU.add)
            dve.tensor_reduce(headL[:], ident[:].rearrange("p (h i) -> p h i", i=QG), AX.X, ALU.add)
            then(dve.tensor_reduce(queryL[:], ident[:].rearrange("p (h i) -> p i h", i=QG), AX.X, ALU.add))
            for part in range(2):
                for h in range(HH):
                    at = 64 * part + D * h
                    dve.tensor_copy(sel[:, part, h, :].rearrange("p (i d) -> p i d", d=D),
                                    rep(ident[:, at:at + D], 1, QG))
            dve.tensor_copy(selL[:], rep(rep(headL[:], 1, 2), 3, D)).then_inc(masks_done, 1)
            dve.wait_ge(rel_in, 32)
            dve.tensor_copy(relR[:], rep(relA[:], 1, QG)).then_inc(rel_rows, 1)
            dve.tensor_copy(relRb[:], rep(relB[:], 1, QG)).then_inc(rel_rows, 1)
            dve.wait_ge(rel_turned, 1)
            then(dve.tensor_copy(relT[:], psT[:, 0, 0:2 * REL + 1]))
            mid = S - QG
            dve.tensor_copy(Tf[:, 0:mid], relT[:, 0:1].broadcast_to([128, mid]))
            dve.tensor_copy(Tf[:, mid:TW], relT[:, 2 * REL:2 * REL + 1].broadcast_to([128, TW - mid]))\
                .then_inc(rel_filled, 1)
            dve.wait_ge(c_done, 1)
            dve.tensor_scalar(c_e[:], c_e[:], 1.0, None, ALU.add).then_inc(c_done, 1)
            dve.wait_ge(c_done, 2)
            then(dve.reciprocal(c_e[:], c_e[:]))
            dve.tensor_tensor(c_s[:], c_s[:], c_e[:], ALU.mult).then_inc(c_done, 1)
            dve.wait_ge(setup_pe, 1)
            dve.tensor_copy(cT[:], psZ[:, 0:B]).then_inc(c_done, 1)
            dve.wait_ge(x_first, 16)
            statistics(then, dve, X, mv, stats, EARLY)
            dve.wait_ge(mod_full, 1)
            then(dve.tensor_copy(modT[:].rearrange("p k b -> p (k b)"), psP[:, 0, 0:6 * B]))
            for k in (1, 4):
                dve.tensor_scalar(modT[:, k, :], modT[:, k, :], 1.0, None, ALU.add)
            for k in (2, 5):
                then(dve.tensor_scalar(gabo[:], modT[:, k, :], 0.0, 2.0, ALU.is_ge, ALU.mult))
                then(dve.tensor_scalar(gabo[:], gabo[:], -1.0, None, ALU.add))
                then(dve.tensor_tensor(modT[:, k, :], modT[:, k, :], gabo[:], ALU.mult))
                then(dve.scalar_tensor_tensor(out=modT[:, k, :], in0=modT[:, k, :], scalar=0.25,
                                              in1=gabo[:], op0=ALU.max, op1=ALU.mult))
            dve.wait_ge(x_rest, 16)
            statistics(then, dve, X, mv, stats, LATER)
            dve.tensor_scalar(mv[:, :, 1], mv[:, :, 1], EPS, None, ALU.add).then_inc(setup_dve, 1)
            dve.wait_ge(mod_full, 2)
            then(dve.tensor_tensor(bo2[:], psP[:, 1, 0:1], boC[:], ALU.add))
            then(dve.tensor_scalar(gabo[:], modT[:, 2, :], bo2[:, 0:1], None, ALU.mult))
            then(dve.tensor_scalar(Wqk[:, :, 1, :], Wqk[:, :, 1, :], float(D) ** -0.5, None, ALU.mult))
            then(dve.tensor_scalar(bqk[64:128, :], bqk[64:128, :], float(D) ** -0.5, None, ALU.mult))
            dve.wait_ge(sqrt_done, 1)
            inverse(then, dve, rstd, mv, tmp, slice(0, TT))
            dve.wait_ge(rel_shifted, 16 * QG // 2)
            dve.wait_ge(rel_odd, 16 * QG // 2)
            then(dve.tensor_copy(TH[:], Tf[:]))
            dve.tensor_tensor(TL[:], Tf[:], TH[:].bitcast(FP), ALU.subtract).then_inc(setup_dve, 1)

            def normalise(b):
                for k in range(2):
                    n = 2 * b + k
                    i = dve.tensor_scalar(nrm[:, k, :], at(X, n), at(mv, n, 0), at(rstd, n),
                                          ALU.subtract, ALU.mult)
                i.then_inc(nrm_done, 1)

            def at(tile, n, *more):
                if len(tile[:].shape) == 2:
                    return tile[:, bass.ds(n, 1)]
                v = tile[:, bass.ds(n, 1), :].rearrange("p a e -> p (a e)")
                return v[:, more[0]:more[0] + 1] if more else v

            def mod(k, b):
                return modT[:, k, bass.ds(b, 1)]

            def queries(b, half, count, bank):
                dve.wait_ge(job_full, count + 1)
                if not (isinstance(b, int) and b == 0 and count == 2):
                    dve.wait_ge(qbd_done, 2 * b + half + 1)
                qs, qbias = bank[0:64, 0:S], bqk[0:64, 1 - half:2 - half]
                then(dve.tensor_scalar(X2[0:64, :], qs, qbias, None, ALU.add))
                dve.scalar_tensor_tensor(out=X2[64:128, :], in0=qs, scalar=qbias,
                                         in1=X2[0:64, :].bitcast(FP), op0=ALU.add,
                                         op1=ALU.subtract).then_inc(x2_done, 1)

            def take(name, b, half, count, bank):
                other = 1 - half
                dve.wait_ge(job_full, count + 1)
                if name == "h":
                    i = dve.tensor_scalar(hT[:], bank[:, 0:S], mod(1, b), mod(0, b), ALU.mult, ALU.add)
                if name[-1] == "v":
                    src = bank[:, S:S + 128] if name in ("hv", "-v") else bank[:, 0:128]
                    src = src.rearrange("p (k h d) -> p k h d", k=JB, d=D)
                    win = V2[:, other, :, :].rearrange("p k (h c) -> p k h c", c=VW)
                    then(dve.tensor_copy(win[:, :, :, 0:D], src))
                    i = dve.tensor_tensor(win[:, :, :, 64:64 + D], src,
                                          win[:, :, :, 0:D].bitcast(FP), ALU.subtract)
                if name == "hv":
                    i = dve.tensor_scalar(hT[:], bank[:, 0:S], mod(1, b + 1), mod(0, b + 1),
                                          ALU.mult, ALU.add)
                elif name == "q":
                    ks, kbias = bank[64:128, 0:S], bqk[64:128, other:other + 1]
                    kh, kl = KK[64:128, other, 0, :], KK[64:128, other, 1, :]
                    then(dve.tensor_scalar(kh, ks, kbias, None, ALU.add))
                    i = dve.scalar_tensor_tensor(out=kl, in0=ks, scalar=kbias, in1=kh.bitcast(FP),
                                                 op0=ALU.add, op1=ALU.subtract)
                elif name[0] == "r":
                    r = int(name[1])
                    dst = (QrH, QrL)[r // 4]
                    h0 = 2 * (r % 4)
                    i = dve.tensor_tensor(
                        dst[:, other, :, h0:h0 + 2, :].rearrange("p g h i -> p h g i"),
                        bank.rearrange("p (h g i) -> p h g i", h=2, i=QG),
                        rep(rep(queryM[:], 1, G), 1, 2), ALU.mult)
                elif name == "y":
                    i = dve.tensor_scalar(yT[:], bank[:, 0:S], mod(2, b - 1), gabo[:, bass.ds(b - 1, 1)],
                                          ALU.mult, ALU.add)
                elif name == "t":
                    xb = X[:, bass.ds(2 * (b - 1), 2), :]
                    i = dve.tensor_tensor(xb, bank[:, 0:S].rearrange("p (k e) -> p k e", k=2), xb,
                                          ALU.add)
                i.then_inc(job_done, 1)

            def maxima(b, half, p):
                dve.wait_ge(scores_done, 16 * b + 8 * half + p + 1)
                dve.tensor_reduce(nmax[:, half, 2 * p:2 * p + 2],
                                  psS[:, p % 2, :].rearrange("p (t j) -> p t j", t=2), AX.X,
                                  ALU.max, negate=True).then_inc(max_done, 1)

            def low(b, half, p):
                dve.wait_ge(high_done, 16 * b + 8 * half + p + 1)
                dve.tensor_tensor(PL[:, half, p, :], psT[:, p % 2, :], PH[:, half, p, :].bitcast(FP),
                                  ALU.subtract).then_inc(low_done, 1)

            def sums(b, half):
                dve.wait_ge(exp_done, 16 * b + 8 * half + 8)
                then(dve.reciprocal(linv[:], lsum[:, half, :]))
                dve.tensor_tensor(ldiag[:], rep(linv[:], 2, QG), rep(queryL[:], 1, G), ALU.mult)\
                    .then_inc(ldiag_done, 1)

            def context(b, half):
                dve.wait_ge(lrow_done, 2 * b + half + 1)
                dve.tensor_tensor(ctxT[:, half, :], psO[:, 0:S], lrow[:], ALU.mult)\
                    .then_inc(ctx_done, 1)

            dve.wait_ge(ident_done, 3)
            normalise(0)
            for n, name in enumerate(["h", "v", "q"] + [f"r{r}" for r in range(8)]):
                if name == "q":
                    queries(0, 1, n, psP[:, n % 2, :])
                take(name, 0, 1, n, psP[:, n % 2, :])

            def batch(b, last=False):
                first = isinstance(b, int) and b == 0
                for half in range(2):
                    pb, ph = (b, 0) if half else (b - 1, 1)
                    before = not (first and half == 0)
                    for p in range(PAIRS):
                        if p == 0 and not first:
                            context(b - 1, half)
                        maxima(b, half, p)
                        if p >= 2:
                            low(b, half, p - 2)
                        elif before:
                            low(pb, ph, PAIRS - 2 + p)
                        if p == 2 and before:
                            sums(pb, ph)
                        if p == 5 and half == 0 and not last:
                            normalise(b + 1)
                        if p == 0:
                            for name, count, bank in slot_jobs(b, half, 0, last):
                                queries(b, half, count, psP[:, bank, :])
                        for at_slot in ([], [0, 1])[p] if p < 2 else [p]:
                            for name, count, bank in slot_jobs(b, half, at_slot, last):
                                take(name, b, half, count, psP[:, bank, :])

            batch(0)
            used = linked["n"]
            per = LINKS
            with dve.Fori(1, B - 1) as b:
                linked["base"], linked["n"] = per * b + (used - per), 0
                batch(b)
                assert linked["n"] == per
            linked["base"], linked["n"] = used + per * (B - 2), 0
            batch(B - 1, last=True)
            context(B - 1, 0)
            low(B - 1, 1, PAIRS - 2)
            low(B - 1, 1, PAIRS - 1)
            sums(B - 1, 1)
            statistics(then, dve, X, mv, stats, EARLY)
            dve.tensor_scalar(mv[:, EARLY, 1], mv[:, EARLY, 1], EPS, None, ALU.add).then_inc(setup_dve, 1)
            context(B - 1, 1)
            dve.wait_ge(sqrt_done, 2)
            inverse(then, dve, rstd, mv, tmp, EARLY)
            done = job_count(B - 1, 1, 0, 0) + 2
            take("y", B, 1, done, psP[:, done % 2, :])
            take("t", B, 1, done + 1, psP[:, (done + 1) % 2, :])


def statistics(then, dve, X, mv, stats, tiles):
    for n in range(tiles.start, tiles.stop):
        i = dve.bn_stats(stats[:, n, :], X[:, n, :])
    then(i)
    for n in range(tiles.start, tiles.stop):
        i = dve.bn_aggr(mv[:, n, :], stats[:, n, :])
    then(i)


def inverse(then, dve, rstd, mv, tmp, tiles):
    then(dve.reciprocal(rstd[:, tiles], rstd[:, tiles]))
    newton(then, dve, rstd[:, tiles], mv[:, tiles, 1], tmp[:, tiles])


def newton(then, dve, r, v, tmp):
    then(dve.tensor_tensor(tmp, r, r, ALU.mult))
    then(dve.tensor_tensor(tmp, tmp, v, ALU.mult))
    then(dve.tensor_scalar(tmp, tmp, -0.5, 1.5, ALU.mult, ALU.add))
    then(dve.tensor_tensor(r, r, tmp, ALU.mult))


def past(engine, semaphore, count):
    if not isinstance(count, int) or count > 0:
        engine.wait_ge(semaphore, count)


def mixture(nc, X, ident, modT, mv, rstd, rw1_s, rb1T, rw2_s, rb2T, w1, b1T, w2, b2T, out_v):
    with ExitStack() as ctx:
        def t(name, shape, dt=FP):
            return ctx.enter_context(nc.sbuf_tensor(name, shape, dt))

        def sm(name):
            return ctx.enter_context(nc.semaphore(name))

        slots_d = nc.dram_tensor("slots_d", (UNUSED + ET, ROW), FP, kind="Internal").ap()
        results_d = nc.dram_tensor("results_d", (2 * TOKENS, E), FP, kind="Internal").ap()
        W = t("W", [128, EXP, 2, 512])
        p1 = t("p1", [128, TT])
        p2 = t("p2", [128, TT])
        gbB = t("gbB", [128, B, E])
        firstrow = t("firstrow", [128, JOBS], U32)
        expert = t("expert", [128, JOBS], U32)
        rows = t("rows", [128, 2, TT, ROW])
        slot_u = t("slot_u", [128, 2, TT], U32)
        fill = t("fill", [128, EK, ROW])
        y = t("y", [128, 2, EK, E])
        row_u = t("row_u", [128, JOBS, EK], U32)
        sent, filled = sm("sent"), sm("filled")
        y_sent = [sm("y_sent0"), sm("y_sent1")]
        route(nc, X, ident, modT, mv, rstd, rw1_s, rb1T, rw2_s, rb2T, w1, w2, slots_d, W,
              p2, gbB, firstrow, expert, rows, slot_u, fill, sent, filled)
        experts(nc, ident, slots_d, results_d, W, b1T, b2T, firstrow, expert, y, row_u, sent,
                filled, y_sent)
        combine(nc, X, results_d, p1, p2, gbB, y_sent, out_v)


def route(nc, X, ident, modT, mv, rstd, rw1_s, rb1T, rw2_s, rb2T, w1, w2, slots_d, W,
          p2, gbB, firstrow, expert, rows, slot_u, fill, sent, filled):
    with ExitStack() as ctx:
        def t(name, shape, dt=FP):
            return ctx.enter_context(nc.sbuf_tensor(name, shape, dt))

        def pt(name, shape):
            return ctx.enter_context(nc.psum_tensor(name, shape, FP))

        def sm(name):
            return ctx.enter_context(nc.semaphore(name))

        logitT = t("logitT", [128, CT])
        stats2 = t("stats2", [128, TT, 6])
        tmp2 = t("tmp2", [128, TT])
        n2 = t("n2", [128, 2, CK, E])
        h2T = t("h2T", [128, 2, CT])
        hid = t("hid", [128, HK, CT])
        logit = t("logit", [128, CK, EXP])
        v1 = t("v1", [128, TT])
        v2 = t("v2", [128, TT])
        key = t("key", [128, CK, EXP])
        kmax = t("kmax", [128, CK])
        chosen = t("chosen", [128, 2, 2, CK, EXP])
        both = t("both", [128, 2, CK, EXP])
        earlier = t("earlier", [128, 2, CK + 1, EXP])
        slot_f = t("slot_f", [128, 2, CK])
        slot_e = t("slot_e", [128, CK, EXP])
        slot_c = t("slot_c", [128, 2, CK, EXP])
        order = t("order", [128, EXP])
        area = t("area", [128, EXP])
        token = t("token", [128, 2, TT])
        before = t("before", [128, 128])
        ones = t("ones", [128, 128])
        gbR = t("gbR", [B, E])
        steps = t("steps", [128, EXP, MOST])
        until = t("until", [128, EXP, EXP])
        cnt = t("cnt", [128, EXP])
        cnt_u = t("cnt_u", [128, EXP], U32)
        more = t("more", [128, EXP, MOST])
        wide = t("wide", [128, EXP, EXP])
        ntile = t("ntile", [128, EXP])
        cum = t("cum", [128, EXP])
        jobno = t("jobno", [128, JOBS])
        gone = t("gone", [128, JOBS, EXP])
        gone_t = t("gone_t", [128, JOBS, EXP])
        ex = t("ex", [128, JOBS])
        start = t("start", [128, JOBS])

        psA = pt("psA", [128, 2, CT])
        psU = pt("psU", [128, 2, CT])
        psB = pt("psB", [128, 512])
        psL = pt("psL", [128, 512])
        psG = pt("psG", [128, 512])
        psR = pt("psR", [128, 512])

        experts_in, deviation_done, variance_done, normalised, tokens_turned, modulated, hidden_full, hidden_done, logits_full, link = (
            sm("experts_in"), sm("deviation_done"), sm("variance_done"), sm("normalised"), sm("tokens_turned"),
            sm("modulated"), sm("hidden_full"), sm("hidden_done"), sm("logits_full"), sm("route_link"))
        logits_taken, choice_done, ranks_full, slots_done = (
            sm("logits_taken"), sm("choice_done"), sm("ranks_full"), sm("slots_done"))
        rows_full, gate_out, constants_done, gate_full = (
            sm("rows_full"), sm("gate_out"), sm("constants_done"), sm("gate_full"))
        counted, counts_done, rows_out, logits_biased, logits_turned = (
            sm("counted"), sm("counts_done"), sm("rows_out"), sm("logits_biased"), sm("logits_turned"))
        block = ctx.enter_context(nc.Block())

        @block.sync
        def _(sp):
            sp.dma_start(W[:, :, 0, :], w1.rearrange("x p h -> p x h")).then_inc(experts_in, 16)
            for x in range(EXP):
                sp.dma_start(W[:, x, 1, :].rearrange("p (k e) -> p k e", k=HK),
                             w2[x].rearrange("(k p) e -> p k e", p=128)).then_inc(experts_in, 16)
            sp.wait_ge(constants_done, 2)
            sp.dma_start(slots_d[UNUSED:UNUSED + ET, :].rearrange("(p k) e -> p k e", p=128),
                         fill[:]).then_inc(filled, 16)
            sp.wait_ge(counts_done, 1)
            for x in range(EXP):
                n = sp.value_load(cnt_u[0:1, x:x + 1], min_val=0, max_val=TOKENS)
                sp.dma_start(slots_d[bass.ds(n + AREA * x, ET), :].rearrange("(p k) e -> p k e", p=128),
                             fill[:]).then_inc(filled, 16)
            sp.wait_ge(experts_in, 16 * (1 + EXP))

        @block.gpsimd
        def _(pool):
            pool.memset(fill[:], 0.0).then_inc(constants_done, 1)
            pool.wait_ge(constants_done, 1)
            pool.memset(fill[:, :, E:ROW], float(NO_ROW))
            pool.memset(ones[:], 1.0).then_inc(constants_done, 1)
            pool.wait_ge(constants_done, 2)
            pool.affine_select(out=before[:], in_=ones[:], compare_op=ALU.is_gt, fill=0.0, base=0,
                               pattern=[[1, 128]], channel_multiplier=-1)
            pool.iota(order[:], [[-1, EXP]], base=EXP, channel_multiplier=0,
                      allow_small_or_imprecise_dtypes=True)
            pool.iota(area[:], [[AREA, EXP]], base=0, channel_multiplier=0,
                      allow_small_or_imprecise_dtypes=True)
            pool.iota(token[:], [[TOKENS, 2], [128, TT]], base=0, channel_multiplier=1,
                      allow_small_or_imprecise_dtypes=True)
            pool.iota(steps[:], [[0, EXP], [ET, MOST]], base=0, channel_multiplier=0,
                      allow_small_or_imprecise_dtypes=True)
            pool.iota(until[:], [[1, EXP], [-1, EXP]], base=0, channel_multiplier=0,
                      allow_small_or_imprecise_dtypes=True)
            pool.iota(jobno[:], [[1, JOBS]], base=0, channel_multiplier=0,
                      allow_small_or_imprecise_dtypes=True).then_inc(constants_done, 1)

            def dispatch(c):
                pool.wait_ge(slots_done, c + 1)
                pool.wait_ge(rows_out, c + 1)
                for j in range(2):
                    for n in range(CK * c, CK * c + CK):
                        pool.indirect_dma_start(
                            out=slots_d,
                            out_offset=bass.IndirectOffsetOnAxis(ap=slot_u[:, j, n:n + 1], axis=0),
                            in_=rows[:, j, n, :], in_offset=None).then_inc(sent, 16)

            for c in range(CHUNKS):
                dispatch(c)

        @block.scalar
        def _(act):
            def step(c):
                for k in range(HK):
                    past(act, hidden_full, HK * c + k + 1)
                    if k == 0:
                        past(act, logits_full, c)
                    act.activation(hid[:, k, :], psU[:, k % 2, :], ACT.Silu,
                                   bias=rb1T[:, k:k + 1]).then_inc(hidden_done, 1)
                act.wait_ge(rows_full, c + 1)
                for j in range(2):
                    i = act.activation(rows[:, j, bass.ds(CK * c, CK), 0:E],
                                       psB[:].rearrange("p (k e) -> p k e", k=CK), ACT.Copy)
                i.then_inc(rows_out, 1)
                act.wait_ge(logits_full, c + 1)
                past(act, logits_turned, c)
                act.activation(logitT[:], psL[:], ACT.Identity, bias=rb2T[:, 0:1])\
                    .then_inc(logits_biased, 1)

            step(0)
            act.wait_ge(variance_done, 1)
            act.activation(rstd[:, LATER], mv[:, LATER, 1], ACT.Sqrt).then_inc(deviation_done, 1)
            step(1)
            with act.Fori(2, CHUNKS) as c:
                step(c)
            act.wait_ge(gate_full, 1)
            act.activation(gbR[:], psL[0:B, 0:E], ACT.Copy).then_inc(gate_full, 1)
            for g in range(B * E // 512):
                act.wait_ge(gate_full, 3 + g)
                act.activation(gbB[:, 4 * g:4 * g + 4, :].rearrange("p b e -> p (b e)"),
                               (psB, psL)[g % 2][:], ACT.Copy).then_inc(gate_out, 1)

        @block.tensor
        def _(pe):
            def turn(c, par):
                pe.wait_ge(normalised, c + 1)
                past(pe, modulated, c - 1)
                for k in range(CK):
                    mm = pe.transpose(psA[:, par, 128 * k:128 * k + 128], n2[:, par, k, :], ident[:])
                mm.then_inc(tokens_turned, 1)

            def rank(c, par):
                pe.wait_ge(choice_done, c + 1)
                past(pe, slots_done, c)
                pe.matmul(psR[:, 0:CK * EXP], before[:], both[:, par, :, :].rearrange("p k e -> p (k e)"),
                          start=True, stop=False)
                pe.matmul(psR[:, 0:CK * EXP], ones[:],
                          earlier[:, par, 0:CK, :].rearrange("p k e -> p (k e)"),
                          start=False, stop=True).then_inc(ranks_full, 1)

            def turn_logits(c):
                pe.wait_ge(logits_biased, c + 1)
                past(pe, logits_taken, c)
                for k in range(CK):
                    mm = pe.transpose(psG[:, 128 * k:128 * k + 128],
                                      logitT[:, 128 * k:128 * k + 128], ident[:])
                mm.then_inc(logits_turned, 1)

            def step(c, par, last=False):
                pe.wait_ge(modulated, c + 1)
                for k in range(HK):
                    if k == 1 and (not isinstance(c, int) or c > 0):
                        turn_logits(c - 1)
                    past(pe, hidden_done, HK * c + k - 1)
                    pe.matmul(psU[:, k % 2, :], rw1_s[:, 128 * k:128 * k + 128], h2T[:, par, :],
                              start=True, stop=True).then_inc(hidden_full, 1)
                if not last:
                    turn(c + 1, 1 - par)
                past(pe, rows_out, c)
                for k in range(CK):
                    mm = pe.transpose(psB[:, 128 * k:128 * k + 128],
                                      h2T[:, par, 128 * k:128 * k + 128], ident[:])
                mm.then_inc(rows_full, 1)
                pe.wait_ge(hidden_done, HK * c + HK)
                past(pe, logits_biased, c)
                for k in range(HK):
                    mm = pe.matmul(psL[:], rw2_s[:, k, :], hid[:, k, :],
                                   start=(k == 0), stop=(k == HK - 1))
                mm.then_inc(logits_full, 1)
                if not isinstance(c, int) or c > 0:
                    rank(c - 1, 1 - par)

            turn(0, 0)
            for c in range(3):
                step(c, c % 2)
            with pe.Fori(1, CHUNKS // 2 - 1) as m:
                step(2 * m + 1, 1)
                step(2 * m + 2, 0)
            step(CHUNKS - 1, 1, last=True)
            turn_logits(CHUNKS - 1)
            rank(CHUNKS - 1, 1)
            pe.wait_ge(slots_done, CHUNKS)
            pe.matmul(psR[:, 0:EXP], ones[:], earlier[:, 1, CK, :], start=True, stop=True)\
                .then_inc(counted, 1)
            pe.transpose(psL[0:B, 0:E], modT[:, 5, :], ident[:]).then_inc(gate_full, 1)
            pe.wait_ge(gate_full, 2)
            for g in range(B * E // 512):
                if g >= 2:
                    pe.wait_ge(gate_out, g - 1)
                for k in range(4):
                    b = 4 * g + k
                    mm = pe.matmul((psB, psL)[g % 2][:, 128 * k:128 * k + 128],
                                   ident[0:B, b:b + 1].broadcast_to([B, 128]), gbR[:],
                                   start=True, stop=True)
                mm.then_inc(gate_full, 1)

        @block.vector
        def _(dve):
            linked = {"base": 0, "n": 0}

            def then(i):
                i.then_inc(link, 1)
                linked["n"] += 1
                dve.wait_ge(link, linked["base"] + linked["n"])

            def normalise(c, par):
                past(dve, tokens_turned, c - 1)
                for k in range(CK):
                    n = CK * c + k
                    i = dve.tensor_scalar(
                        n2[:, par, k, :], X[:, bass.ds(n, 1), :].rearrange("p a e -> p (a e)"),
                        mv[:, bass.ds(n, 1), 0:1].rearrange("p a e -> p (a e)"),
                        rstd[:, bass.ds(n, 1)], ALU.subtract, ALU.mult)
                i.then_inc(normalised, 1)

            def modulate(c, par):
                dve.wait_ge(tokens_turned, c + 1)
                past(dve, rows_full, c - 1)
                for k in range(2):
                    i = dve.tensor_scalar(h2T[:, par, S * k:S * k + S], psA[:, par, S * k:S * k + S],
                                          modT[:, 4, bass.ds(2 * c + k, 1)],
                                          modT[:, 3, bass.ds(2 * c + k, 1)], ALU.mult, ALU.add)
                i.then_inc(modulated, 1)

            def choose(c, par):
                dve.wait_ge(logits_turned, c + 1)
                dve.tensor_copy(logit[:], psG[:].rearrange("p (n e) -> p n e", n=CK)[:, :, 0:EXP])\
                    .then_inc(logits_taken, 1)
                dve.wait_ge(logits_taken, c + 1)
                for r, v in enumerate((v1, v2)):
                    v = v[:, bass.ds(CK * c, CK)]
                    mask = chosen[:, par, r, :, :]
                    then(dve.tensor_reduce(v, logit[:], AX.X, ALU.max))
                    then(dve.tensor_tensor(key[:], logit[:], rep(v, 2, EXP), ALU.is_equal))
                    then(dve.tensor_tensor(key[:], key[:], rep(order[:], 1, CK), ALU.mult))
                    then(dve.tensor_reduce(kmax[:], key[:], AX.X, ALU.max))
                    then(dve.tensor_tensor(mask, key[:], rep(kmax[:], 2, EXP), ALU.is_equal))
                    if r == 0:
                        then(dve.scalar_tensor_tensor(out=logit[:], in0=mask, scalar=-3e38,
                                                      in1=logit[:], op0=ALU.mult, op1=ALU.add))
                dve.tensor_copy(earlier[:, par, 0, :], earlier[:, 1 - par, CK, :])
                then(dve.tensor_tensor(both[:, par, :, :], chosen[:, par, 0, :, :],
                                       chosen[:, par, 1, :, :], ALU.add))
                for k in range(CK):
                    i = dve.tensor_tensor(earlier[:, par, k + 1, :], earlier[:, par, k, :],
                                          both[:, par, k, :], ALU.add)
                    if k < CK - 1:
                        then(i)
                i.then_inc(choice_done, 1)
                dve.wait_ge(choice_done, c + 1)

            def slots(c, par):
                dve.wait_ge(ranks_full, c + 1)
                then(dve.tensor_tensor(slot_e[:], psR[:, 0:CK * EXP].rearrange("p (k e) -> p k e", e=EXP),
                                       rep(area[:], 1, CK), ALU.add))
                then(dve.tensor_tensor(slot_c[:], chosen[:, par, :, :, :], rep(slot_e[:], 1, 2),
                                       ALU.mult))
                then(dve.tensor_reduce(slot_f[:], slot_c[:], AX.X, ALU.add))
                dve.tensor_copy(slot_u[:, :, bass.ds(CK * c, CK)], slot_f[:]).then_inc(slots_done, 1)
                dve.wait_ge(slots_done, c + 1)

            normalise(0, 0)
            modulate(0, 0)
            normalise(1, 1)
            dve.wait_ge(constants_done, 3)
            dve.tensor_scalar(until[:], until[:], 0.0, None, ALU.is_ge)
            dve.tensor_copy(rows[:, :, :, E:ROW].rearrange("p j n a -> p j (n a)"), token[:])
            then(dve.memset(earlier[:], 0.0))
            statistics(then, dve, X, mv, stats2, LATER)
            dve.tensor_scalar(mv[:, LATER, 1], mv[:, LATER, 1], EPS, None, ALU.add).then_inc(variance_done, 1)

            def step(c, par, last=False):
                if not isinstance(c, int) or c > 0:
                    choose(c - 1, 1 - par)
                if not last:
                    modulate(c + 1, 1 - par)
                if isinstance(c, int) and c == 0:
                    dve.wait_ge(deviation_done, 1)
                    inverse(then, dve, rstd, mv, tmp2, LATER)
                if not (isinstance(c, int) and c >= CHUNKS - 2):
                    normalise(c + 2, par)
                if not isinstance(c, int) or c > 0:
                    slots(c - 1, 1 - par)

            for c in range(3):
                step(c, c % 2)
            used = linked["n"]
            LINKS_OF_CHUNK = 18
            with dve.Fori(1, CHUNKS // 2 - 2) as m:
                linked["base"], linked["n"] = 2 * LINKS_OF_CHUNK * m + (used - 2 * LINKS_OF_CHUNK), 0
                step(2 * m + 1, 1)
                step(2 * m + 2, 0)
                assert linked["n"] == 2 * LINKS_OF_CHUNK, linked["n"]
            linked["base"], linked["n"] = used + LINKS_OF_CHUNK * (CHUNKS - 6), 0
            step(CHUNKS - 3, 1)
            step(CHUNKS - 2, 0)
            step(CHUNKS - 1, 1, last=True)
            choose(CHUNKS - 1, 1)
            slots(CHUNKS - 1, 1)
            dve.tensor_tensor(p2[:], v2[:], v1[:], ALU.subtract)
            dve.wait_ge(counted, 1)
            then(dve.tensor_copy(cnt[:], psR[:, 0:EXP]))
            dve.tensor_copy(cnt_u[:], cnt[:]).then_inc(counts_done, 1)
            then(dve.tensor_tensor(more[:], rep(cnt[:], 2, MOST), steps[:], ALU.is_gt))
            then(dve.tensor_reduce(ntile[:], more[:], AX.X, ALU.add))
            then(dve.tensor_tensor(wide[:], rep(ntile[:], 1, EXP), until[:], ALU.mult))
            then(dve.tensor_reduce(cum[:], wide[:], AX.X, ALU.add))
            then(dve.tensor_tensor(gone[:], rep(jobno[:], 2, EXP), rep(cum[:], 1, JOBS), ALU.is_ge))
            then(dve.tensor_tensor(gone_t[:], gone[:], rep(ntile[:], 1, JOBS), ALU.mult))
            dve.tensor_reduce(ex[:], gone[:], AX.X, ALU.add)
            then(dve.tensor_reduce(start[:], gone_t[:], AX.X, ALU.add))
            then(dve.tensor_tensor(start[:], jobno[:], start[:], ALU.subtract))
            then(dve.tensor_scalar(start[:], start[:], float(ET), None, ALU.mult))
            then(dve.scalar_tensor_tensor(out=start[:], in0=ex[:], scalar=float(AREA), in1=start[:],
                                          op0=ALU.mult, op1=ALU.add))
            dve.tensor_scalar(ex[:], ex[:], float(EXP - 1), None, ALU.min)
            then(dve.tensor_scalar(start[:], start[:], float(UNUSED), None, ALU.min))
            dve.tensor_copy(expert[:], ex[:])
            dve.tensor_copy(firstrow[:], start[:])


def experts(nc, ident, slots_d, results_d, W, b1T, b2T, firstrow, expert, y, row_u, sent,
            filled, y_sent):
    with ExitStack() as ctx:
        def t(name, shape, dt=FP):
            return ctx.enter_context(nc.sbuf_tensor(name, shape, dt))

        def pt(name, shape):
            return ctx.enter_context(nc.psum_tensor(name, shape, FP))

        def sm(name):
            return ctx.enter_context(nc.semaphore(name))

        x = t("x", [128, 2, EK, ROW])
        w1H = t("w1H", [128, 2, HID], FR)
        w1L = t("w1L", [128, 2, HID], FR)
        w2H = t("w2H", [128, 2, HID], FR)
        w2L = t("w2L", [128, 2, HID], FR)
        xH = t("xH", [128, 2, ET], FR)
        xL = t("xL", [128, 2, ET], FR)
        F = t("F", [128, HK, ET])
        FH = t("FH", [128, 2, HK, ET], FR)
        FL = t("FL", [128, 2, HK, ET], FR)
        one = t("one", [128, HID])
        yT = t("yT2", [128, 2, ET])

        psX = pt("psX", [128, 512])
        psH = pt("psH", [128, 2, 512])
        psD = pt("psD", [128, 2, 512])
        psY = pt("psY", [128, 2, 512])

        x_in = [sm("x_in0"), sm("x_in1")]
        x_turned, x_high, x_low, w1_high, w1_low, w2_high, w2_low = (
            sm("x_turned"), sm("x_high"), sm("x_low"), sm("w1_high"), sm("w1_low"), sm("w2_high"),
            sm("w2_low"))
        up, silu, high, low, down, y_biased, y_turned, y_rows, rows_known = (
            sm("up"), sm("silu"), sm("high"), sm("low"), sm("down"), sm("y_biased"),
            sm("y_turned"), sm("y_rows"), sm("rows_known"))
        block = ctx.enter_context(nc.Block())

        def each(step, engine):
            for j in range(3):
                step(j, j % 2)
            with engine.Fori(1, JOBS // 2 - 1) as m:
                step(2 * m + 1, 1)
                step(2 * m + 2, 0)
            for j in range(JOBS - 2, JOBS + 2):
                step(j, j % 2)

        assert JOBS % 2

        def has(j, n):
            return (j + n >= 0 and j + n < JOBS) if isinstance(j, int) else True

        def of_tile(engine, j):
            return engine.value_load(expert[0:1, bass.ds(j, 1)], min_val=0, max_val=EXP - 1)

        @block.sync
        def _(sp):
            def load(j, par):
                past(sp, x_turned, j - 1)
                past(sp, rows_known, j - 1)
                n = sp.value_load(firstrow[0:1, bass.ds(j, 1)], min_val=0, max_val=UNUSED)
                sp.dma_start(x[:, par, :, :], slots_d[bass.ds(n, ET), :].rearrange(
                    "(p k) e -> p k e", p=128)).then_inc(x_in[par], 16)

            sp.wait_ge(sent, 16 * 2 * TT)
            sp.wait_ge(filled, 16 * (EXP + 1))
            for j in range(3):
                load(j, j % 2)
            with sp.Fori(1, JOBS // 2) as m:
                load(2 * m + 1, 1)
                load(2 * m + 2, 0)

        @block.gpsimd
        def _(pool):
            def send(j, par):
                pool.wait_ge(y_rows, j + 1)
                for k in range(EK):
                    pool.indirect_dma_start(
                        out=results_d,
                        out_offset=bass.IndirectOffsetOnAxis(ap=row_u[:, j, k:k + 1], axis=0),
                        in_=y[:, par, k, :], in_offset=None, bounds_check=2 * TOKENS - 1,
                        oob_is_err=False).then_inc(y_sent[par], 16)

            def split(j, n, hi, done):
                par = j % 2
                e = of_tile(pool, j)
                past(pool, (up, down)[n], (HK * (j - 1), j - 1)[n])
                pool.tensor_tensor(hi[:, par, :], W[:, bass.ds(e, 1), n, :].rearrange("p a h -> p (a h)"),
                                   one[:], ALU.mult)\
                    .then_inc(done, 1)

            pool.memset(one[:], 1.0).then_inc(w2_high, 1)
            pool.wait_ge(w2_high, 1)
            for j in range(JOBS + 2):
                if has(j, 0):
                    split(j, 1, w2H, w2_high)
                if has(j, -2):
                    send(j - 2, j % 2)

        def sent_before(j, par):
            return (j - par) * (16 * EK // 2)

        @block.scalar
        def _(act):
            def split_x(j, par):
                act.wait_ge(x_turned, j + 1)
                past(act, up, HK * (j - 1))
                act.activation(xH[:, par, :], psX[:, 0:ET], ACT.Copy).then_inc(x_high, 1)

            split_x(0, 0)

            def step(j, par):
                if has(j, 0):
                    e = of_tile(act, j)
                for k in range(HK + 1):
                    if has(j, 0) and k < HK:
                        act.wait_ge(up, HK * j + k + 1)
                        past(act, low, HK * (j - 1) + k + 1)
                        act.activation(F[:, k, :], psH[:, k % 2, 0:ET], ACT.Silu,
                                       bias=b1T[:, bass.ds(e, 1), k:k + 1].rearrange("p a k -> p (a k)"))\
                            .then_inc(silu, 1)
                    if k == 1 and has(j, 1):
                        split_x(j + 1, 1 - par)
                    if has(j, 0) and k > 0:
                        act.wait_ge(silu, HK * j + k)
                        if k == 1:
                            past(act, down, j - 1)
                        act.activation(FH[:, par, k - 1, :], F[:, k - 1, :], ACT.Copy).then_inc(high, 1)
                    if k == HK and has(j, -2):
                        act.wait_ge(y_turned, j - 1)
                        if not isinstance(j, int) or j >= 4:
                            act.wait_ge(y_sent[par], sent_before(j - 2, par))
                        act.activation(y[:, par, :, :], psY[:, par, 0:ET].rearrange("p (k e) -> p k e", k=EK),
                                       ACT.Copy).then_inc(y_rows, 1)

            each(step, act)

        @block.tensor
        def _(pe):
            def turn_x(j, par):
                pe.wait_ge(x_in[par], (j - par + 2) * 8)
                past(pe, x_high, j)
                past(pe, x_low, j)
                for k in range(EK):
                    mm = pe.transpose(psX[:, 128 * k:128 * k + 128], x[:, par, k, 0:E], ident[:])
                mm.then_inc(x_turned, 1)

            def step(j, par):
                if has(j, 0):
                    pe.wait_ge(x_low, j + 1)
                    pe.wait_ge(w1_low, j + 1)
                for k in range(HK):
                    if has(j, 0):
                        past(pe, silu, HK * j + k - 1)
                        at = slice(128 * k, 128 * k + 128)
                        pe.matmul(psH[:, k % 2, 0:ET], w1H[:, par, at], xH[:, par, :], start=True, stop=False)
                        pe.matmul(psH[:, k % 2, 0:ET], w1H[:, par, at], xL[:, par, :], start=False, stop=False)
                        pe.matmul(psH[:, k % 2, 0:ET], w1L[:, par, at], xH[:, par, :], start=False, stop=True)\
                            .then_inc(up, 1)
                    if k == 1 and has(j, 1):
                        turn_x(j + 1, 1 - par)
                    if k == 3 and has(j, -2):
                        pe.wait_ge(y_biased, j - 1)
                        past(pe, y_rows, j - 3)
                        for i in range(EK):
                            mm = pe.transpose(psY[:, par, 128 * i:128 * i + 128],
                                              yT[:, par, 128 * i:128 * i + 128], ident[:])
                        mm.then_inc(y_turned, 1)
                if has(j, -1):
                    n, q = j - 1, 1 - par
                    pe.wait_ge(w2_low, n + 1)
                    pe.wait_ge(low, HK * n + HK)
                    past(pe, y_biased, n - 1)
                    for k in range(HK):
                        at = slice(128 * k, 128 * k + 128)
                        pe.matmul(psD[:, q, 0:ET], w2H[:, q, at], FH[:, q, k, :], start=(k == 0), stop=False)
                        pe.matmul(psD[:, q, 0:ET], w2H[:, q, at], FL[:, q, k, :], start=False, stop=False)
                        mm = pe.matmul(psD[:, q, 0:ET], w2L[:, q, at], FH[:, q, k, :], start=False,
                                       stop=(k == HK - 1))
                    mm.then_inc(down, 1)

            turn_x(0, 0)
            each(step, pe)

        @block.vector
        def _(dve):
            def split_x(j, par):
                dve.wait_ge(x_high, j + 1)
                past(dve, up, HK * (j - 1))
                dve.tensor_copy(row_u[:, bass.ds(j, 1), :], x[:, par, :, E:ROW].rearrange("p k a -> p a k"))\
                    .then_inc(rows_known, 1)
                dve.tensor_tensor(xL[:, par, :], psX[:, 0:ET], xH[:, par, :].bitcast(FP), ALU.subtract)\
                    .then_inc(x_low, 1)

            def split_w(j, par, n, hi, lo, hi_done, lo_done):
                e = of_tile(dve, j)
                if n == 0:
                    past(dve, up, HK * (j - 1))
                    dve.tensor_copy(hi[:, par, :], W[:, bass.ds(e, 1), n, :].rearrange("p a h -> p (a h)"))\
                        .then_inc(hi_done, 1)
                dve.wait_ge(hi_done, j + 1 + n)
                dve.tensor_tensor(lo[:, par, :], W[:, bass.ds(e, 1), n, :].rearrange("p a h -> p (a h)"),
                                  hi[:, par, :].bitcast(FP), ALU.subtract).then_inc(lo_done, 1)

            split_w(0, 0, 0, w1H, w1L, w1_high, w1_low)
            split_x(0, 0)

            def step(j, par):
                if has(j, -2):
                    n = j - 2
                    e = of_tile(dve, n)
                    dve.wait_ge(down, n + 1)
                    past(dve, y_turned, n - 1)
                    dve.tensor_scalar(yT[:, par, :], psD[:, par, 0:ET], b2T[:, bass.ds(e, 1)], None,
                                      ALU.add).then_inc(y_biased, 1)
                if has(j, 1):
                    split_w(j + 1, 1 - par, 0, w1H, w1L, w1_high, w1_low)
                for k in range(HK):
                    if k == 1 and has(j, 1):
                        split_x(j + 1, 1 - par)
                    if has(j, 0):
                        dve.wait_ge(high, HK * j + k + 1)
                        if k == 0:
                            past(dve, down, j - 1)
                        dve.tensor_tensor(FL[:, par, k, :], F[:, k, :],
                                          FH[:, par, k, :].bitcast(FP), ALU.subtract).then_inc(low, 1)
                        if k == 2:
                            split_w(j, par, 1, w2H, w2L, w2_high, w2_low)

            each(step, dve)


def combine(nc, X, results_d, p1, p2, gbB, y_sent, out_v):
    with ExitStack() as ctx:
        def t(name, shape, dt=FP):
            return ctx.enter_context(nc.sbuf_tensor(name, shape, dt))

        def sm(name):
            return ctx.enter_context(nc.semaphore(name))

        y1 = t("y1", [128, TT, E])
        y2 = t("y2", [128, TT, E])
        loaded = [sm(f"loaded{c}") for c in range(CHUNKS)]
        probs, weighted, summed, gated, added, stored = (
            sm("probs"), sm("weighted"), sm("summed"), sm("gated"), sm("added"), sm("stored"))
        block = ctx.enter_context(nc.Block())

        @block.sync
        def _(sp):
            for par in range(2):
                sp.wait_ge(y_sent[par], 16 * EK * ((JOBS + 1 - par) // 2))
            for c in range(CHUNKS):
                at = slice(CK * c, CK * c + CK)
                for j, y in enumerate((y1, y2)):
                    src = results_d[TOKENS * j:TOKENS * j + TOKENS, :].rearrange("(n p) e -> p n e", p=128)
                    sp.dma_start(y[:, at, :], src[:, at, :]).then_inc(loaded[c], 16)
            for c in range(CHUNKS):
                at = slice(CK * c, CK * c + CK)
                sp.wait_ge(added, c + 1)
                sp.dma_start(out_v[:, at, :], y2[:, at, :]).then_inc(stored, 16)
            sp.wait_ge(stored, 16 * CHUNKS)

        @block.scalar
        def _(act):
            act.activation(p2[:], p2[:], ACT.Exp).then_inc(probs, 1)
            act.wait_ge(probs, 4)
            for c in range(CHUNKS):
                act.wait_ge(loaded[c], 32)
                for k in range(CK):
                    n = CK * c + k
                    i = act.activation(y1[:, n, :], y1[:, n, :], ACT.Copy, scale=p1[:, n:n + 1])
                i.then_inc(weighted, 1)

        @block.vector
        def _(dve):
            dve.wait_ge(probs, 1)
            dve.tensor_scalar(p1[:], p2[:], 1.0, None, ALU.add).then_inc(probs, 1)
            dve.wait_ge(probs, 2)
            dve.reciprocal(p1[:], p1[:]).then_inc(probs, 1)
            dve.wait_ge(probs, 3)
            dve.tensor_tensor(p2[:], p2[:], p1[:], ALU.mult).then_inc(probs, 1)
            dve.wait_ge(probs, 4)
            for c in range(CHUNKS):
                at = slice(CK * c, CK * c + CK)
                dve.wait_ge(weighted, c + 1)
                for k in range(CK):
                    n = CK * c + k
                    i = dve.scalar_tensor_tensor(out=y2[:, n, :], in0=y2[:, n, :], scalar=p2[:, n:n + 1],
                                                 in1=y1[:, n, :], op0=ALU.mult, op1=ALU.add)
                i.then_inc(summed, 1)
                dve.wait_ge(summed, c + 1)
                yb = y2[:, at, :].rearrange("p (b k) e -> p b k e", b=2)
                dve.tensor_tensor(yb, yb, rep(gbB[:, 2 * c:2 * c + 2, :], 2, 2), ALU.mult)\
                    .then_inc(gated, 1)

        @block.gpsimd
        def _(pool):
            for c in range(CHUNKS):
                at = slice(CK * c, CK * c + CK)
                pool.wait_ge(gated, c + 1)
                pool.tensor_tensor(y2[:, at, :], y2[:, at, :], X[:, at, :], ALU.add).then_inc(added, 1)


_INS = ['L0_attn_q', 'L0_attn_Wq', 'L0_attn_bq', 'L0_attn_Wk', 'L0_attn_bk', 'L0_attn_Wv',
        'L0_attn_bv', 'L0_attn_Wo', 'L0_attn_bo', 'L0_attn_rel_table', 'L0_ffn_rw1', 'L0_ffn_rb1',
        'L0_ffn_rw2', 'L0_ffn_rb2', 'L0_ffn_w1', 'L0_ffn_b1', 'L0_ffn_w2', 'L0_ffn_b2', 'L0_c',
        'L0_wmod']
_OUTS = [((16, 256, 128), 'float32')]


def kernel(**inputs):
    import numpy as _np
    import concourse.bacc as _bacc
    from concourse import mybir as _mybir
    from concourse.bass_utils import run_bass_kernel_spmd as _run

    nc = _bacc.Bacc("TRN2", target_bir_lowering=False, num_devices=1)
    arrays, args = {}, []
    for name in _INS:
        a = _np.ascontiguousarray(inputs[name])
        arrays[f"in_{name}_dram"] = a
        args.append(nc.dram_tensor(f"in_{name}_dram", a.shape, _mybir.dt.from_np(a.dtype), kind="ExternalInput").ap())
    for i, (shape, dtype) in enumerate(_OUTS):
        dt = _mybir.dt.from_np(_np.dtype(dtype))
        args.append(nc.dram_tensor(f"out_{i}_dram", shape, dt, kind="ExternalOutput").ap())
    program(nc, *args)
    r = _run(nc, [arrays], core_ids=[0])
    return r.results[0]["out_0_dram"]
```
